# Optimizing a Trainium2 kernel written in Bass

```python
import numpy as np
import jax
import jax.numpy as jnp

def _softmax(x, axis=-1):
    return jax.nn.softmax(x, axis=axis)

def _gelu(x):
    return jax.nn.gelu(x, approximate=True)

def _silu(x):
    return jax.nn.silu(x)

def _sigmoid(x):
    return jax.nn.sigmoid(x)

def _layernorm(x, axis=-1, eps=1e-05):
    m = jnp.mean(x, axis=axis, keepdims=True)
    v = jnp.var(x, axis=axis, keepdims=True)
    return (x - m) / jnp.sqrt(v + eps)

def _scatter_add(tgt, idx, src, axis=0):
    return tgt.at[idx].add(src)

def _segment_sum(src, seg, n):
    return jax.ops.segment_sum(src, seg, n)
kernel_name = 'mk_vit_tower_d2_tok_img1024_r4_f09528'

def setup_inputs(seed: int=0):
    np.random.seed(seed)
    _w = jnp.asarray

    def _rec_inputs():
        import jax
        import jax.numpy as jnp
        _rk = jax.random.key(seed)
        x = 7.22013e-05 + 1.00017 * jax.random.normal(jax.random.fold_in(_rk, 1), (8, 1, 512, 256), jnp.float32)
        return x
    x = _rec_inputs()

    def _L0_tok_setup():
        import jax, jax.numpy as jnp
        import numpy as np
        import math
        EMBED_DIM = 256
        NUM_HEADS = 16
        HEAD_DIM = EMBED_DIM // NUM_HEADS
        INPUT_DIM = 256
        key = jax.random.key(seed)
        k_x, k_wqkv, k_wout = jax.random.split(key, 3)
        x = jax.random.normal(k_x, (4, 1, 512, INPUT_DIM), dtype=jnp.float32)

        def xavier(k, shape):
            fan_out, fan_in = shape
            bound = math.sqrt(6.0 / (fan_in + fan_out))
            return jax.random.uniform(k, shape, jnp.float32, -bound, bound)
        w_qkv = xavier(k_wqkv, (3 * EMBED_DIM, INPUT_DIM))
        b_qkv = jnp.zeros((3 * EMBED_DIM,), jnp.float32)
        w_out = xavier(k_wout, (EMBED_DIM, EMBED_DIM))
        b_out = jnp.zeros((EMBED_DIM,), jnp.float32)
        return {'x': x, 'w_qkv': w_qkv, 'b_qkv': b_qkv, 'w_out': w_out, 'b_out': b_out}
    _L0_tok_all = _L0_tok_setup()
    _L0_tok_in = {k: v for k, v in _L0_tok_all.items() if k in ('w_qkv', 'b_qkv', 'w_out', 'b_out')}
    del _L0_tok_all

    def _L0_attn_setup():
        import jax, jax.numpy as jnp
        import numpy as np
        from functools import partial
        B, S, D, H, DK, DV, DFF = (4, 512, 256, 8, 128, 128, 1024)
        EPS = 1e-06

        def rms_norm(x):
            return x * jax.lax.rsqrt(jnp.mean(x * x, axis=-1, keepdims=True) + EPS)

        def l2norm(x):
            return x * jax.lax.rsqrt(jnp.sum(x * x, axis=-1, keepdims=True) + EPS)

        def gated_delta_net(h, Wq, Wk, Wv, Wb, Wa, A_log, dt_bias, Wg, o_norm_w, Wo):
            b, s, _ = h.shape
            q = l2norm(jax.nn.silu(h @ Wq).reshape(b, s, H, DK))
            k = l2norm(jax.nn.silu(h @ Wk).reshape(b, s, H, DK))
            v = jax.nn.silu(h @ Wv).reshape(b, s, H, DV)
            beta = jax.nn.sigmoid(h @ Wb)
            g = -jnp.exp(A_log) * jax.nn.softplus(h @ Wa + dt_bias)
            alpha = jnp.exp(g)
            scale = DK ** (-0.5)
            tm = lambda a: jnp.moveaxis(a, 1, 0)
            qs, ks_, vs, als, bts = (tm(q), tm(k), tm(v), tm(alpha), tm(beta))

            def step(Sst, inp):
                q_t, k_t, v_t, a_t, b_t = inp
                Sst = Sst * a_t[..., None, None]
                kv = jnp.einsum('bhd,bhde->bhe', k_t, Sst)
                delta = (v_t - kv) * b_t[..., None]
                Sst = Sst + jnp.einsum('bhd,bhe->bhde', k_t, delta)
                o_t = jnp.einsum('bhd,bhde->bhe', q_t, Sst) * scale
                return (Sst, o_t)
            S0 = jnp.zeros((b, H, DK, DV), dtype=h.dtype)
            _, o = jax.lax.scan(step, S0, (qs, ks_, vs, als, bts))
            o = jnp.moveaxis(o, 0, 1)
            gate = (h @ Wg).reshape(b, s, H, DV)
            o = rms_norm(o) * o_norm_w * jax.nn.silu(gate)
            return o.reshape(b, s, H * DV) @ Wo
        key = jax.random.key(seed)
        ks = jax.random.split(key, 16)
        w = lambda k, shp: jax.random.normal(k, shp, dtype=jnp.float32) * 0.02
        return {'x': jax.random.normal(ks[0], (B, S, D), dtype=jnp.float32), 'Wq': w(ks[1], (D, H * DK)), 'Wk': w(ks[2], (D, H * DK)), 'Wv': w(ks[3], (D, H * DV)), 'Wb': w(ks[4], (D, H)), 'Wa': w(ks[5], (D, H)), 'A_log': jnp.log(jnp.linspace(1.0, 8.0, H).astype(jnp.float32)), 'dt_bias': jax.random.normal(ks[6], (H,), dtype=jnp.float32) * 0.1, 'Wg': w(ks[7], (D, H * DV)), 'o_norm_w': jnp.ones((DV,), dtype=jnp.float32), 'Wo': w(ks[8], (H * DV, D)), 'W_fc': w(ks[9], (D, DFF)), 'W_proj': w(ks[10], (DFF, D))}
    _L0_attn_all = _L0_attn_setup()
    _L0_attn_in = {k: v for k, v in _L0_attn_all.items() if k in ('Wq', 'Wk', 'Wv', 'Wb', 'Wa', 'A_log', 'dt_bias', 'Wg', 'o_norm_w', 'Wo', 'W_fc', 'W_proj')}
    del _L0_attn_all

    def _L0_ffn_setup():
        import jax, jax.numpy as jnp
        import numpy as np
        from jax import lax
        D = 256
        H = 352
        E = 8
        K = 2
        ROUTER_SCALE = 1.0

        def _expert(x, w1, b1, w3, b3, w2, b2):
            h = jax.nn.silu((x @ w1 + b1) * (x @ w3 + b3))
            return h @ w2 + b2
        key = jax.random.key(seed)
        ks = jax.random.split(key, 16)
        s = 0.02
        inp = {'x': jax.random.normal(ks[0], (2, 512, D), dtype=jnp.float32), 'gate_w': jax.random.normal(ks[1], (E, D), dtype=jnp.float32) * s, 'gate_b': jax.random.normal(ks[2], (E,), dtype=jnp.float32) * s, 'w1': jax.random.normal(ks[3], (E, D, H), dtype=jnp.float32) * s, 'b1': jax.random.normal(ks[4], (E, H), dtype=jnp.float32) * s, 'w3': jax.random.normal(ks[5], (E, D, H), dtype=jnp.float32) * s, 'b3': jax.random.normal(ks[6], (E, H), dtype=jnp.float32) * s, 'w2': jax.random.normal(ks[7], (E, H, D), dtype=jnp.float32) * s, 'b2': jax.random.normal(ks[8], (E, D), dtype=jnp.float32) * s, 'sw1': jax.random.normal(ks[9], (D, H), dtype=jnp.float32) * s, 'sb1': jax.random.normal(ks[10], (H,), dtype=jnp.float32) * s, 'sw3': jax.random.normal(ks[11], (D, H), dtype=jnp.float32) * s, 'sb3': jax.random.normal(ks[12], (H,), dtype=jnp.float32) * s, 'sw2': jax.random.normal(ks[13], (H, D), dtype=jnp.float32) * s, 'sb2': jax.random.normal(ks[14], (D,), dtype=jnp.float32) * s}
        return inp
    _L0_ffn_all = _L0_ffn_setup()
    _L0_ffn_in = {k: v for k, v in _L0_ffn_all.items() if k in ('gate_w', 'gate_b', 'w1', 'b1', 'w3', 'b3', 'w2', 'b2', 'sw1', 'sb1', 'sw3', 'sb3', 'sw2', 'sb2')}
    del _L0_ffn_all

    def _L1_attn_setup():
        import jax, jax.numpy as jnp
        import numpy as np
        import math
        H = 256
        NHALF = 32
        B = 4
        L = 1024
        DT_MIN, DT_MAX = (0.001, 0.1)

        def _kernel(log_dt, log_A_real, A_imag, C, L_len):
            dt = jnp.exp(log_dt)
            A = -jnp.exp(log_A_real) + 1j * A_imag
            Cc = C[..., 0] + 1j * C[..., 1]
            dtA = A * dt[:, None]
            Cw = Cc * (jnp.exp(dtA) - 1.0) / A
            l = jnp.arange(L_len)
            vand = jnp.exp(dtA[..., None] * l)
            K = 2.0 * jnp.einsum('hn,hnl->hl', Cw, vand).real
            return K
        key = jax.random.key(seed)
        k_x, k_dt, k_c, k_d = jax.random.split(key, 4)
        x = jax.random.normal(k_x, (B, L, H), dtype=jnp.float32)
        log_dt = jax.random.uniform(k_dt, (H,), dtype=jnp.float32) * (math.log(DT_MAX) - math.log(DT_MIN)) + math.log(DT_MIN)
        log_A_real = jnp.log(0.5 * jnp.ones((H, NHALF), dtype=jnp.float32))
        A_imag = math.pi * jnp.broadcast_to(jnp.arange(NHALF, dtype=jnp.float32), (H, NHALF))
        C = jax.random.normal(k_c, (H, NHALF, 2), dtype=jnp.float32) / math.sqrt(NHALF)
        D = jax.random.normal(k_d, (H,), dtype=jnp.float32)
        return {'x': x, 'log_dt': log_dt, 'log_A_real': log_A_real, 'A_imag': A_imag, 'C': C, 'D': D}
    _L1_attn_all = _L1_attn_setup()
    _L1_attn_in = {k: v for k, v in _L1_attn_all.items() if k in ('log_dt', 'log_A_real', 'A_imag', 'C', 'D')}
    del _L1_attn_all

    def _L1_ffn_setup():
        import jax, jax.numpy as jnp
        import numpy as np
        D_MODEL, D_FF, RANK = (256, 1024, 64)
        B, S = (4, 1024)
        key = jax.random.key(seed)
        ks = jax.random.split(key, 7)
        return {'x': jax.random.normal(ks[0], (B, S, D_MODEL), dtype=jnp.float32), 'U1': jax.random.normal(ks[1], (D_MODEL, RANK), dtype=jnp.float32) * 0.02, 'V1': jax.random.normal(ks[2], (RANK, D_FF), dtype=jnp.float32) * 0.02, 'b1': jnp.zeros((D_FF,), dtype=jnp.float32), 'U2': jax.random.normal(ks[3], (D_FF, RANK), dtype=jnp.float32) * 0.02, 'V2': jax.random.normal(ks[4], (RANK, D_MODEL), dtype=jnp.float32) * 0.02, 'b2': jnp.zeros((D_MODEL,), dtype=jnp.float32)}
    _L1_ffn_all = _L1_ffn_setup()
    _L1_ffn_in = {k: v for k, v in _L1_ffn_all.items() if k in ('U1', 'V1', 'b1', 'U2', 'V2', 'b2')}
    del _L1_ffn_all
    return {'x': x, 'L0_tok_w_qkv': _L0_tok_in['w_qkv'], 'L0_tok_b_qkv': _L0_tok_in['b_qkv'], 'L0_tok_w_out': _L0_tok_in['w_out'], 'L0_tok_b_out': _L0_tok_in['b_out'], 'L0_attn_Wq': _L0_attn_in['Wq'], 'L0_attn_Wk': _L0_attn_in['Wk'], 'L0_attn_Wv': _L0_attn_in['Wv'], 'L0_attn_Wb': _L0_attn_in['Wb'], 'L0_attn_Wa': _L0_attn_in['Wa'], 'L0_attn_A_log': _L0_attn_in['A_log'], 'L0_attn_dt_bias': _L0_attn_in['dt_bias'], 'L0_attn_Wg': _L0_attn_in['Wg'], 'L0_attn_o_norm_w': _L0_attn_in['o_norm_w'], 'L0_attn_Wo': _L0_attn_in['Wo'], 'L0_attn_W_fc': _L0_attn_in['W_fc'], 'L0_attn_W_proj': _L0_attn_in['W_proj'], 'L0_ffn_gate_w': _L0_ffn_in['gate_w'], 'L0_ffn_gate_b': _L0_ffn_in['gate_b'], 'L0_ffn_w1': _L0_ffn_in['w1'], 'L0_ffn_b1': _L0_ffn_in['b1'], 'L0_ffn_w3': _L0_ffn_in['w3'], 'L0_ffn_b3': _L0_ffn_in['b3'], 'L0_ffn_w2': _L0_ffn_in['w2'], 'L0_ffn_b2': _L0_ffn_in['b2'], 'L0_ffn_sw1': _L0_ffn_in['sw1'], 'L0_ffn_sb1': _L0_ffn_in['sb1'], 'L0_ffn_sw3': _L0_ffn_in['sw3'], 'L0_ffn_sb3': _L0_ffn_in['sb3'], 'L0_ffn_sw2': _L0_ffn_in['sw2'], 'L0_ffn_sb2': _L0_ffn_in['sb2'], 'L1_attn_log_dt': _L1_attn_in['log_dt'], 'L1_attn_log_A_real': _L1_attn_in['log_A_real'], 'L1_attn_A_imag': _L1_attn_in['A_imag'], 'L1_attn_C': _L1_attn_in['C'], 'L1_attn_D': _L1_attn_in['D'], 'L1_ffn_U1': _L1_ffn_in['U1'], 'L1_ffn_V1': _L1_ffn_in['V1'], 'L1_ffn_b1': _L1_ffn_in['b1'], 'L1_ffn_U2': _L1_ffn_in['U2'], 'L1_ffn_V2': _L1_ffn_in['V2'], 'L1_ffn_b2': _L1_ffn_in['b2']}

def reference(x, L0_tok_w_qkv, L0_tok_b_qkv, L0_tok_w_out, L0_tok_b_out, L0_attn_Wq, L0_attn_Wk, L0_attn_Wv, L0_attn_Wb, L0_attn_Wa, L0_attn_A_log, L0_attn_dt_bias, L0_attn_Wg, L0_attn_o_norm_w, L0_attn_Wo, L0_attn_W_fc, L0_attn_W_proj, L0_ffn_gate_w, L0_ffn_gate_b, L0_ffn_w1, L0_ffn_b1, L0_ffn_w3, L0_ffn_b3, L0_ffn_w2, L0_ffn_b2, L0_ffn_sw1, L0_ffn_sb1, L0_ffn_sw3, L0_ffn_sb3, L0_ffn_sw2, L0_ffn_sb2, L1_attn_log_dt, L1_attn_log_A_real, L1_attn_A_imag, L1_attn_C, L1_attn_D, L1_ffn_U1, L1_ffn_V1, L1_ffn_b1, L1_ffn_U2, L1_ffn_V2, L1_ffn_b2):
    import jax
    import jax.numpy as jnp

    def _L0_tok_ref(x, w_qkv, b_qkv, w_out, b_out):
        import jax, jax.numpy as jnp
        import numpy as np
        import math
        EMBED_DIM = 256
        NUM_HEADS = 16
        HEAD_DIM = EMBED_DIM // NUM_HEADS
        INPUT_DIM = 256
        B, y, S, _ = x.shape
        qkv = jnp.einsum('bysd,ed->byse', x, w_qkv) + b_qkv
        qkv = qkv.reshape(B, S, NUM_HEADS, 3 * HEAD_DIM).transpose(0, 2, 1, 3)
        q, k, v = jnp.split(qkv, 3, axis=-1)
        logits = jnp.einsum('bhqd,bhkd->bhqk', q, k) / math.sqrt(HEAD_DIM)
        attn = jax.nn.softmax(logits, axis=-1)
        vals = jnp.einsum('bhqk,bhkd->bhqd', attn, v)
        vals = vals.transpose(0, 2, 1, 3).reshape(B, S, EMBED_DIM)
        return jnp.einsum('bse,oe->bso', vals, w_out) + b_out

    def _L0_attn_ref(x, Wq, Wk, Wv, Wb, Wa, A_log, dt_bias, Wg, o_norm_w, Wo, W_fc, W_proj):
        import jax, jax.numpy as jnp
        import numpy as np
        from functools import partial
        B, S, D, H, DK, DV, DFF = (4, 512, 256, 8, 128, 128, 1024)
        EPS = 1e-06

        def rms_norm(x):
            return x * jax.lax.rsqrt(jnp.mean(x * x, axis=-1, keepdims=True) + EPS)

        def l2norm(x):
            return x * jax.lax.rsqrt(jnp.sum(x * x, axis=-1, keepdims=True) + EPS)

        def gated_delta_net(h, Wq, Wk, Wv, Wb, Wa, A_log, dt_bias, Wg, o_norm_w, Wo):
            b, s, _ = h.shape
            q = l2norm(jax.nn.silu(h @ Wq).reshape(b, s, H, DK))
            k = l2norm(jax.nn.silu(h @ Wk).reshape(b, s, H, DK))
            v = jax.nn.silu(h @ Wv).reshape(b, s, H, DV)
            beta = jax.nn.sigmoid(h @ Wb)
            g = -jnp.exp(A_log) * jax.nn.softplus(h @ Wa + dt_bias)
            alpha = jnp.exp(g)
            scale = DK ** (-0.5)
            tm = lambda a: jnp.moveaxis(a, 1, 0)
            qs, ks_, vs, als, bts = (tm(q), tm(k), tm(v), tm(alpha), tm(beta))

            def step(Sst, inp):
                q_t, k_t, v_t, a_t, b_t = inp
                Sst = Sst * a_t[..., None, None]
                kv = jnp.einsum('bhd,bhde->bhe', k_t, Sst)
                delta = (v_t - kv) * b_t[..., None]
                Sst = Sst + jnp.einsum('bhd,bhe->bhde', k_t, delta)
                o_t = jnp.einsum('bhd,bhde->bhe', q_t, Sst) * scale
                return (Sst, o_t)
            S0 = jnp.zeros((b, H, DK, DV), dtype=h.dtype)
            _, o = jax.lax.scan(step, S0, (qs, ks_, vs, als, bts))
            o = jnp.moveaxis(o, 0, 1)
            gate = (h @ Wg).reshape(b, s, H, DV)
            o = rms_norm(o) * o_norm_w * jax.nn.silu(gate)
            return o.reshape(b, s, H * DV) @ Wo
        ln_scale = 1.0
        h = gated_delta_net(ln_scale * rms_norm(x), Wq, Wk, Wv, Wb, Wa, A_log, dt_bias, Wg, o_norm_w, Wo)
        x = x + h
        m = ln_scale * rms_norm(x)
        y = jnp.square(jax.nn.relu(m @ W_fc)) @ W_proj
        return x + y

    def _L0_ffn_ref(x, gate_w, gate_b, w1, b1, w3, b3, w2, b2, sw1, sb1, sw3, sb3, sw2, sb2):
        import jax, jax.numpy as jnp
        import numpy as np
        from jax import lax
        D = 256
        H = 352
        E = 8
        K = 2
        ROUTER_SCALE = 1.0

        def _expert(x, w1, b1, w3, b3, w2, b2):
            h = jax.nn.silu((x @ w1 + b1) * (x @ w3 + b3))
            return h @ w2 + b2
        shape = x.shape
        xf = x.reshape(-1, D)
        T = xf.shape[0]
        scores = jax.nn.softmax(xf @ gate_w.T, axis=-1)
        biased = scores + gate_b
        _, idx = lax.top_k(biased, K)
        w = jnp.take_along_axis(scores, idx, axis=-1) * ROUTER_SCALE
        rw = jnp.zeros((T, E), dtype=xf.dtype).at[jnp.arange(T)[:, None], idx].add(w)
        h = jax.nn.silu((jnp.einsum('td,edh->teh', xf, w1) + b1) * (jnp.einsum('td,edh->teh', xf, w3) + b3))
        oe = jnp.einsum('teh,ehd->ted', h, w2) + b2
        y = jnp.einsum('te,ted->td', rw, oe)
        z = _expert(xf, sw1, sb1, sw3, sb3, sw2, sb2)
        return (y + z).reshape(shape)

    def _L1_attn_ref(x, log_dt, log_A_real, A_imag, C, D):
        import jax, jax.numpy as jnp
        import numpy as np
        import math
        H = 256
        NHALF = 32
        B = 4
        L = 1024
        DT_MIN, DT_MAX = (0.001, 0.1)

        def _kernel(log_dt, log_A_real, A_imag, C, L_len):
            dt = jnp.exp(log_dt)
            A = -jnp.exp(log_A_real) + 1j * A_imag
            Cc = C[..., 0] + 1j * C[..., 1]
            dtA = A * dt[:, None]
            Cw = Cc * (jnp.exp(dtA) - 1.0) / A
            l = jnp.arange(L_len)
            vand = jnp.exp(dtA[..., None] * l)
            K = 2.0 * jnp.einsum('hn,hnl->hl', Cw, vand).real
            return K
        xt = jnp.swapaxes(x, -1, -2)
        Lc = xt.shape[-1]
        K = _kernel(log_dt, log_A_real, A_imag, C, Lc)
        n = 2 * Lc
        Kf = jnp.fft.rfft(K.astype(jnp.float32), n=n)
        xf = jnp.fft.rfft(xt.astype(jnp.float32), n=n)
        y = jnp.fft.irfft(xf * Kf, n=n)[..., :Lc]
        y = y + xt * D[:, None]
        return jnp.swapaxes(y, -1, -2).astype(x.dtype)

    def _L1_ffn_ref(x, U1, V1, b1, U2, V2, b2):
        import jax, jax.numpy as jnp
        import numpy as np
        D_MODEL, D_FF, RANK = (256, 1024, 64)
        B, S = (4, 1024)
        P = jnp.einsum('bsd,dr->bsr', x, U1)
        H = jax.nn.gelu(jnp.einsum('bsr,rf->bsf', P, V1) + b1)
        Q = jnp.einsum('bsf,fr->bsr', H, U2)
        return jnp.einsum('bsr,rd->bsd', Q, V2) + b2
    h = _L0_tok_ref(x, L0_tok_w_qkv, L0_tok_b_qkv, L0_tok_w_out, L0_tok_b_out)
    h = h + _L0_attn_ref(_layernorm(h, axis=-1), L0_attn_Wq, L0_attn_Wk, L0_attn_Wv, L0_attn_Wb, L0_attn_Wa, L0_attn_A_log, L0_attn_dt_bias, L0_attn_Wg, L0_attn_o_norm_w, L0_attn_Wo, L0_attn_W_fc, L0_attn_W_proj)
    h = h + _L0_ffn_ref(_layernorm(h, axis=-1), L0_ffn_gate_w, L0_ffn_gate_b, L0_ffn_w1, L0_ffn_b1, L0_ffn_w3, L0_ffn_b3, L0_ffn_w2, L0_ffn_b2, L0_ffn_sw1, L0_ffn_sb1, L0_ffn_sw3, L0_ffn_sb3, L0_ffn_sw2, L0_ffn_sb2)
    h = h + _L1_attn_ref(_layernorm(h, axis=-1), L1_attn_log_dt, L1_attn_log_A_real, L1_attn_A_imag, L1_attn_C, L1_attn_D)
    h = h + _L1_ffn_ref(_layernorm(h, axis=-1), L1_ffn_U1, L1_ffn_V1, L1_ffn_b1, L1_ffn_U2, L1_ffn_V2, L1_ffn_b2)
    return h

_drawn_inputs = setup_inputs


def setup_inputs(seed=0):
    import zlib

    import numpy as np

    out = dict(_drawn_inputs(seed))
    spreads = {'L0_tok_b_qkv': (0.0, 0.1),
     'L0_tok_b_out': (0.0, 0.1),
     'L0_attn_o_norm_w': (1.0, 0.6),
     'L1_attn_log_A_real': (-0.6931471824645996, 0.6),
     'L1_ffn_b1': (0.0, 0.8),
     'L1_ffn_b2': (0.0, 0.8)}
    factors = {'L0_attn_Wb': 8.0,
     'L0_attn_Wa': 8.0,
     'L0_attn_A_log': 8.0,
     'L0_attn_dt_bias': 64.0,
     'L0_ffn_gate_w': 8.0,
     'L0_ffn_gate_b': 8.0,
     'L0_ffn_w1': 8.0,
     'L0_ffn_b1': 8.0,
     'L0_ffn_w3': 8.0,
     'L0_ffn_b3': 8.0,
     'L0_ffn_w2': 8.0,
     'L0_ffn_b2': 44.312,
     'L0_ffn_sw1': 3.411,
     'L0_ffn_sb1': 24.558,
     'L0_ffn_sw3': 3.683,
     'L0_ffn_sb3': 26.542,
     'L0_ffn_sw2': 3.239,
     'L0_ffn_sb2': 23.562,
     'L1_ffn_U1': 8.0,
     'L1_ffn_V1': 8.0,
     'L1_ffn_U2': 8.0,
     'L1_ffn_V2': 8.0}
    for name, (base, spread) in spreads.items():
        noise = np.random.default_rng([zlib.crc32(name.encode()), seed]).standard_normal(out[name].shape)
        drawn = base * np.exp(spread * noise) if base else spread * noise
        out[name] = jnp.asarray(drawn.astype(out[name].dtype))
    for name, factor in factors.items():
        out[name] = (out[name] * factor).astype(out[name].dtype)
    return out
```

```python
from contextlib import ExitStack

import numpy as np

import concourse.bass as bass
from concourse import mybir

F32 = mybir.dt.float32
F32R = mybir.dt.float32r
ACT = mybir.ActivationFunctionType
ALU = mybir.AluOpType
AXX = mybir.AxisListType.X

P = 128
B = 8
S = 512
D = 256
NJ = S // P
NT = B * NJ
ND = D // P
BANK = 512

NH, HD = 16, 16
GH, DK = 8, 128
GD = GH * DK
FF = 1024
NE, TOPK, EH = 8, 2, 352
RANK = 64
MODES = 32
NF = 2 * S
LN_EPS, RMS_EPS = 1e-5, 1e-6


class Handoff:

    def __init__(self, ctx, nc, name, uses=("x",), depth=1):
        self.depth = depth
        self.full = ctx.enter_context(nc.semaphore(name + "_full"))
        self.free = ctx.enter_context(nc.semaphore(name + "_free"))
        self.at = {u: k for k, u in enumerate(uses)}
        self.n = len(self.at)

    def open(self, eng):
        eng.sem_inc(self.free, self.depth)

    def wait_full(self, eng, turn, use="x"):
        eng.wait_ge(self.full, turn * self.n + (self.at[use] + 1))

    def wait_free(self, eng, turn, use="x"):
        eng.wait_ge(self.free, turn * self.n + (self.at[use] + 1))

    def wait_emptied(self, eng, turn, use="x"):
        eng.wait_ge(self.free, turn * self.n + (self.at[use] + 1 + self.depth))


class Chain:

    def __init__(self, sem, per):
        self.sem, self.per, self.k = sem, per, 0

    def __call__(self, eng, turn, ins):
        self.k += 1
        ins.then_inc(self.sem, 1)
        eng.wait_ge(self.sem, turn * self.per + self.k)

    def close(self):
        assert self.k == self.per, (self.k, self.per)


def bcast(ap, shape):
    while len(ap.shape) < len(shape):
        ap = ap.unsqueeze(len(ap.shape))
    return ap.broadcast_to(shape)


class Norm:

    DVE_STEPS = 4

    def __init__(self, ctx, nc, name):
        def sb(n, shape):
            return ctx.enter_context(nc.sbuf_tensor(f"{name}_{n}", shape, F32))

        self.x = sb("x", [P, NJ, D])
        self.stats, self.both = sb("stats", [P, NJ, 6]), sb("both", [P, NJ, 3])
        self.diff, self.mean, self.var = sb("diff", [P, NJ]), sb("mean", [P, NJ]), sb("var", [P, NJ])
        self.log, self.rstd = sb("log", [P, NJ]), sb("rstd", [P, NJ])
        self.var_done = ctx.enter_context(nc.semaphore(name + "_var_done"))
        self.log_done = ctx.enter_context(nc.semaphore(name + "_log_done"))
        self.rstd_done = ctx.enter_context(nc.semaphore(name + "_rstd_done"))
        self.x_done = ctx.enter_context(nc.semaphore(name + "_x_done"))

    def vector_statistics(self, dve, turn, after, resid):
        for j in range(NJ):
            ins = dve.bn_stats(self.stats[:, j, :], resid[:, bass.ds(turn * NJ + j, 1), :].rearrange("p a d -> p (a d)"))
        after(ins)
        after(dve.tensor_reduce(self.both[:, :, :], self.stats[:, :, :].rearrange("p j (a b) -> p j b a", a=2),
                                AXX, ALU.add))
        dve.tensor_scalar(self.mean[:, :], self.both[:, :, 1], 0.5, None, ALU.mult)
        after(dve.tensor_tensor(self.diff[:, :], self.stats[:, :, 1], self.stats[:, :, 4], ALU.subtract))
        dve.tensor_scalar(self.var[:, :], self.both[:, :, 2], 1.0 / D, LN_EPS, ALU.mult, ALU.add)
        after(dve.tensor_tensor(self.diff[:, :], self.diff[:, :], self.diff[:, :], ALU.mult))
        dve.scalar_tensor_tensor(out=self.var[:, :], in0=self.diff[:, :], scalar=0.25, in1=self.var[:, :],
                                 op0=ALU.mult, op1=ALU.add).then_inc(self.var_done, 1)

    def scalar_root(self, act, turn):
        act.wait_ge(self.var_done, turn + 1)
        act.activation(self.log[:, :], self.var[:, :], ACT.Ln).then_inc(self.log_done, 1)
        act.wait_ge(self.log_done, turn + 1)
        act.activation(self.rstd[:, :], self.log[:, :], ACT.Exp, scale=-0.5).then_inc(self.rstd_done, 1)

    def vector_scale(self, dve, turn, resid):
        dve.wait_ge(self.rstd_done, turn + 1)
        for j in range(NJ):
            dve.tensor_scalar(self.x[:, j, :], resid[:, bass.ds(turn * NJ + j, 1), :].rearrange("p a d -> p (a d)"),
                              self.mean[:, j:j + 1], self.rstd[:, j:j + 1], ALU.subtract, ALU.mult)\
                .then_inc(self.x_done, 1)


def transpose_sequence(pe, out, x, c, ident):
    for j in range(NJ):
        mm = pe.transpose(out[:, j * P:(j + 1) * P], x[:, j, c * P:(c + 1) * P], ident[:, :])
    return mm


def attention_stage(nc, w, resid, ident):
    TURNS = B
    PAIRS = NH // 2
    VW = HD + 1
    with ExitStack() as ctx:
        def sb(name, shape, dt=F32):
            return ctx.enter_context(nc.sbuf_tensor(name, shape, dt))

        def sem(name):
            return ctx.enter_context(nc.semaphore(name))

        wqkv = sb("wqkv", [P, ND, 3 * D])
        wout = sb("wout", [P, ND, D])
        bqk = sb("bqk", [P, 4])
        bv = sb("bv", [P, D])
        bo = sb("bo", [P, D])
        sel32 = sb("sel32", [P, 4, 4, P])
        sel = sb("sel", [P, 4, 4, P], F32R)
        selm32 = sb("selm32", [NH, 2, PAIRS, P])
        selm = sb("selm", [NH, 2, PAIRS, P], F32R)
        onerow = sb("onerow", [P, 1])

        x_in = sb("x_in", [P, NJ, D])
        xT = sb("xT", [P, ND, S])
        qk32 = sb("qk32", [P, 4, S])
        qk_hi = sb("qk_hi", [P, 4, S], F32R)
        qk_lo = sb("qk_lo", [P, 4, S], F32R)
        v1 = sb("v1", [P, NJ, NH, VW])
        qstack = sb("qstack", [P, PAIRS, S], F32R)
        kstack = sb("kstack", [P, PAIRS, S], F32R)
        maxima = sb("maxima", [P, NJ, NH])
        max_hi = sb("max_hi", [NH, S], F32R)
        max_lo = sb("max_lo", [NH, S], F32R)
        probs = sb("probs", [P, 2, NJ, S])
        rsum = sb("rsum", [P, 2, NJ])
        vals = sb("vals", [P, NJ, D])
        valsT = sb("valsT", [P, ND, S])

        scores = ctx.enter_context(nc.psum_tensor("scores", [P, 2, 2, BANK], F32))
        heads_out = ctx.enter_context(nc.psum_tensor("heads_out", [P, 2, BANK], F32))
        work = ctx.enter_context(nc.psum_tensor("work", [P, 2, BANK], F32))

        weights_in = sem("a_weights_in")
        consts_done = sem("a_consts_done")
        x_loaded = sem("x_loaded")
        x_used = sem("x_used")
        qk_hi_done = sem("qk_hi_done")
        qk_lo_done = sem("qk_lo_done")
        own = sem("a_vector_order")
        even = ["xT0", "qk0", "qk2", "v0"] + [f"k{p}" for p in range(PAIRS)] + ["max"] + \
               [f"m{p}" for p in range(1, PAIRS, 2)] + ["vT0", "out0"]
        odd = ["xT1", "qk1", "qk3", "v1"] + [f"q{p}" for p in range(PAIRS)] + \
              [f"m{p}" for p in range(0, PAIRS, 2)] + ["vT1", "out1"]
        bank = [Handoff(ctx, nc, "work0", even), Handoff(ctx, nc, "work1", odd)]
        units = [("s", h, u) for h in range(NH) for u in range(2)] + \
                [("t", h, u) for h in range(NH) for u in range(2)]
        score = [Handoff(ctx, nc, f"score{k}", units[k::2]) for k in range(2)]
        head = [Handoff(ctx, nc, f"head{k}", range(k, NH, 2)) for k in range(2)]

        block = ctx.enter_context(nc.Block())

        @block.sync
        def _(sp):
            for h in (*bank, *score, *head):
                h.open(sp)
            sp.sem_inc(x_used, 1)
            sp.dma_start(wqkv[:, :, :], w["wqkvT"].rearrange("(c p) n -> p c n", p=P)).then_inc(weights_in, 16)
            sp.dma_start(sel32[:, :, :, :], w["sel"]).then_inc(weights_in, 16)
            sp.dma_start(bqk[:, :], w["bqk"]).then_inc(weights_in, 16)
            sp.dma_start(bv[:, :], w["bv"].partition_broadcast(P)).then_inc(weights_in, 16)
            sp.dma_start(onerow[:, :], w["onerow"]).then_inc(weights_in, 16)
            sp.dma_start(selm32[:, :, :, :], w["selm"]).then_inc(weights_in, 16)
            sp.dma_start(wout[:, :, :], w["woutT"].rearrange("(c p) n -> p c n", p=P)).then_inc(weights_in, 16)
            sp.dma_start(bo[:, :], w["bo"].partition_broadcast(P)).then_inc(weights_in, 16)
            with sp.Fori(0, TURNS) as b:
                sp.wait_ge(x_used, b + 1)
                sp.dma_start(x_in[:, :, :], w["x"][b].rearrange("(j p) d -> p j d", p=P)).then_inc(x_loaded, 16)

        @block.gpsimd
        def _(pool):
            pool.memset(v1[:, :, :, HD:VW], 1.0).then_inc(consts_done, 1)
            pool.wait_ge(weights_in, 8 * 16)
            pool.tensor_copy(sel[:, :, :, :], sel32[:, :, :, :]).then_inc(consts_done, 1)
            pool.tensor_copy(selm[:, :, :, :], selm32[:, :, :, :]).then_inc(consts_done, 1)

        @block.scalar
        def _(act):
            act.wait_ge(weights_in, 8 * 16)
            with act.Fori(0, TURNS) as b:
                for c in range(ND):
                    bank[c].wait_full(act, b, f"xT{c}")
                    act.activation(xT[:, c, :], work[:, c, :], ACT.Copy).then_inc(bank[c].free, 1)
                for m in range(4):
                    bank[m % 2].wait_emptied(act, b, f"qk{m}")
                    act.activation(qk_hi[:, m, :], qk32[:, m, :], ACT.Copy).then_inc(qk_hi_done, 1)
                for p in range(PAIRS):
                    bank[0].wait_full(act, b, f"k{p}")
                    act.activation(kstack[:, p, :], work[:, 0, :], ACT.Identity, bias=onerow[:, 0:1])\
                       .then_inc(bank[0].free, 1)
                for p in range(1, PAIRS, 2):
                    bank[0].wait_full(act, b, f"m{p}")
                    act.activation(qstack[:, p, :], work[:, 0, :], ACT.Copy).then_inc(bank[0].free, 1)
                for h in range(NH):
                    for u in range(2):
                        score[u].wait_full(act, b, ("t", h, u))
                        if u == 0:
                            if h >= 2:
                                head[h % 2].wait_full(act, b, h - 2)
                        act.activation(probs[:, h % 2, 2 * u:2 * u + 2, :], scores[:, u, :, :], ACT.Exp)\
                           .then_inc(score[u].free, 1)
                for c in range(ND):
                    bank[c].wait_full(act, b, f"vT{c}")
                    act.activation(valsT[:, c, :], work[:, c, :], ACT.Copy).then_inc(bank[c].free, 1)

        @block.vector
        def _(dve):
            per = 1 + NH
            dve.wait_ge(weights_in, 8 * 16)
            dve.wait_ge(consts_done, 3)
            with dve.Fori(0, TURNS) as b:
                after = Chain(own, per)
                for m in range(4):
                    k = m % 2
                    bank[k].wait_full(dve, b, f"qk{m}")
                    dve.tensor_scalar(qk32[:, m, :], work[:, k, :], bqk[:, m:m + 1], 0.25 if m < 2 else 1.0,
                                      ALU.add, ALU.mult).then_inc(bank[k].free, 1)
                    dve.wait_ge(qk_hi_done, b * 4 + (m + 1))
                    dve.tensor_tensor(qk_lo[:, m, :], qk32[:, m, :], qk_hi[:, m, :].bitcast(F32), ALU.subtract)\
                       .then_inc(qk_lo_done, 1)
                for c in range(2):
                    bank[c].wait_full(dve, b, f"v{c}")
                    dve.tensor_tensor(v1[:, 2 * c:2 * c + 2, :, 0:HD],
                                      work[:, c, :].rearrange("p (j h e) -> p j h e", j=2, h=NH),
                                      bv[:, :].rearrange("p (h e) -> p h e", h=NH).unsqueeze(1)
                                      .broadcast_to([P, 2, NH, HD]), ALU.add).then_inc(bank[c].free, 1)
                for p in range(PAIRS):
                    bank[1].wait_full(dve, b, f"q{p}")
                    dve.tensor_copy(qstack[:, p, :], work[:, 1, :]).then_inc(bank[1].free, 1)
                for h in range(NH):
                    for u in range(2):
                        score[u].wait_full(dve, b, ("s", h, u))
                        dve.tensor_reduce(maxima[:, 2 * u:2 * u + 2, h], scores[:, u, :, :], AXX, ALU.max)\
                           .then_inc(score[u].free, 1)
                bank[0].wait_full(dve, b, "max")
                after(dve, b, dve.tensor_copy(max_hi[:, :], work[0:NH, 0, :]))
                dve.tensor_tensor(max_lo[:, :], work[0:NH, 0, :], max_hi[:, :].bitcast(F32), ALU.subtract)\
                   .then_inc(bank[0].free, 1)
                for p in range(0, PAIRS, 2):
                    bank[1].wait_full(dve, b, f"m{p}")
                    dve.tensor_copy(qstack[:, p, :], work[:, 1, :]).then_inc(bank[1].free, 1)
                for h in range(NH):
                    k = h % 2
                    head[k].wait_full(dve, b, h)
                    o = heads_out[:, k, 0:NJ * VW].rearrange("p (j e) -> p j e", j=NJ)
                    after(dve, b, dve.reciprocal(rsum[:, k, :], o[:, :, HD]))
                    dve.tensor_tensor(vals[:, :, h * HD:(h + 1) * HD], o[:, :, 0:HD],
                                      bcast(rsum[:, k, :], [P, NJ, HD]), ALU.mult).then_inc(head[k].free, 1)
                for c in range(2):
                    bank[c].wait_full(dve, b, f"out{c}")
                    dve.tensor_tensor(resid[:, bass.ds(b * NJ + 2 * c, 2), :],
                                      work[:, c, :].rearrange("p (j d) -> p j d", j=2),
                                      bo[:, :].unsqueeze(1).broadcast_to([P, 2, D]), ALU.add)\
                       .then_inc(bank[c].free, 1)
                after.close()

        @block.tensor
        def _(pe):
            def select(out, kind, part, tile, c, start, stop):
                return pe.matmul(out, sel[:, c, kind, :], part[:, tile, :], start=start, stop=stop)

            def values(b, h):
                k = h % 2
                for u in range(2):
                    score[u].wait_emptied(pe, b, ("t", h, u))
                head[k].wait_free(pe, b, h)
                for j in range(NJ):
                    for t in range(NJ):
                        mm = pe.matmul(heads_out[:, k, j * VW:(j + 1) * VW], probs[:, k, t, j * P:(j + 1) * P],
                                       v1[:, t, h, :], start=(t == 0), stop=(t == NJ - 1))
                mm.then_inc(head[k].full, 1)

            pe.wait_ge(weights_in, 8 * 16)
            pe.wait_ge(consts_done, 3)
            with pe.Fori(0, TURNS) as b:
                pe.wait_ge(x_loaded, b * 16 + 16)
                for c in range(ND):
                    bank[c].wait_free(pe, b, f"xT{c}")
                    for j in range(NJ):
                        mm = pe.transpose(work[:, c, j * P:(j + 1) * P], x_in[:, j, c * P:(c + 1) * P], ident[:, :])
                    mm.then_inc(bank[c].full, 1)
                pe.wait_ge(x_loaded, b * 16 + 16)
                for c in range(ND):
                    bank[c].wait_emptied(pe, b, f"xT{c}")
                pe.sem_inc(x_used, 1)
                for m in range(4):
                    k = m % 2
                    bank[k].wait_free(pe, b, f"qk{m}")
                    for c in range(ND):
                        mm = pe.matmul(work[:, k, :], wqkv[:, c, m * P:(m + 1) * P], xT[:, c, :],
                                       start=(c == 0), stop=(c == ND - 1))
                    mm.then_inc(bank[k].full, 1)
                for k in range(2):
                    bank[k].wait_free(pe, b, f"v{k}")
                    for j in range(2):
                        for c in range(ND):
                            mm = pe.matmul(work[:, k, j * D:(j + 1) * D],
                                           xT[:, c, (2 * k + j) * P:(2 * k + j + 1) * P], wqkv[:, c, 2 * D:3 * D],
                                           start=(c == 0), stop=(c == ND - 1))
                    mm.then_inc(bank[k].full, 1)
                for p in range(PAIRS):
                    m, c = p // 4, p % 4
                    pe.wait_ge(qk_lo_done, b * 4 + (m + 3))
                    for k, kind, name in ((0, 2, "k"), (1, 0, "q")):
                        bank[k].wait_free(pe, b, f"{name}{p}")
                        tile = m + 2 if name == "k" else m
                        select(work[:, k, :], kind, qk_hi, tile, c, True, False)
                        select(work[:, k, :], kind + 1, qk_lo, tile, c, False, True).then_inc(bank[k].full, 1)
                for h in range(NH):
                    p, r = h // 2, 64 * (h % 2)
                    bank[0].wait_emptied(pe, b, f"k{p}")
                    bank[1].wait_emptied(pe, b, f"q{p}")
                    for u in range(2):
                        score[u].wait_free(pe, b, ("s", h, u))
                        for j in range(2):
                            t = 2 * u + j
                            mm = pe.matmul(scores[:, u, j, :], qstack[r:r + 64, p, t * P:(t + 1) * P],
                                           kstack[r:r + 64, p, :], start=True, stop=True)
                        mm.then_inc(score[u].full, 1)
                for u in range(2):
                    score[u].wait_emptied(pe, b, ("s", NH - 1, u))
                bank[0].wait_free(pe, b, "max")
                for j in range(NJ):
                    mm = pe.transpose(work[0:NH, 0, j * P:(j + 1) * P], maxima[:, j, :], ident[:, :])
                mm.then_inc(bank[0].full, 1)
                bank[0].wait_emptied(pe, b, "max")
                for p in range(PAIRS):
                    m, c, k = p // 4, p % 4, (p + 1) % 2
                    bank[k].wait_free(pe, b, f"m{p}")
                    select(work[:, k, :], 0, qk_hi, m, c, True, False)
                    select(work[:, k, :], 1, qk_lo, m, c, False, False)
                    pe.matmul(work[:, k, :], selm[:, 0, p, :], max_hi[:, :], start=False, stop=False)
                    pe.matmul(work[:, k, :], selm[:, 1, p, :], max_lo[:, :], start=False, stop=True)\
                      .then_inc(bank[k].full, 1)
                for h in range(NH):
                    p, r = h // 2, 64 * (h % 2)
                    bank[(p + 1) % 2].wait_emptied(pe, b, f"m{p}")
                    for u in range(2):
                        score[u].wait_free(pe, b, ("t", h, u))
                        for j in range(2):
                            t = 2 * u + j
                            mm = pe.matmul(scores[:, u, j, :], kstack[r:r + 64, p, t * P:(t + 1) * P],
                                           qstack[r:r + 64, p, :], start=True, stop=True)
                        mm.then_inc(score[u].full, 1)
                    if h > 0:
                        values(b, h - 1)
                values(b, NH - 1)
                for k in range(2):
                    head[k].wait_emptied(pe, b, NH - 2 + k)
                for c in range(ND):
                    bank[c].wait_free(pe, b, f"vT{c}")
                    for j in range(NJ):
                        mm = pe.transpose(work[:, c, j * P:(j + 1) * P], vals[:, j, c * P:(c + 1) * P], ident[:, :])
                    mm.then_inc(bank[c].full, 1)
                for c in range(ND):
                    bank[c].wait_emptied(pe, b, f"vT{c}")
                for k in range(2):
                    bank[k].wait_free(pe, b, f"out{k}")
                    for j in range(2):
                        for c in range(ND):
                            mm = pe.matmul(work[:, k, j * D:(j + 1) * D],
                                           valsT[:, c, (2 * k + j) * P:(2 * k + j + 1) * P], wout[:, c, :],
                                           start=(c == 0), stop=(c == ND - 1))
                    mm.then_inc(bank[k].full, 1)


def delta_stage(nc, w, resid, ident):
    TURNS = NT
    LEVELS = 7
    HG = 4
    G = GH // HG
    HW = HG * P
    with ExitStack() as ctx:
        def sb(name, shape, dt=F32):
            return ctx.enter_context(nc.sbuf_tensor(name, shape, dt))

        def sem(name):
            return ctx.enter_context(nc.semaphore(name))

        wq4 = sb("wq4", [P, ND, 4, GD])
        wab = sb("wab", [P, ND, 2 * GH])
        wo = sb("wo", [P, GH, D])
        wfc = sb("wfc", [P, ND, FF])
        wproj = sb("wproj", [P, FF // P, D])
        dtb = sb("dtb", [P, GH])
        alog = sb("alog", [P, GH])
        expa = sb("expa", [P, GH])
        onw = sb("onw", [P, DK])
        upto = sb("upto", [P, P])
        beyond = sb("beyond", [P, P])
        ones = sb("ones", [P, P])
        level = sb("level", [P, LEVELS, P])
        keep = sb("keep", [P, NT])

        stats = sb("stats", [P, 6])
        both = sb("both", [P, 3])
        mv = sb("mv", [P, 2])
        var = sb("var", [P, 4])
        rs = sb("rs", [P, 4])
        lnv = sb("lnv", [P, 4])
        X = sb("X", [P, D])
        Rn = sb("Rn", [P, D])
        RT = sb("RT", [P, ND, P])
        qkvg = sb("qkvg", [P, 4, GH, DK])
        ab = sb("ab", [P, 2 * GH])
        ex = sb("ex", [P, 2 * GH])
        t1 = sb("t1", [P, GH])
        t2 = sb("t2", [P, GH])
        t3 = sb("t3", [P, GH])
        g = sb("g", [P, GH])
        beta = sb("beta", [P, GH])
        eg = sb("eg", [P, 3, GH])
        egk = sb("egk", [P, GH])
        egc = sb("egc", [P, GH])
        nbe = sb("nbe", [P, GH])
        norm = sb("norm", [P, 2, GH])
        normln = sb("normln", [P, 2, GH])
        rnorm = sb("rnorm", [P, 2, GH])
        gu = sb("gu", [P, GH, P])
        E = sb("E", [P, GH, P])
        nat = sb("nat", [P, 7, GH, DK])
        tra = sb("tra", [P, 5, GH, P])
        sq = tra[:, 3:5]
        mp = sb("mp", [P, GH, 2, P])
        T = sb("T", [P, GH, P])
        Y = sb("Y", [P, GH, P])
        Xl = sb("Xl", [P, GH, P])
        R = sb("R", [P, GH, DK])
        U = E
        O = sb("O", [P, GH, DK])
        St = sb("St", [P, GH, DK])
        og = T
        osum = sb("osum", [P, GH])
        oln = sb("oln", [P, GH])
        ro = sb("ro", [P, GH])
        ogT = Xl
        X2 = sb("X2", [P, D])
        hid, hT = gu, R
        y = sb("y", [P, D])

        wide = ctx.enter_context(nc.psum_tensor("g_wide", [P, 2, BANK], F32))
        stateb = ctx.enter_context(nc.psum_tensor("g_state", [P, 2, BANK], F32))
        tri_a = ctx.enter_context(nc.psum_tensor("g_tri_a", [P, 2, BANK], F32))
        tri_b = ctx.enter_context(nc.psum_tensor("g_tri_b", [P, 2, BANK], F32))

        weights_in = sem("g_weights_in")
        vec = sem("g_vector_order")
        sca = sem("g_scalar_order")
        poo = sem("g_pool_order")
        root = Handoff(ctx, nc, "g_root", ["ln", "rms", "qk", "o", "rms2"], depth=0)
        gate = Handoff(ctx, nc, "g_gate")
        wides = [[], []]
        order = [("RT",), ("ab",)] + [("proj", n, f) for n in range(4) for f in range(2)] + \
                [("decay", k) for k in range(G)] + [("tra", n, k) for n in range(5) for k in range(G)] + \
                [("mp", k) for k in range(GH // 2)] + [("ogT", k) for k in range(G)] + \
                [("mT",), ("pad",)] + [("hid", k) for k in range(2)]
        order.remove(("pad",))
        place = {}
        for n, use in enumerate(order):
            place[use] = n % 2
            wides[n % 2].append(use)
        wb = [Handoff(ctx, nc, f"g_wide{k}", wides[k]) for k in range(2)]
        sbk = [Handoff(ctx, nc, f"g_state{k}", (["cum"] if k == 0 else []) + ["ks", "u", "o", "s"] +
                       (["wo"] if k == 0 else ["down"])) for k in range(2)]
        ta = [Handoff(ctx, nc, f"g_tri_a{k}", [("t", 0)] + [x for l in range(1, LEVELS) for x in
              ([("a", l), ("t", l)] if l < LEVELS - 1 else [("a", l)])]) for k in range(G)]
        tb = [Handoff(ctx, nc, f"g_tri_b{k}", range(1, LEVELS)) for k in range(G)]
        pool_sq = sem("g_pool_sq")
        pool_gu = sem("g_pool_gu")
        pool_E = sem("g_pool_E")
        pool_nat = sem("g_pool_nat")
        pool_og = sem("g_pool_og")
        dve_rnorm = sem("g_rnorm_scaled")
        dve_beta = sem("g_beta_done")
        dve_g = sem("g_g_done")
        dve_scal = sem("g_scalars_done")
        dve_nat = sem("g_vector_nat")
        Y_done = [sem(f"g_Y{k}") for k in range(G)]
        R_done = sem("g_R_done")
        S_done = sem("g_S_done")
        og_done = sem("g_og_done")
        rn_done = sem("g_rn_done")
        hid_relu = sem("g_hid_relu")

        block = ctx.enter_context(nc.Block())

        def heads(ap, k):
            return ap[:, HG * k:HG * (k + 1), :]

        def grp(ap, k):
            return ap[:, k, :].rearrange("p (h e) -> p h e", h=HG)

        @block.sync
        def _(sp):
            for h in (*wb, *sbk, *ta, *tb):
                h.open(sp)
            for n, name in enumerate(("Wq", "Wk", "Wv", "Wg")):
                sp.dma_start(wq4[:, :, n, :], w[name].rearrange("(c p) n -> p c n", p=P)).then_inc(weights_in, 16)
            sp.dma_start(wab[:, :, :], w["wab"].rearrange("(c p) n -> p c n", p=P)).then_inc(weights_in, 16)
            sp.dma_start(wo[:, :, :], w["Wo"].rearrange("(c p) n -> p c n", p=P)).then_inc(weights_in, 16)
            sp.dma_start(wfc[:, :, :], w["Wfc"].rearrange("(c p) n -> p c n", p=P)).then_inc(weights_in, 16)
            sp.dma_start(wproj[:, :, :], w["Wproj"].rearrange("(c p) n -> p c n", p=P)).then_inc(weights_in, 16)
            sp.dma_start(dtb[:, :], w["dtb"].partition_broadcast(P)).then_inc(weights_in, 16)
            sp.dma_start(alog[:, :], w["alog"].partition_broadcast(P)).then_inc(weights_in, 16)
            sp.dma_start(onw[:, :], w["onw"].partition_broadcast(P)).then_inc(weights_in, 16)
            sp.dma_start(upto[:, :], w["upto"]).then_inc(weights_in, 16)
            sp.dma_start(beyond[:, :], w["beyond"]).then_inc(weights_in, 16)
            sp.dma_start(level[:, :, :], w["level"]).then_inc(weights_in, 16)
            sp.dma_start(keep[:, :], w["keep"].partition_broadcast(P)).then_inc(weights_in, 16)
            sp.dma_start(ones[:, :], w["ones"]).then_inc(weights_in, 16)
        IN = 16 * 16

        @block.gpsimd
        def _(pool):
            pool.wait_ge(weights_in, IN)
            with pool.Fori(0, TURNS) as t:
                for n in range(2):
                    for f in range(2):
                        wb[place["proj", n, f]].wait_emptied(pool, t, ("proj", n, f))
                    pool.tensor_tensor(sq[:, n, :, :], qkvg[:, n, :, :], qkvg[:, n, :, :], ALU.mult)\
                        .then_inc(pool_sq, 1)
                pool.wait_ge(dve_g, t + 1)
                pool.tensor_tensor(gu[:, :, :], upto[:, :].unsqueeze(1).broadcast_to([P, GH, P]),
                                   bcast(g[:, :], [P, GH, P]), ALU.mult).then_inc(pool_gu, 1)
                for f in range(2):
                    wb[place["proj", 3, f]].wait_emptied(pool, t, ("proj", 3, f))
                pool.tensor_tensor(qkvg[:, 3, :, :], qkvg[:, 3, :, :],
                                   onw[:, :].unsqueeze(1).broadcast_to([P, GH, DK]), ALU.mult)\
                    .then_inc(poo, 1)
                for k in range(G):
                    wb[place["decay", k]].wait_emptied(pool, t, ("decay", k))
                pool.tensor_tensor(E[:, :, :], E[:, :, :], upto[:, :].unsqueeze(1).broadcast_to([P, GH, P]),
                                   ALU.mult).then_inc(pool_E, 1)
                pool.wait_ge(dve_scal, t + 1)
                pool.wait_ge(dve_nat, t * 5 + 1)
                pool.tensor_tensor(nat[:, 5, :, :], nat[:, 0, :, :], bcast(eg[:, 1, :], [P, GH, DK]),
                                   ALU.mult).then_inc(pool_nat, 1)
                for f in range(2):
                    wb[place["proj", 2, f]].wait_emptied(pool, t, ("proj", 2, f))
                pool.tensor_tensor(nat[:, 6, :, :], qkvg[:, 2, :, :], bcast(beta[:, :], [P, GH, DK]),
                                   ALU.mult).then_inc(pool_nat, 1)
                for k in range(G):
                    sbk[k].wait_emptied(pool, t, "o")
                pool.wait_ge(poo, t + 1)
                pool.tensor_tensor(sq[:, 0, :, :], O[:, :, :], O[:, :, :], ALU.mult).then_inc(pool_sq, 1)
                pool.tensor_tensor(og[:, :, :], O[:, :, :], qkvg[:, 3, :, :], ALU.mult).then_inc(pool_og, 1)

        @block.scalar
        def _(act):
            act.wait_ge(weights_in, IN)
            act.activation(expa[:, :], alog[:, :], ACT.Exp).then_inc(gate.free, 1)
            with act.Fori(0, TURNS) as t:
                after = Chain(sca, 5)

                def inv_root(use, out, ln, v):
                    root.wait_full(act, t, use)
                    after(act, t, act.activation(ln, v, ACT.Ln))
                    act.activation(out, ln, ACT.Exp, scale=-0.5).then_inc(root.free, 1)

                inv_root("ln", rs[:, 0:1], lnv[:, 0:1], var[:, 0:1])
                inv_root("rms", rs[:, 1:2], lnv[:, 1:2], var[:, 1:2])
                k = place["RT",]
                wb[k].wait_full(act, t, ("RT",))
                act.activation(RT[:, :, :], wide[:, k, 0:D].rearrange("p (c t) -> p c t", c=ND), ACT.Copy)\
                   .then_inc(wb[k].free, 1)
                for n in range(4):
                    for f in range(2):
                        k = place["proj", n, f]
                        wb[k].wait_full(act, t, ("proj", n, f))
                        act.activation(qkvg[:, n, HG * f:HG * (f + 1), :], grp(wide, k), ACT.Silu)\
                           .then_inc(wb[k].free, 1)
                gate.wait_full(act, t)
                act.activation(ex[:, :], ab[:, :], ACT.Exp).then_inc(gate.free, 1)
                inv_root("qk", rnorm[:, :, :], normln[:, :, :], norm[:, :, :])
                sbk[0].wait_full(act, t, "cum")
                act.activation(eg[:, :, :], stateb[:, 0, 0:3 * GH].rearrange("p (a h) -> p a h", a=3), ACT.Exp)\
                   .then_inc(sbk[0].free, 1)
                for k in range(G):
                    b = place["decay", k]
                    wb[b].wait_full(act, t, ("decay", k))
                    act.activation(heads(E, k), grp(wide, b), ACT.Exp).then_inc(wb[b].free, 1)
                for n in range(5):
                    b = place["tra", n, 0]
                    wb[b].wait_full(act, t, ("tra", n, 0))
                    act.activation(heads(tra[:, n], 0), grp(wide, b), ACT.Copy).then_inc(wb[b].free, 1)
                for l in range(LEVELS - 1):
                    for k in range(G):
                        ta[k].wait_full(act, t, ("t", l))
                        act.activation(heads(T, k), grp(tri_a, k), ACT.Copy).then_inc(ta[k].free, 1)
                for use, to in (("u", U), ("o", O)):
                    for k in range(G):
                        sbk[k].wait_full(act, t, use)
                        act.activation(heads(to, k), grp(stateb, k), ACT.Copy).then_inc(sbk[k].free, 1)
                inv_root("o", ro[:, :], oln[:, :], osum[:, :])
                for k in range(G):
                    b = place["ogT", k]
                    wb[b].wait_full(act, t, ("ogT", k))
                    act.activation(heads(ogT, k), grp(wide, b), ACT.Copy).then_inc(wb[b].free, 1)
                inv_root("rms2", rs[:, 2:3], lnv[:, 2:3], var[:, 2:3])
                b = place["mT",]
                wb[b].wait_full(act, t, ("mT",))
                act.activation(RT[:, :, :], wide[:, b, 0:D].rearrange("p (c t) -> p c t", c=ND), ACT.Copy)\
                   .then_inc(wb[b].free, 1)
                for k in range(2):
                    b = place["hid", k]
                    wb[b].wait_full(act, t, ("hid", k))
                    act.activation(heads(hid, k), grp(wide, b), ACT.Relu).then_inc(hid_relu, 1)
                after.close()

        @block.vector
        def _(dve):
            dve.wait_ge(weights_in, IN)
            dve.memset(St[:, :, :], 0.0).then_inc(vec, 1)
            dve.wait_ge(vec, 1)
            dve.wait_ge(gate.free, 1)
            with dve.Fori(0, TURNS) as t:
                inner = Chain(vec, 43)

                def after(ins):
                    inner.k += 1
                    ins.then_inc(vec, 1)
                    dve.wait_ge(vec, t * inner.per + inner.k + 1)

                after(dve.bn_stats(stats[:, :], resid[:, bass.ds(t, 1), :].rearrange("p a d -> p (a d)")))
                after(dve.tensor_reduce(both[:, :], stats[:, :].rearrange("p (a b) -> p b a", a=2), AXX, ALU.add))
                after(dve.tensor_tensor(mv[:, 1:2], stats[:, 1:2], stats[:, 4:5], ALU.subtract))
                after(dve.tensor_tensor(mv[:, 1:2], mv[:, 1:2], mv[:, 1:2], ALU.mult))
                after(dve.tensor_scalar(var[:, 3:4], both[:, 2:3], 1.0 / D, LN_EPS, ALU.mult, ALU.add))
                dve.tensor_scalar(mv[:, 0:1], both[:, 1:2], 0.5, None, ALU.mult)
                dve.scalar_tensor_tensor(out=var[:, 0:1], in0=mv[:, 1:2], scalar=0.25, in1=var[:, 3:4],
                                         op0=ALU.mult, op1=ALU.add).then_inc(root.full, 1)
                root.wait_emptied(dve, t, "ln")
                after(dve.tensor_scalar(X[:, :], resid[:, bass.ds(t, 1), :].rearrange("p a d -> p (a d)"),
                                        mv[:, 0:1], rs[:, 0:1], ALU.subtract, ALU.mult))

                def mean_square(x, col, use):
                    after(dve.tensor_tensor_reduce(out=y[:, :], in0=x, in1=x, scale=1.0 / D, scalar=0.0,
                                                   op0=ALU.mult, op1=ALU.add, accum_out=var[:, 3:4]))
                    dve.tensor_scalar(var[:, col:col + 1], var[:, 3:4], RMS_EPS, None, ALU.add)\
                       .then_inc(root.full, 1)
                    root.wait_emptied(dve, t, use)
                    dve.tensor_scalar(Rn[:, :], x, rs[:, col:col + 1], None, ALU.mult).then_inc(rn_done, 1)

                mean_square(X[:, :], 1, "rms")
                k = place["ab",]
                wb[k].wait_full(dve, t, ("ab",))
                after(dve.tensor_tensor(t1[:, :], wide[:, k, GH:2 * GH], dtb[:, :], ALU.add))
                after(dve.scalar_tensor_tensor(out=ab[:, GH:2 * GH], in0=t1[:, :], scalar=-1.0, in1=t1[:, :],
                                               op0=ALU.mult, op1=ALU.min))
                dve.tensor_scalar(ab[:, 0:GH], wide[:, k, 0:GH], -1.0, None, ALU.mult).then_inc(wb[k].free, 1)
                wb[k].wait_emptied(dve, t, ("ab",))
                after(dve.tensor_scalar(t1[:, :], t1[:, :], 0.0, None, ALU.max))
                dve.sem_inc(gate.full, 1)
                gate.wait_emptied(dve, t)
                after(dve.tensor_scalar(beta[:, :], ex[:, 0:GH], 1.0, None, ALU.add))
                dve.reciprocal(beta[:, :], beta[:, :]).then_inc(dve_beta, 1)
                after(dve.tensor_scalar(t2[:, :], ex[:, GH:2 * GH], 2.0, None, ALU.add))
                after(dve.reciprocal(t2[:, :], t2[:, :]))
                after(dve.tensor_tensor(t2[:, :], t2[:, :], ex[:, GH:2 * GH], ALU.mult))
                after(dve.tensor_tensor(t3[:, :], t2[:, :], t2[:, :], ALU.mult))
                after(dve.tensor_scalar(g[:, :], t3[:, :], 1.0 / 17, 1.0 / 15, ALU.mult, ALU.add))
                for n in (13, 11, 9, 7, 5, 3, 1):
                    after(dve.tensor_tensor(g[:, :], g[:, :], t3[:, :], ALU.mult))
                    after(dve.tensor_scalar(g[:, :], g[:, :], 1.0 / n, None, ALU.add))
                after(dve.tensor_tensor(g[:, :], g[:, :], t2[:, :], ALU.mult))
                after(dve.scalar_tensor_tensor(out=g[:, :], in0=g[:, :], scalar=2.0, in1=t1[:, :],
                                               op0=ALU.mult, op1=ALU.add))
                after(dve.scalar_tensor_tensor(out=g[:, :], in0=g[:, :], scalar=-1.0, in1=expa[:, :],
                                               op0=ALU.mult, op1=ALU.mult))
                dve.tensor_scalar(g[:, :], g[:, :], -200.0, None, ALU.max).then_inc(dve_g, 1)
                for n in range(2):
                    dve.wait_ge(pool_sq, t * 3 + (n + 1))
                    after(dve.tensor_reduce(norm[:, n, :], sq[:, n, :, :], AXX, ALU.add))
                dve.tensor_scalar(norm[:, :, :], norm[:, :, :], RMS_EPS, None, ALU.add).then_inc(root.full, 1)
                root.wait_emptied(dve, t, "qk")
                after(dve.tensor_scalar(rnorm[:, 0, :], rnorm[:, 0, :], DK ** -0.5, None, ALU.mult))
                sbk[0].wait_emptied(dve, t, "cum")
                after(dve.tensor_scalar(egk[:, :], eg[:, 0, :], keep[:, bass.ds(t, 1)], None, ALU.mult))
                dve.tensor_scalar(egc[:, :], eg[:, 2, :], keep[:, bass.ds(t, 1)], None, ALU.mult)\
                   .then_inc(dve_scal, 1)
                dve.wait_ge(dve_beta, t + 1)
                after(dve.scalar_tensor_tensor(out=nbe[:, :], in0=egk[:, :], scalar=-1.0, in1=beta[:, :],
                                               op0=ALU.mult, op1=ALU.mult))

                def scaled(n, src, by):
                    dve.tensor_tensor(nat[:, n, :, :], src, bcast(by, [P, GH, DK]), ALU.mult)\
                       .then_inc(dve_nat, 1)

                scaled(0, qkvg[:, 1, :, :], rnorm[:, 1, :])
                scaled(3, qkvg[:, 0, :, :], rnorm[:, 0, :])
                dve.wait_ge(dve_nat, t * 5 + 2)
                scaled(1, nat[:, 0, :, :], beta[:, :])
                scaled(2, nat[:, 0, :, :], nbe[:, :])
                scaled(4, nat[:, 3, :, :], egk[:, :])
                for n in range(5):
                    b = place["tra", n, 1]
                    wb[b].wait_full(dve, t, ("tra", n, 1))
                    dve.tensor_copy(heads(tra[:, n], 1), grp(wide, b)).then_inc(wb[b].free, 1)
                dve.wait_ge(pool_E, t + 1)
                for k in range(GH // 2):
                    b = place["mp", k]
                    wb[b].wait_full(dve, t, ("mp", k))
                    dve.tensor_tensor(mp[:, 2 * k:2 * k + 2, :, :],
                                      wide[:, b, :].rearrange("p (h a e) -> p h a e", h=2, a=2),
                                      E[:, 2 * k:2 * k + 2, :].unsqueeze(2).broadcast_to([P, 2, 2, P]),
                                      ALU.mult).then_inc(wb[b].free, 1)
                for k in range(G):
                    wb[place["mp", 2 * k + 1]].wait_emptied(dve, t, ("mp", 2 * k + 1))
                    wb[place["mp", 2 * k]].wait_emptied(dve, t, ("mp", 2 * k))
                    after(dve.tensor_tensor(heads(Xl, k), mp[:, HG * k:HG * (k + 1), 0, :],
                                            level[:, 0, :].unsqueeze(1).broadcast_to([P, HG, P]), ALU.mult))
                    dve.tensor_tensor(heads(Y, k), ident[:, :].unsqueeze(1).broadcast_to([P, HG, P]),
                                      heads(Xl, k), ALU.subtract).then_inc(Y_done[k], 1)
                for l in range(1, LEVELS):
                    for k in range(G):
                        ta[k].wait_full(dve, t, ("a", l))
                        dve.tensor_tensor(heads(Xl, k), grp(tri_a, k),
                                          level[:, l, :].unsqueeze(1).broadcast_to([P, HG, P]), ALU.mult)\
                           .then_inc(ta[k].free, 1)
                    for k in range(G):
                        tb[k].wait_full(dve, t, l)
                        dve.tensor_tensor(heads(Y, k), heads(Y, k), grp(tri_b, k), ALU.subtract)\
                           .then_inc(tb[k].free, 1)
                dve.wait_ge(pool_nat, t * 2 + 2)
                for k in range(G):
                    sbk[k].wait_full(dve, t, "ks")
                    dve.tensor_tensor(heads(R, k), grp(stateb, k), heads(nat[:, 6], k), ALU.add)\
                       .then_inc(sbk[k].free, 1)
                for k in range(G):
                    sbk[k].wait_full(dve, t, "s")
                    for h in range(HG):
                        ins = dve.scalar_tensor_tensor(out=St[:, HG * k + h, :], in0=St[:, HG * k + h, :],
                                                       scalar=egc[:, HG * k + h:HG * k + h + 1],
                                                       in1=stateb[:, k, h * P:(h + 1) * P],
                                                       op0=ALU.mult, op1=ALU.add)
                    ins.then_inc(sbk[k].free, 1)
                dve.wait_ge(pool_sq, t * 3 + 3)
                after(dve.tensor_reduce(osum[:, :], sq[:, 0, :, :], AXX, ALU.add))
                dve.tensor_scalar(osum[:, :], osum[:, :], 1.0 / DK, RMS_EPS, ALU.mult, ALU.add)\
                   .then_inc(root.full, 1)
                root.wait_emptied(dve, t, "o")
                dve.wait_ge(pool_og, t + 1)
                dve.tensor_tensor(og[:, :, :], og[:, :, :], bcast(ro[:, :], [P, GH, DK]), ALU.mult)\
                   .then_inc(og_done, 1)
                sbk[0].wait_full(dve, t, "wo")
                dve.tensor_tensor(X2[:, :], stateb[:, 0, 0:D], X[:, :], ALU.add).then_inc(sbk[0].free, 1)
                sbk[0].wait_emptied(dve, t, "wo")
                mean_square(X2[:, :], 2, "rms2")
                for k in range(2):
                    b = place["hid", k]
                    dve.wait_ge(hid_relu, t * 2 + (k + 1))
                    dve.tensor_tensor(heads(hT, k), grp(wide, b), heads(hid, k), ALU.mult)\
                       .then_inc(wb[b].free, 1)
                sbk[1].wait_full(dve, t, "down")
                dve.tensor_tensor(y[:, :], stateb[:, 1, 0:D], X2[:, :], ALU.add).then_inc(sbk[1].free, 1)
                sbk[1].wait_emptied(dve, t, "down")
                row = resid[:, bass.ds(t, 1), :].rearrange("p a d -> p (a d)")
                after(dve.tensor_tensor(row, row, y[:, :], ALU.add))
                inner.close()

        @block.tensor
        def _(pe):
            def transposes(use, out, src, n):
                for i in range(n):
                    mm = pe.transpose(out[:, i * P:(i + 1) * P], src(i), ident[:, :])
                return mm

            pe.wait_ge(weights_in, IN)
            with pe.Fori(0, TURNS) as t:
                def to_wide(use):
                    k = place[use]
                    wb[k].wait_free(pe, t, use)
                    return wide[:, k, :], wb[k]

                pe.wait_ge(rn_done, t * 2 + 1)
                out, bank = to_wide(("RT",))
                transposes(None, out, lambda i: Rn[:, i * P:(i + 1) * P], ND).then_inc(bank.full, 1)
                wb[place["RT",]].wait_emptied(pe, t, ("RT",))
                out, bank = to_wide(("ab",))
                for c in range(ND):
                    mm = pe.matmul(out[:, 0:2 * GH], RT[:, c, :], wab[:, c, :], start=(c == 0), stop=(c == ND - 1))
                mm.then_inc(bank.full, 1)
                for n in range(4):
                    for f in range(2):
                        out, bank = to_wide(("proj", n, f))
                        for c in range(ND):
                            mm = pe.matmul(out, RT[:, c, :], wq4[:, c, n, f * BANK:(f + 1) * BANK],
                                           start=(c == 0), stop=(c == ND - 1))
                        mm.then_inc(bank.full, 1)
                pe.wait_ge(dve_g, t + 1)
                sbk[0].wait_free(pe, t, "cum")
                for n, mask in enumerate((upto, beyond, ones)):
                    mm = pe.matmul(stateb[:, 0, n * GH:(n + 1) * GH], mask[:, :], g[:, :], start=True, stop=True)
                mm.then_inc(sbk[0].full, 1)
                pe.wait_ge(pool_gu, t + 1)
                for k in range(G):
                    out, bank = to_wide(("decay", k))
                    pe.matmul(out, beyond[:, :], heads(gu, k), start=True, stop=True).then_inc(bank.full, 1)
                for n in range(5):
                    pe.wait_ge(dve_nat, t * 5 + (1, 3, 4, 5, 5)[n])
                    for k in range(G):
                        out, bank = to_wide(("tra", n, k))
                        transposes(None, out, lambda i: nat[:, n, HG * k + i, :], HG).then_inc(bank.full, 1)
                for k in range(GH // 2):
                    wb[place["tra", 3, k // 2]].wait_emptied(pe, t, ("tra", 3, k // 2))
                    out, bank = to_wide(("mp", k))
                    for i in range(2):
                        h = 2 * k + i
                        pe.matmul(out[:, 2 * i * P:(2 * i + 1) * P], tra[:, 0, h, :], tra[:, 1, h, :],
                                  start=True, stop=True)
                        mm = pe.matmul(out[:, (2 * i + 1) * P:(2 * i + 2) * P], tra[:, 0, h, :], tra[:, 3, h, :],
                                       start=True, stop=True)
                    mm.then_inc(bank.full, 1)
                for l in range(LEVELS):
                    for k in range(G):
                        if l == 0:
                            pe.wait_ge(Y_done[k], t + 1)
                        else:
                            ta[k].wait_emptied(pe, t, ("t", l - 1))
                            ta[k].wait_free(pe, t, ("a", l))
                            for h in range(HG):
                                mm = pe.matmul(tri_a[:, k, h * P:(h + 1) * P], mp[:, HG * k + h, 0, :],
                                               T[:, HG * k + h, :], start=True, stop=True)
                            mm.then_inc(ta[k].full, 1)
                    if l > 0:
                        for k in range(G):
                            ta[k].wait_emptied(pe, t, ("a", l))
                            tb[k].wait_free(pe, t, l)
                            for h in range(HG):
                                mm = pe.matmul(tri_b[:, k, h * P:(h + 1) * P], Xl[:, HG * k + h, :],
                                               Y[:, HG * k + h, :], start=True, stop=True)
                            mm.then_inc(tb[k].full, 1)
                    if l < LEVELS - 1:
                        for k in range(G):
                            if l > 0:
                                tb[k].wait_emptied(pe, t, l)
                            ta[k].wait_free(pe, t, ("t", l))
                            transposes(None, tri_a[:, k, :], lambda i: Y[:, HG * k + i, :], HG)\
                                .then_inc(ta[k].full, 1)
                for k in range(G):
                    wb[place["tra", 2, k]].wait_emptied(pe, t, ("tra", 2, k))
                    sbk[k].wait_free(pe, t, "ks")
                    for h in range(HG):
                        mm = pe.matmul(stateb[:, k, h * P:(h + 1) * P], tra[:, 2, HG * k + h, :],
                                       St[:, HG * k + h, :], start=True, stop=True)
                    mm.then_inc(sbk[k].full, 1)
                for k in range(G):
                    tb[k].wait_emptied(pe, t, LEVELS - 1)
                    sbk[k].wait_emptied(pe, t, "ks")
                    for h in range(HG):
                        mm = pe.matmul(stateb[:, k, h * P:(h + 1) * P], Y[:, HG * k + h, :],
                                       R[:, HG * k + h, :], start=True, stop=True)
                    mm.then_inc(sbk[k].full, 1)
                for k in range(G):
                    wb[place["tra", 4, k]].wait_emptied(pe, t, ("tra", 4, k))
                    sbk[k].wait_emptied(pe, t, "u")
                    for h in range(HG):
                        out = stateb[:, k, h * P:(h + 1) * P]
                        pe.matmul(out, tra[:, 4, HG * k + h, :], St[:, HG * k + h, :], start=True, stop=False)
                        mm = pe.matmul(out, mp[:, HG * k + h, 1, :], U[:, HG * k + h, :], start=False, stop=True)
                    mm.then_inc(sbk[k].full, 1)
                pe.wait_ge(pool_nat, t * 2 + 1)
                for k in range(G):
                    sbk[k].wait_emptied(pe, t, "o")
                    for h in range(HG):
                        mm = pe.matmul(stateb[:, k, h * P:(h + 1) * P], nat[:, 5, HG * k + h, :],
                                       U[:, HG * k + h, :], start=True, stop=True)
                    mm.then_inc(sbk[k].full, 1)
                pe.wait_ge(og_done, t + 1)
                for k in range(G):
                    out, bank = to_wide(("ogT", k))
                    transposes(None, out, lambda i: og[:, HG * k + i, :], HG).then_inc(bank.full, 1)
                sbk[0].wait_free(pe, t, "wo")
                for h in range(GH):
                    if h % HG == 0:
                        wb[place["ogT", h // HG]].wait_emptied(pe, t, ("ogT", h // HG))
                    mm = pe.matmul(stateb[:, 0, 0:D], ogT[:, h, :], wo[:, h, :], start=(h == 0), stop=(h == GH - 1))
                mm.then_inc(sbk[0].full, 1)
                pe.wait_ge(rn_done, t * 2 + 2)
                out, bank = to_wide(("mT",))
                transposes(None, out, lambda i: Rn[:, i * P:(i + 1) * P], ND).then_inc(bank.full, 1)
                wb[place["mT",]].wait_emptied(pe, t, ("mT",))
                for k in range(2):
                    out, bank = to_wide(("hid", k))
                    for f in range(4):
                        for c in range(ND):
                            mm = pe.matmul(out[:, f * P:(f + 1) * P], wfc[:, c, (4 * k + f) * P:(4 * k + f + 1) * P],
                                           RT[:, c, :], start=(c == 0), stop=(c == ND - 1))
                    mm.then_inc(bank.full, 1)
                sbk[1].wait_free(pe, t, "down")
                for f in range(FF // P):
                    if f % 4 == 0:
                        wb[place["hid", f // 4]].wait_emptied(pe, t, ("hid", f // 4))
                    mm = pe.matmul(stateb[:, 1, 0:D], hT[:, f, :], wproj[:, f, :], start=(f == 0),
                                   stop=(f == FF // P - 1))
                mm.then_inc(sbk[1].full, 1)


def experts_stage(nc, w, resid, ident):
    TURNS = B
    NX = NE + 1
    SIZES = [128, 128, EH - 256]
    NM = len(SIZES)
    with ExitStack() as ctx:
        def sb(name, shape, dt=F32):
            return ctx.enter_context(nc.sbuf_tensor(name, shape, dt))

        def sem(name):
            return ctx.enter_context(nc.semaphore(name))

        norm = Norm(ctx, nc, "m")
        gw = sb("gw", [P, ND, NE])
        gb = sb("gb", [P, NE])
        before = sb("before", [P, NE, NE])
        w13 = sb("w13", [P, NX, 2, ND, EH])
        b13 = sb("b13", [P, NX, 2, NM])
        w2 = sb("w2", [P, NX, NM, D])
        XT = sb("m_XT", [P, ND, S])
        lg = sb("lg", [P, NJ, NE])
        eq = sb("eq", [P, NJ, NE, NE])
        gt = sb("gt", [P, NJ, NE, NE])
        small = sb("small", [P, NJ])
        score = sb("score", [P, NJ, NE])
        biased = sb("biased", [P, NJ, NE])
        rank = sb("rank", [P, NJ, NE])
        rw = sb("rw", [P, NJ, NX])
        up = sb("up", [P, 2, S])
        pre = sb("pre", [P, 2, S])
        hT = sb("m_hT", [P, 2, NM, S])

        ups = ctx.enter_context(nc.psum_tensor("m_ups", [P, 2, 2, BANK], F32))
        outs = ctx.enter_context(nc.psum_tensor("m_outs", [P, 2, 2, BANK], F32))

        tiles = [(e, m) for e in range(NX) for m in range(NM)]
        first = [["XT0", "gate"], ["XT1"]]
        hb = [Handoff(ctx, nc, f"m_up{k}", first[k] + [x for n, x in enumerate(tiles) if n % 2 == k]) for k in range(2)]
        hid_done = sem("m_hid_done")
        ob = [Handoff(ctx, nc, f"m_out{k}", range(k, NX, 2)) for k in range(2)]
        up_done = sem("m_up_done")
        small_in = sem("m_small_in")
        w_in = [sem(f"m_w_in{e}") for e in range(NX)]
        vec = sem("m_vector_order")
        ones_done = sem("m_ones_done")
        lg_done = sem("m_logits")
        lg_exp = sem("m_exps")
        VSTEPS = Norm.DVE_STEPS + 10

        block = ctx.enter_context(nc.Block())

        @block.sync
        def _(sp):
            for h in (*hb, *ob):
                h.open(sp)
            sp.dma_start(gw[:, :, :], w["gw"].rearrange("(c p) n -> p c n", p=P)).then_inc(small_in, 16)
            sp.dma_start(gb[:, :], w["gb"].partition_broadcast(P)).then_inc(small_in, 16)
            sp.dma_start(before[:, :, :], w["before"].partition_broadcast(P)
                         .rearrange("p a (e f) -> p (a e) f", e=NE)).then_inc(small_in, 16)
            sp.dma_start(b13[:, :, :, :], w["b13"]).then_inc(small_in, 16)
            for e in range(NX):
                sp.dma_start(w13[:, e, :, :, :], w["w13"][e]).then_inc(w_in[e], 16)
                sp.dma_start(w2[:, e, 0:2, :], w["w2a"][e]).then_inc(w_in[e], 16)
                sp.dma_start(w2[0:SIZES[2] + 1, e, 2, :], w["w2b"][e]).then_inc(w_in[e], 16)

        @block.gpsimd
        def _(pool):
            pool.memset(hT[SIZES[2]:SIZES[2] + 1, :, NM - 1, :], 1.0).then_inc(ones_done, 1)
            pool.wait_ge(ones_done, 1)
            pool.memset(rw[:, :, NE:NX], 1.0).then_inc(ones_done, 1)

        @block.scalar
        def _(act):
            act.wait_ge(small_in, 4 * 16)
            with act.Fori(0, TURNS) as t:
                norm.scalar_root(act, t)
                for c in range(ND):
                    hb[c].wait_full(act, t, f"XT{c}")
                    act.activation(XT[:, c, :], ups[:, c, 0, :], ACT.Copy).then_inc(hb[c].free, 1)
                act.wait_ge(lg_done, t + 1)
                act.activation(lg[:, :, :], lg[:, :, :], ACT.Exp).then_inc(lg_exp, 1)

                def silu(n):
                    e, m = tiles[n]
                    s, k = SIZES[m], n % 2
                    hb[k].wait_emptied(act, t, (e, m))
                    if e >= 2:
                        ob[e % 2].wait_full(act, t, e - 2)
                    act.activation(hT[0:s, e % 2, m, :], pre[0:s, k, :], ACT.Silu).then_inc(hid_done, 1)

                for n, (e, m) in enumerate(tiles):
                    s, k = SIZES[m], n % 2
                    hb[k].wait_full(act, t, (e, m))
                    act.activation(up[0:s, k, :], ups[0:s, k, 0, :], ACT.Identity, bias=b13[0:s, e, 0, m:m + 1])\
                       .then_inc(up_done, 1)
                    if n > 0:
                        silu(n - 1)
                silu(len(tiles) - 1)

        @block.vector
        def _(dve):
            dve.wait_ge(small_in, 4 * 16)
            dve.wait_ge(ones_done, 2)
            with dve.Fori(0, TURNS) as t:
                order = Chain(vec, VSTEPS)

                def after(ins):
                    order(dve, t, ins)

                norm.vector_statistics(dve, t, after, resid)
                norm.vector_scale(dve, t, resid)
                hb[0].wait_full(dve, t, "gate")
                logits = ups[:, 0, 0, 0:NJ * NE].rearrange("p (j e) -> p j e", j=NJ)
                after(dve.tensor_reduce(small[:, :], logits, AXX, ALU.max))
                dve.tensor_tensor(lg[:, :, :], logits, bcast(small[:, :], [P, NJ, NE]), ALU.subtract)\
                    .then_inc(hb[0].free, 1)
                hb[0].wait_emptied(dve, t, "gate")
                dve.sem_inc(lg_done, 1)
                dve.wait_ge(lg_exp, t + 1)
                after(dve.tensor_reduce(small[:, :], lg[:, :, :], AXX, ALU.add))
                after(dve.reciprocal(small[:, :], small[:, :]))
                after(dve.tensor_tensor(score[:, :, :], lg[:, :, :], bcast(small[:, :], [P, NJ, NE]), ALU.mult))
                after(dve.tensor_tensor(biased[:, :, :], score[:, :, :],
                                        gb[:, :].unsqueeze(1).broadcast_to([P, NJ, NE]), ALU.add))
                mine = bcast(biased[:, :, :], [P, NJ, NE, NE])
                other = biased[:, :, :].unsqueeze(2).broadcast_to([P, NJ, NE, NE])
                dve.tensor_tensor(gt[:, :, :, :], other, mine, ALU.is_gt)
                after(dve.tensor_tensor(eq[:, :, :, :], other, mine, ALU.is_equal))
                after(dve.tensor_tensor(eq[:, :, :, :], eq[:, :, :, :],
                                        before[:, :, :].unsqueeze(1).broadcast_to([P, NJ, NE, NE]), ALU.mult))
                after(dve.tensor_tensor(gt[:, :, :, :], gt[:, :, :, :], eq[:, :, :, :], ALU.add))
                after(dve.tensor_reduce(rank[:, :, :], gt[:, :, :, :], AXX, ALU.add))
                after(dve.scalar_tensor_tensor(out=rw[:, :, 0:NE], in0=rank[:, :, :], scalar=float(TOPK) - 0.5,
                                               in1=score[:, :, :], op0=ALU.is_lt, op1=ALU.mult))

                def combine(e):
                    ob[e % 2].wait_full(dve, t, e)
                    if e >= 1:
                        ob[(e - 1) % 2].wait_emptied(dve, t, e - 1)
                    for j in range(NJ):
                        row = resid[:, bass.ds(t * NJ + j, 1), :].rearrange("p a d -> p (a d)")
                        ins = dve.scalar_tensor_tensor(
                            out=row, in0=outs[:, e % 2, j // 2, (j % 2) * D:(j % 2 + 1) * D],
                            scalar=rw[:, j, e:e + 1], in1=row, op0=ALU.mult, op1=ALU.add)
                    ins.then_inc(ob[e % 2].free, 1)

                for n, (e, m) in enumerate(tiles):
                    s, k = SIZES[m], n % 2
                    dve.wait_ge(up_done, t * len(tiles) + (n + 1))
                    dve.scalar_tensor_tensor(out=pre[0:s, k, :], in0=ups[0:s, k, 1, :],
                                             scalar=b13[0:s, e, 1, m:m + 1], in1=up[0:s, k, :],
                                             op0=ALU.add, op1=ALU.mult).then_inc(hb[k].free, 1)
                    if e >= 1 and m == NM - 1:
                        combine(e - 1)
                combine(NX - 1)
                order.close()

        @block.tensor
        def _(pe):
            pe.wait_ge(small_in, 4 * 16)
            pe.wait_ge(ones_done, 2)
            with pe.Fori(0, TURNS) as t:
                pe.wait_ge(norm.x_done, t * NJ + NJ)
                for c in range(ND):
                    hb[c].wait_free(pe, t, f"XT{c}")
                    transpose_sequence(pe, ups[:, c, 0, :], norm.x, c, ident).then_inc(hb[c].full, 1)
                for c in range(ND):
                    hb[c].wait_emptied(pe, t, f"XT{c}")
                hb[0].wait_free(pe, t, "gate")
                for j in range(NJ):
                    for c in range(ND):
                        mm = pe.matmul(ups[:, 0, 0, j * NE:(j + 1) * NE], XT[:, c, j * P:(j + 1) * P], gw[:, c, :],
                                       start=(c == 0), stop=(c == ND - 1))
                mm.then_inc(hb[0].full, 1)

                def down(e):
                    k = e % 2
                    pe.wait_ge(hid_done, t * len(tiles) + (e + 1) * NM)
                    ob[k].wait_free(pe, t, e)
                    for j in range(NJ):
                        for m, s in enumerate(SIZES):
                            rows = s + (m == NM - 1)
                            mm = pe.matmul(outs[:, k, j // 2, (j % 2) * D:(j % 2 + 1) * D],
                                           hT[0:rows, k, m, j * P:(j + 1) * P], w2[0:rows, e, m, :],
                                           start=(m == 0), stop=(m == NM - 1))
                    mm.then_inc(ob[k].full, 1)

                for n, (e, m) in enumerate(tiles):
                    s, k = SIZES[m], n % 2
                    if m == 0:
                        pe.wait_ge(w_in[e], 3 * 16)
                    hb[k].wait_free(pe, t, (e, m))
                    for i in range(2):
                        for c in range(ND):
                            mm = pe.matmul(ups[0:s, k, i, :], w13[:, e, i, c, m * P:m * P + s], XT[:, c, :],
                                           start=(c == 0), stop=(c == ND - 1))
                    mm.then_inc(hb[k].full, 1)
                    if e >= 1 and m == 1:
                        down(e - 1)
                down(NX - 1)


def convolution_stage(nc, w, resid, ident):
    LA, LB = 32, 16
    ROWS = 2 * MODES
    GROUPS = D // 4
    NFT = NF // P
    HALF = NFT // 2
    TURNS = B
    with ExitStack() as outer:
        fwd = outer.enter_context(nc.sbuf_tensor("fwd", [P, NJ, NF], F32))
        inv = outer.enter_context(nc.sbuf_tensor("inv", [P, NFT, S], F32))
        ka = outer.enter_context(nc.sbuf_tensor("ka", [P, HALF, 2, D], F32))
        kb = outer.enter_context(nc.sbuf_tensor("kb", [P, HALF, 2, D], F32))
        mats_in = outer.enter_context(nc.semaphore("mats_in"))
        convolution_kernel(nc, w, fwd, inv, ka, kb, mats_in, LA, LB, ROWS, GROUPS, NFT, HALF)

        with ExitStack() as ctx:
            def sb(name, shape, dt=F32):
                return ctx.enter_context(nc.sbuf_tensor(name, shape, dt))

            def sem(name):
                return ctx.enter_context(nc.semaphore(name))

            norm = Norm(ctx, nc, "c")
            pa = sb("pa", [P, 2, 2, D])
            pb = sb("pb", [P, 2, 2, D])
            ys = sb("ys", [P, HALF, 2, D])
            spec = ctx.enter_context(nc.psum_tensor("spec", [P, HALF, 2, D], F32))
            back = ctx.enter_context(nc.psum_tensor("back", [P, 2, 2, D], F32))
            sp_h = [Handoff(ctx, nc, f"c_spec{k}") for k in range(HALF)]
            pr_h = [Handoff(ctx, nc, f"c_prod{k}", range(k, HALF, 2)) for k in range(2)]
            back_h = [Handoff(ctx, nc, f"c_back{k}") for k in range(2)]
            ys_done = sem("c_ys_done")
            vec = sem("c_vector_order")

            block = ctx.enter_context(nc.Block())

            @block.sync
            def _(sp):
                for h in (*sp_h, *pr_h, *back_h):
                    h.open(sp)

            @block.scalar
            def _(act):
                with act.Fori(0, TURNS) as t:
                    norm.scalar_root(act, t)

            @block.gpsimd
            def _(pool):
                with pool.Fori(0, TURNS) as t:
                    for m in range(HALF):
                        sp_h[m].wait_emptied(pool, t)
                        pool.tensor_tensor(ys[:, m, :, :], pa[:, m % 2, :, :], pb[:, m % 2, :, :], ALU.add)\
                            .then_inc(pr_h[m % 2].free, 1)

            @block.vector
            def _(dve):
                with dve.Fori(0, TURNS) as t:
                    order = Chain(vec, Norm.DVE_STEPS)
                    norm.vector_statistics(dve, t, lambda ins: order(dve, t, ins), resid)
                    norm.vector_scale(dve, t, resid)
                    for m in range(HALF):
                        sp_h[m].wait_full(dve, t)
                        pr_h[m % 2].wait_free(dve, t, m)
                        dve.tensor_tensor(pa[:, m % 2, :, :], spec[:, m, 0, :].unsqueeze(1).broadcast_to([P, 2, D]),
                                          ka[:, m, :, :], ALU.mult)
                        dve.tensor_tensor(pb[:, m % 2, :, :], spec[:, m, 1, :].unsqueeze(1).broadcast_to([P, 2, D]),
                                          kb[:, m, :, :], ALU.mult).then_inc(sp_h[m].free, 1)
                    for k in range(2):
                        back_h[k].wait_full(dve, t)
                        rows = resid[:, bass.ds(t * NJ + 2 * k, 2), :]
                        dve.tensor_tensor(rows, rows, back[:, k, :, :], ALU.add).then_inc(back_h[k].free, 1)
                    order.close()

            @block.tensor
            def _(pe):
                with pe.Fori(0, TURNS) as t:
                    pe.wait_ge(norm.x_done, t * NJ + NJ)
                    for m in range(HALF):
                        sp_h[m].wait_free(pe, t)
                        for part in range(2):
                            f = (part * HALF + m) * P
                            for j in range(NJ):
                                mm = pe.matmul(spec[:, m, part, :], fwd[:, j, f:f + P], norm.x[:, j, :],
                                               start=(j == 0), stop=(j == NJ - 1))
                        mm.then_inc(sp_h[m].full, 1)
                    for m in (HALF - 2, HALF - 1):
                        pr_h[m % 2].wait_emptied(pe, t, m)
                    for j in range(NJ):
                        if j % 2 == 0:
                            back_h[j // 2].wait_free(pe, t)
                        for f in range(NFT):
                            mm = pe.matmul(back[:, j // 2, j % 2, :], inv[:, f, j * P:(j + 1) * P],
                                           ys[:, f % HALF, f // HALF, :], start=(f == 0), stop=(f == NFT - 1))
                        if j % 2 == 1:
                            mm.then_inc(back_h[j // 2].full, 1)


def convolution_kernel(nc, w, fwd, inv, ka, kb, mats_in, LA, LB, ROWS, GROUPS, NFT, HALF):
    CH = 8
    NCA, NCB = LA // CH, LB // CH
    MAGIC = 1.5 * 2.0 ** 23
    TWO_PI_HI = 6.28125
    TWO_PI_LO = 2 * np.pi - TWO_PI_HI
    PI = 3.1415925
    with ExitStack() as ctx:
        def sb(name, shape, dt=F32):
            return ctx.enter_context(nc.sbuf_tensor(name, shape, dt))

        def sem(name):
            return ctx.enter_context(nc.semaphore(name))

        par = sb("par", [ROWS, 5, D])
        lv = sb("lv", [ROWS, LA + LB])
        names = ("dt", "are", "dre", "dim", "em1", "er", "sn", "cs", "hs", "nr", "ni", "wr", "wi",
                 "den", "u", "v", "al", "be")
        v = {n: sb("k_" + n, [ROWS, D]) for n in names}
        th = sb("th", [ROWS, CH, D])
        kk = sb("kk", [ROWS, CH, D])
        mg = sb("mg", [ROWS, CH, D])
        arg = sb("arg", [ROWS, CH, D])
        cz = sb("cz", [ROWS, CH, D])
        q = sb("q", [ROWS, GROUPS, 4, LA])
        pz = sb("pz", [ROWS, LB, D])
        kl = sb("kl", [P, LB, GROUPS])
        kt = sb("kt", [P, NJ, D])
        drow = sb("drow", [1, D])
        scratch = nc.dram_tensor("k_scratch", (S, D), F32).ap()
        kp = ctx.enter_context(nc.psum_tensor("kp", [P, 8, 8, 64], F32))

        params_in = sem("params_in")
        vec = sem("k_vector_order")
        tables_done = sem("k_tables_done")
        ask = sem("k_ask")
        ans = sem("k_answer")
        products = sem("k_products")
        gathered = sem("k_gathered")
        stored = sem("k_stored")
        loaded = sem("k_loaded")
        row_done = sem("k_row_done")
        spectra = sem("k_spectra")

        block = ctx.enter_context(nc.Block())

        @block.sync
        def _(sp):
            for half in range(2):
                rows = slice(MODES * half, MODES * (half + 1))
                sp.dma_start(par[rows, 0, :], w["log_dt"].partition_broadcast(MODES)
                             .rearrange("p a h -> p (a h)")).then_inc(params_in, 16)
                sp.dma_start(par[rows, 1:5, :], w["modes"]).then_inc(params_in, 16)
            sp.dma_start(lv[:, :], w["lvals"].partition_broadcast(ROWS)
                         .rearrange("p a l -> p (a l)")).then_inc(params_in, 16)
            sp.dma_start(drow[:, :], w["skip"]).then_inc(params_in, 16)
            sp.dma_start(fwd[:, :, :], w["fwd"].rearrange("(j p) f -> p j f", p=P)).then_inc(mats_in, 16)
            sp.dma_start(inv[:, :, :], w["inv"].rearrange("(m p) l -> p m l", p=P)).then_inc(mats_in, 16)
            sp.wait_ge(gathered, 8)
            dst = scratch.rearrange("(a b) (j g) -> j a b g", b=LB, j=4)
            for j in range(4):
                sp.dma_start(dst[j], kl[32 * j:32 * j + 32, :, :]).then_inc(stored, 16)
            sp.wait_ge(stored, 4 * 16)
            sp.dma_start(kt[:, :, :], scratch.rearrange("(t p) h -> p t h", p=P)).then_inc(loaded, 16)

        asked = [(ACT.Exp, v["dt"], par[:, 0, :], 1.0), (ACT.Exp, v["are"], par[:, 1, :], 1.0),
                 (ACT.Tanh, v["em1"], v["dre"][:, :], 0.5)]
        trig = [(v["sn"], v["sn"]), (v["cs"], v["cs"]), (v["hs"], v["hs"])]

        @block.scalar
        def _(act):
            act.wait_ge(params_in, 6 * 16)
            for n, (f, out, src, scale) in enumerate(asked):
                if n == 2:
                    act.wait_ge(ask, 1)
                act.activation(out[:, :], src, f, scale=scale).then_inc(ans, 1)
            act.wait_ge(ask, 2)
            for out, src in trig:
                act.activation(out[:, :], src[:, :], ACT.Sin).then_inc(ans, 1)
            for n in range(NCA + NCB):
                act.wait_ge(ask, 3 + n)
                act.activation(mg[:, :, :], mg[:, :, :], ACT.Exp).then_inc(ans, 1)
                act.activation(arg[:, :, :], arg[:, :, :], ACT.Sin).then_inc(ans, 1)
                if n >= NCA:
                    act.activation(cz[:, :, :], cz[:, :, :], ACT.Sin).then_inc(ans, 1)

        @block.vector
        def _(dve):
            count = [0]

            def after(ins):
                count[0] += 1
                ins.then_inc(vec, 1)
                dve.wait_ge(vec, count[0])

            def tt(o, a, b, op):
                after(dve.tensor_tensor(v[o][:, :], v[a][:, :], v[b][:, :], op))

            def stt(o, a, s, b, op0, op1):
                after(dve.scalar_tensor_tensor(out=v[o][:, :], in0=v[a][:, :], scalar=s, in1=v[b][:, :],
                                               op0=op0, op1=op1))

            def ts(o, a, s1, s2, op0, op1):
                after(dve.tensor_scalar(v[o][:, :], v[a][:, :], s1, s2, op0, op1))

            def reduce_angle(angle, turns):
                after(dve.tensor_scalar(turns, angle, 1 / (2 * np.pi), MAGIC, ALU.mult, ALU.add))
                after(dve.tensor_scalar(turns, turns, -MAGIC, None, ALU.add))
                after(dve.scalar_tensor_tensor(out=angle, in0=turns, scalar=-TWO_PI_HI, in1=angle,
                                               op0=ALU.mult, op1=ALU.add))
                after(dve.scalar_tensor_tensor(out=angle, in0=turns, scalar=-TWO_PI_LO, in1=angle,
                                               op0=ALU.mult, op1=ALU.add))
                after(dve.tensor_scalar(angle, angle, PI, -PI, ALU.min, ALU.max))

            def cosine_angle(out, angle):
                after(dve.scalar_tensor_tensor(out=out, in0=angle, scalar=-1.0, in1=angle,
                                               op0=ALU.mult, op1=ALU.min))
                after(dve.tensor_scalar(out, out, float(np.pi / 2), None, ALU.add))

            M, A_, S_ = ALU.mult, ALU.add, ALU.subtract
            dve.wait_ge(params_in, 6 * 16)
            dve.wait_ge(ans, 2)
            ts("are", "are", -1.0, None, M, ALU.bypass)
            tt("dre", "are", "dt", M)
            after(dve.tensor_tensor(v["dim"][:, :], par[:, 2, :], v["dt"][:, :], M))
            dve.sem_inc(ask, 1)
            after(dve.tensor_copy(v["sn"][:, :], v["dim"][:, :]))
            reduce_angle(v["sn"][:, :], v["u"][:, :])
            cosine_angle(v["cs"][:, :], v["sn"][:, :])
            ts("hs", "sn", 0.5, None, M, ALU.bypass)
            dve.sem_inc(ask, 1)
            dve.wait_ge(ans, 6)
            ts("u", "em1", -1.0, 1.0, M, A_)
            after(dve.reciprocal(v["u"][:, :], v["u"][:, :]))
            stt("em1", "em1", 2.0, "u", M, M)
            ts("er", "em1", 1.0, None, A_, ALU.bypass)
            tt("nr", "em1", "cs", M)
            tt("hs", "hs", "hs", M)
            stt("nr", "hs", -2.0, "nr", M, A_)
            tt("ni", "er", "sn", M)
            after(dve.tensor_tensor(v["wr"][:, :], par[:, 3, :], v["nr"][:, :], M))
            after(dve.tensor_tensor(v["u"][:, :], par[:, 4, :], v["ni"][:, :], M))
            tt("wr", "wr", "u", S_)
            after(dve.tensor_tensor(v["wi"][:, :], par[:, 3, :], v["ni"][:, :], M))
            after(dve.tensor_tensor(v["u"][:, :], par[:, 4, :], v["nr"][:, :], M))
            tt("wi", "wi", "u", A_)
            tt("den", "are", "are", M)
            after(dve.tensor_tensor(v["u"][:, :], par[:, 2, :], par[:, 2, :], M))
            tt("den", "den", "u", A_)
            after(dve.reciprocal(v["den"][:, :], v["den"][:, :]))
            tt("u", "wr", "are", M)
            after(dve.tensor_tensor(v["v"][:, :], v["wi"][:, :], par[:, 2, :], M))
            tt("u", "u", "v", A_)
            tt("u", "u", "den", M)
            tt("v", "wi", "are", M)
            after(dve.tensor_tensor(v["wr"][:, :], v["wr"][:, :], par[:, 2, :], M))
            tt("v", "v", "wr", S_)
            tt("v", "v", "den", M)
            re, im = slice(0, MODES), slice(MODES, ROWS)
            after(dve.tensor_scalar(v["al"][re, :], v["u"][re, :], 2.0, None, M))
            after(dve.tensor_scalar(v["be"][re, :], v["v"][re, :], -2.0, None, M))
            after(dve.tensor_scalar(v["al"][im, :], v["v"][im, :], -2.0, None, M))
            after(dve.tensor_scalar(v["be"][im, :], v["u"][im, :], -2.0, None, M))

            got = 6
            for n in range(NCA + NCB):
                steps = bcast(lv[:, CH * n:CH * (n + 1)], [ROWS, CH, D])
                after(dve.tensor_tensor(mg[:, :, :], steps, v["dre"][:, :].unsqueeze(1)
                                        .broadcast_to([ROWS, CH, D]), M))
                after(dve.tensor_tensor(th[:, :, :], steps, v["dim"][:, :].unsqueeze(1)
                                        .broadcast_to([ROWS, CH, D]), M))
                reduce_angle(th[:, :, :], kk[:, :, :])
                if n < NCA:
                    cosine_angle(arg[re, :, :], th[re, :, :])
                    after(dve.tensor_copy(arg[im, :, :], th[im, :, :]))
                else:
                    after(dve.tensor_copy(arg[:, :, :], th[:, :, :]))
                    cosine_angle(cz[:, :, :], th[:, :, :])
                dve.sem_inc(ask, 1)
                got += 2 if n < NCA else 3
                dve.wait_ge(ans, got)
                if n < NCA:
                    after(dve.tensor_tensor(q[:, :, :, CH * n:CH * (n + 1)].rearrange("r g j a -> r a j g"),
                                            mg[:, :, :].rearrange("r a (j g) -> r a j g", j=4),
                                            arg[:, :, :].rearrange("r a (j g) -> r a j g", j=4), M))
                else:
                    after(dve.tensor_tensor(cz[:, :, :], cz[:, :, :], v["al"][:, :].unsqueeze(1)
                                            .broadcast_to([ROWS, CH, D]), M))
                    after(dve.tensor_tensor(arg[:, :, :], arg[:, :, :], v["be"][:, :].unsqueeze(1)
                                            .broadcast_to([ROWS, CH, D]), M))
                    after(dve.tensor_tensor(cz[:, :, :], cz[:, :, :], arg[:, :, :], A_))
                    after(dve.tensor_tensor(pz[:, CH * (n - NCA):CH * (n - NCA + 1), :], mg[:, :, :],
                                            cz[:, :, :], M))
            dve.sem_inc(tables_done, 1)
            for k in range(8):
                dve.wait_ge(products, k + 1)
                for j in range(4):
                    rows = slice(32 * j, 32 * j + 32)
                    ins = dve.tensor_copy(kl[rows, :, 8 * k:8 * k + 8],
                                          kp[rows, k, :, LB * j:LB * (j + 1)].rearrange("p g b -> p b g"))
                ins.then_inc(gathered, 1)
            dve.wait_ge(loaded, 16)
            dve.tensor_tensor(kt[0:1, 0, :], kt[0:1, 0, :], drow[:, :], A_).then_inc(row_done, 1)
            dve.wait_ge(spectra, HALF)
            for m in range(HALF):
                kr, ki = kp[:, m, 0:4, :].rearrange("p a b -> p (a b)"), kp[:, m, 4:8, :].rearrange("p a b -> p (a b)")
                dve.tensor_copy(ka[:, m, 0, :], kr)
                dve.tensor_copy(ka[:, m, 1, :], ki)
                dve.tensor_scalar(kb[:, m, 0, :], ki, -1.0, None, M)
                after(dve.tensor_copy(kb[:, m, 1, :], kr))
            first = kp[0:1, 0, 4:8, :].rearrange("p a b -> p (a b)")
            dve.tensor_scalar(ka[0:1, 0, 1, :], first, 0.0, None, M)
            dve.tensor_scalar(kb[0:1, 0, 0, :], first, 0.0, None, M)
            after(dve.tensor_copy(kb[0:1, 0, 1, :], first))

        @block.tensor
        def _(pe):
            pe.wait_ge(tables_done, 1)
            qv = q[:, :, :, :].rearrange("r g j a -> r g (j a)")
            pv = pz[:, :, :].rearrange("r b (j g) -> r g j b", j=4)
            for k in range(8):
                for i in range(8):
                    grp = 8 * k + i
                    mm = pe.matmul(kp[:, k, i, :], qv[:, grp, :], pv[:, grp, :, :], start=True, stop=True)
                mm.then_inc(products, 1)
            pe.wait_ge(row_done, 1)
            pe.wait_ge(mats_in, 2 * 16)
            pe.wait_ge(gathered, 8)
            for m in range(HALF):
                for part in range(2):
                    f = (part * HALF + m) * P
                    for j in range(NJ):
                        mm = pe.matmul(kp[:, m, 4 * part:4 * part + 4, :], fwd[:, j, f:f + P], kt[:, j, :],
                                       start=(j == 0), stop=(j == NJ - 1))
                mm.then_inc(spectra, 1)


def low_rank_stage(nc, w, resid, ident, out):
    TURNS = B
    NFT = FF // P
    with ExitStack() as ctx:
        def sb(name, shape, dt=F32):
            return ctx.enter_context(nc.sbuf_tensor(name, shape, dt))

        def sem(name):
            return ctx.enter_context(nc.semaphore(name))

        norm = Norm(ctx, nc, "f")
        u1 = sb("u1", [P, ND, RANK])
        v1 = sb("f_v1", [RANK, FF])
        b1 = sb("b1", [P, NFT])
        u2 = sb("u2", [P, NFT, RANK])
        v2 = sb("v2", [RANK + 1, D])
        XT = sb("f_XT", [P, ND, S])
        PT = sb("PT", [RANK, S])
        H = sb("H", [P, NFT, S])
        QT = sb("QT", [RANK + 1, S])
        y = sb("f_y", [P, NJ, D])

        xb = ctx.enter_context(nc.psum_tensor("f_xps", [P, 2, BANK], F32))
        hb = ctx.enter_context(nc.psum_tensor("f_hps", [P, 2, BANK], F32))
        rb = ctx.enter_context(nc.psum_tensor("f_r", [P, 2, BANK], F32))
        yb = ctx.enter_context(nc.psum_tensor("f_y_out", [P, 2, BANK], F32))
        x_h = [Handoff(ctx, nc, f"f_x{k}") for k in range(2)]
        h_h = [Handoff(ctx, nc, f"f_h{k}", range(k, NFT, 2)) for k in range(2)]
        r_h = [Handoff(ctx, nc, f"f_r{k}") for k in range(2)]
        y_h = [Handoff(ctx, nc, f"f_yb{k}") for k in range(2)]
        weights_in = sem("f_weights_in")
        ones_done = sem("f_ones_done")
        vec = sem("f_vector_order")
        stored = sem("f_stored")
        block = ctx.enter_context(nc.Block())

        @block.sync
        def _(sp):
            for h in (*x_h, *h_h, *r_h, *y_h):
                h.open(sp)
            sp.sem_inc(stored, 1)
            sp.dma_start(u1[:, :, :], w["U1"].rearrange("(c p) r -> p c r", p=P)).then_inc(weights_in, 16)
            sp.dma_start(v1[:, :], w["V1"]).then_inc(weights_in, 16)
            sp.dma_start(b1[:, :], w["fb1"]).then_inc(weights_in, 16)
            sp.dma_start(u2[:, :, :], w["U2"].rearrange("(c p) r -> p c r", p=P)).then_inc(weights_in, 16)
            sp.dma_start(v2[:, :], w["V2"]).then_inc(weights_in, 16)
            with sp.Fori(0, TURNS) as t:
                for k in range(2):
                    y_h[k].wait_emptied(sp, t)
                sp.dma_start(out[t].rearrange("(j p) d -> p j d", p=P), y[:, :, :]).then_inc(stored, 16)
            sp.wait_ge(stored, TURNS * 16 + 1)

        @block.gpsimd
        def _(pool):
            pool.memset(QT[RANK:RANK + 1, :], 1.0).then_inc(ones_done, 1)

        @block.scalar
        def _(act):
            act.wait_ge(weights_in, 5 * 16)
            with act.Fori(0, TURNS) as t:
                norm.scalar_root(act, t)
                for c in range(ND):
                    x_h[c].wait_full(act, t)
                    act.activation(XT[:, c, :], xb[:, c, :], ACT.Copy).then_inc(x_h[c].free, 1)
                r_h[0].wait_full(act, t)
                act.activation(PT[:, :], rb[0:RANK, 0, :], ACT.Copy).then_inc(r_h[0].free, 1)
                for f in range(NFT):
                    h_h[f % 2].wait_full(act, t, f)
                    act.activation(H[:, f, :], hb[:, f % 2, :], ACT.Gelu_apprx_tanh, bias=b1[:, f:f + 1])\
                       .then_inc(h_h[f % 2].free, 1)
                r_h[1].wait_full(act, t)
                act.activation(QT[0:RANK, :], rb[0:RANK, 1, :], ACT.Copy).then_inc(r_h[1].free, 1)

        @block.vector
        def _(dve):
            with dve.Fori(0, TURNS) as t:
                order = Chain(vec, Norm.DVE_STEPS)
                norm.vector_statistics(dve, t, lambda ins: order(dve, t, ins), resid)
                norm.vector_scale(dve, t, resid)
                dve.wait_ge(stored, t * 16 + 1)
                for k in range(2):
                    y_h[k].wait_full(dve, t)
                    dve.tensor_tensor(y[:, 2 * k:2 * k + 2, :], resid[:, bass.ds(t * NJ + 2 * k, 2), :],
                                      yb[:, k, :].rearrange("p (j d) -> p j d", j=2), ALU.add)\
                        .then_inc(y_h[k].free, 1)
                order.close()

        @block.tensor
        def _(pe):
            pe.wait_ge(weights_in, 5 * 16)
            pe.wait_ge(ones_done, 1)
            with pe.Fori(0, TURNS) as t:
                pe.wait_ge(norm.x_done, t * NJ + NJ)
                for c in range(ND):
                    x_h[c].wait_free(pe, t)
                    transpose_sequence(pe, xb[:, c, :], norm.x, c, ident).then_inc(x_h[c].full, 1)
                for c in range(ND):
                    x_h[c].wait_emptied(pe, t)
                r_h[0].wait_free(pe, t)
                for c in range(ND):
                    mm = pe.matmul(rb[0:RANK, 0, :], u1[:, c, :], XT[:, c, :], start=(c == 0), stop=(c == ND - 1))
                mm.then_inc(r_h[0].full, 1)
                r_h[0].wait_emptied(pe, t)
                for f in range(NFT):
                    h_h[f % 2].wait_free(pe, t, f)
                    pe.matmul(hb[:, f % 2, :], v1[:, f * P:(f + 1) * P], PT[:, :], start=True, stop=True)\
                      .then_inc(h_h[f % 2].full, 1)
                r_h[1].wait_free(pe, t)
                for f in range(NFT):
                    h_h[f % 2].wait_emptied(pe, t, f)
                    mm = pe.matmul(rb[0:RANK, 1, :], u2[:, f, :], H[:, f, :], start=(f == 0), stop=(f == NFT - 1))
                mm.then_inc(r_h[1].full, 1)
                r_h[1].wait_emptied(pe, t)
                for k in range(2):
                    y_h[k].wait_free(pe, t)
                    for j in range(2):
                        mm = pe.matmul(yb[:, k, j * D:(j + 1) * D], QT[:, (2 * k + j) * P:(2 * k + j + 1) * P],
                                       v2[:, :], start=True, stop=True)
                    mm.then_inc(y_h[k].full, 1)


def identity_into(nc, ident):
    with ExitStack() as ctx:
        made = ctx.enter_context(nc.semaphore("ident_made"))
        block = ctx.enter_context(nc.Block())

        @block.gpsimd
        def _(pool):
            pool.memset(ident[:, :], 0.0).then_inc(made, 1)
            pool.wait_ge(made, 1)
            pool.affine_select(out=ident[:, :], in_=ident[:, :], compare_op=ALU.not_equal, fill=1.0,
                               base=0, pattern=[[-1, P]], channel_multiplier=1).then_inc(made, 1)
            pool.wait_ge(made, 2)


def tower(nc, w, out):
    with ExitStack() as ctx:
        resid = ctx.enter_context(nc.sbuf_tensor("resid", [P, NT, D], F32))
        ident = ctx.enter_context(nc.sbuf_tensor("ident", [P, P], F32))
        identity_into(nc, ident)
        attention_stage(nc, w, resid, ident)
        delta_stage(nc, w, resid, ident)
        experts_stage(nc, w, resid, ident)
        convolution_stage(nc, w, resid, ident)
        low_rank_stage(nc, w, resid, ident, out)


def layout(i):
    c = np.ascontiguousarray
    w = {}
    w["x"] = c(i["x"].reshape(B, S, D))
    w["wqkvT"] = c(i["L0_tok_w_qkv"].reshape(NH, 3, HD, D).transpose(3, 1, 0, 2).reshape(D, 3 * D))
    b = i["L0_tok_b_qkv"].reshape(NH, 3, HD).transpose(1, 0, 2).reshape(3, D)
    w["bqk"] = c(b[0:2].reshape(4, P).T)
    w["bv"] = c(b[2:3])
    w["woutT"] = c(i["L0_tok_w_out"].T)
    w["bo"] = c(i["L0_tok_b_out"].reshape(1, D))
    w.update(attention_constants())
    for name in ("Wq", "Wk", "Wv", "Wg", "Wo"):
        w[name] = c(i["L0_attn_" + name])
    w["wab"] = c(np.concatenate([i["L0_attn_Wb"], i["L0_attn_Wa"]], axis=1))
    w["Wfc"], w["Wproj"] = c(i["L0_attn_W_fc"]), c(i["L0_attn_W_proj"])
    w["dtb"], w["alog"], w["onw"] = (c(i["L0_attn_" + n][None]) for n in ("dt_bias", "A_log", "o_norm_w"))
    w.update(delta_constants())
    w["gw"], w["gb"] = c(i["L0_ffn_gate_w"].T), c(i["L0_ffn_gate_b"][None])
    at = np.arange(NE)
    w["before"] = (at[None, :] < at[:, None]).astype(np.float32).reshape(1, NE * NE)
    w1 = np.concatenate([i["L0_ffn_w1"], i["L0_ffn_sw1"][None]])
    w3 = np.concatenate([i["L0_ffn_w3"], i["L0_ffn_sw3"][None]])
    w13 = np.stack([w1, w3], axis=1)
    w["w13"] = c(w13.reshape(NE + 1, 2, ND, P, EH).transpose(0, 3, 1, 2, 4))
    b1 = np.concatenate([i["L0_ffn_b1"], i["L0_ffn_sb1"][None]])
    b3 = np.concatenate([i["L0_ffn_b3"], i["L0_ffn_sb3"][None]])
    b13 = np.zeros((NE + 1, 2, 3 * P), np.float32)
    b13[:, :, :EH] = np.stack([b1, b3], axis=1)
    w["b13"] = c(b13.reshape(NE + 1, 2, 3, P).transpose(3, 0, 1, 2))
    w2 = np.concatenate([i["L0_ffn_w2"], i["L0_ffn_sw2"][None]])
    b2 = np.concatenate([i["L0_ffn_b2"], i["L0_ffn_sb2"][None]])
    w["w2a"] = c(w2[:, :2 * P].reshape(NE + 1, 2, P, D).transpose(0, 2, 1, 3))
    w["w2b"] = c(np.concatenate([w2[:, 2 * P:], b2[:, None]], axis=1))
    w["log_dt"] = c(i["L1_attn_log_dt"][None])
    w["modes"] = c(np.stack([i["L1_attn_log_A_real"].T, i["L1_attn_A_imag"].T,
                             i["L1_attn_C"][:, :, 0].T, i["L1_attn_C"][:, :, 1].T], axis=1))
    w["skip"] = c(i["L1_attn_D"][None])
    w.update(fourier_constants())
    w["U1"], w["V1"], w["U2"] = c(i["L1_ffn_U1"]), c(i["L1_ffn_V1"]), c(i["L1_ffn_U2"])
    w["fb1"] = c(i["L1_ffn_b1"].reshape(FF // P, P).T)
    w["V2"] = c(np.concatenate([i["L1_ffn_V2"], i["L1_ffn_b2"][None]]))
    return w


def fourier_constants():
    l, f = np.arange(S)[:, None], np.arange(S)[None, :]
    angle = 2 * np.pi * (l * f % NF) / NF
    alternating = (-1.0) ** np.arange(S)
    fwd = np.concatenate([np.cos(angle), -np.sin(angle)], axis=1)
    fwd[:, S] = alternating
    weight = np.where(np.arange(S) == 0, 1.0, 2.0)[:, None] / NF
    inv = np.concatenate([weight * np.cos(angle.T), -weight * np.sin(angle.T)])
    inv[S] = alternating / NF
    return {"fwd": fwd.astype(np.float32), "inv": inv.astype(np.float32),
            "lvals": np.concatenate([16 * np.arange(32), np.arange(16)]).astype(np.float32)[None]}


def delta_constants():
    at = np.arange(P)
    level = np.zeros((P, 7, P), np.float32)
    for l in range(7):
        m = 1 << l
        under = (at[:, None] // (2 * m) == at // (2 * m)) & (at[:, None] // m % 2 == 1) & (at // m % 2 == 0)
        level[:, l, :] = under.T if l == 0 else under
    return {
        "upto": (at[:, None] <= at).astype(np.float32),
        "beyond": (at[:, None] > at).astype(np.float32),
        "ones": np.ones((P, P), np.float32),
        "level": level,
        "keep": (np.arange(NT) % NJ != 0).astype(np.float32)[None],
    }


def attention_constants():
    sel = np.zeros((P, 4, 4, P), np.float32)
    for kind, starts in enumerate(((0, 16), (32,), (0, 32), (16,))):
        for start in starts:
            for head in range(2):
                for e in range(HD):
                    for pair in range(4):
                        sel[32 * pair + head * HD + e, pair, kind, 64 * head + start + e] = 1.0
    selm = np.zeros((NH, 2, NH // 2, P), np.float32)
    onerow = np.zeros((P, 1), np.float32)
    for h in range(NH):
        for part in range(2):
            selm[h, part, h // 2, 64 * (h % 2) + 48 + part] = -1.0
            onerow[64 * (h % 2) + 48 + part] = 1.0
    return {"sel": sel, "selm": selm, "onerow": onerow}


def kernel(**inputs):
    from concourse.bacc import Bacc
    from concourse.bass_utils import run_bass_kernel_spmd

    nc = Bacc("TRN2", target_bir_lowering=False, num_devices=1)
    arrays = layout({k: np.asarray(v) for k, v in inputs.items()})
    w = {}
    for name, a in arrays.items():
        w[name] = nc.dram_tensor("in_" + name, a.shape, mybir.dt.from_np(a.dtype), kind="ExternalInput").ap()
    out = nc.dram_tensor("out", (B, S, D), F32, kind="ExternalOutput").ap()
    tower(nc, w, out)
    result = run_bass_kernel_spmd(nc, [{"in_" + k: a for k, a in arrays.items()}], core_ids=[0])
    return result.results[0]["out"]
```

```python
from contextlib import ExitStack

import numpy as np

import concourse.bass as bass
from concourse import mybir

F32 = mybir.dt.float32
F32R = mybir.dt.float32r
ACT = mybir.ActivationFunctionType
ALU = mybir.AluOpType
AXX = mybir.AxisListType.X

P = 128
B = 8
S = 512
D = 256
NJ = S // P
NT = B * NJ
ND = D // P
BANK = 512

NH, HD = 16, 16
GH, DK = 8, 128
GD = GH * DK
FF = 1024
NE, TOPK, EH = 8, 2, 352
RANK = 64
MODES = 32
NF = 2 * S
LN_EPS, RMS_EPS = 1e-5, 1e-6


class Handoff:

    def __init__(self, ctx, nc, name, uses=("x",), depth=1):
        self.depth = depth
        self.full = ctx.enter_context(nc.semaphore(name + "_full"))
        self.free = ctx.enter_context(nc.semaphore(name + "_free"))
        self.at = {u: k for k, u in enumerate(uses)}
        self.n = len(self.at)

    def open(self, eng):
        eng.sem_inc(self.free, self.depth)

    def wait_full(self, eng, turn, use="x"):
        eng.wait_ge(self.full, turn * self.n + (self.at[use] + 1))

    def wait_free(self, eng, turn, use="x"):
        eng.wait_ge(self.free, turn * self.n + (self.at[use] + 1))

    def wait_emptied(self, eng, turn, use="x"):
        eng.wait_ge(self.free, turn * self.n + (self.at[use] + 1 + self.depth))


class Chain:

    def __init__(self, sem, per):
        self.sem, self.per, self.k = sem, per, 0

    def __call__(self, eng, turn, ins):
        self.k += 1
        ins.then_inc(self.sem, 1)
        eng.wait_ge(self.sem, turn * self.per + self.k)

    def close(self):
        assert self.k == self.per, (self.k, self.per)


def bcast(ap, shape):
    while len(ap.shape) < len(shape):
        ap = ap.unsqueeze(len(ap.shape))
    return ap.broadcast_to(shape)


class Norm:

    DVE_STEPS = 4

    def __init__(self, ctx, nc, name):
        def sb(n, shape):
            return ctx.enter_context(nc.sbuf_tensor(f"{name}_{n}", shape, F32))

        self.x = sb("x", [P, NJ, D])
        self.stats, self.both = sb("stats", [P, NJ, 6]), sb("both", [P, NJ, 3])
        self.diff, self.mean, self.var = sb("diff", [P, NJ]), sb("mean", [P, NJ]), sb("var", [P, NJ])
        self.rstd, self.minus_half = sb("rstd", [P, NJ]), sb("minus_half", [P, NJ])
        self.var_done = ctx.enter_context(nc.semaphore(name + "_var_done"))
        self.half_done = ctx.enter_context(nc.semaphore(name + "_half_done"))
        self.rstd_done = ctx.enter_context(nc.semaphore(name + "_rstd_done"))
        self.x_done = ctx.enter_context(nc.semaphore(name + "_x_done"))

    def vector_statistics(self, dve, turn, after, resid):
        for j in range(NJ):
            ins = dve.bn_stats(self.stats[:, j, :], resid[:, bass.ds(turn * NJ + j, 1), :].rearrange("p a d -> p (a d)"))
        after(ins)
        after(dve.tensor_reduce(self.both[:, :, :], self.stats[:, :, :].rearrange("p j (a b) -> p j b a", a=2),
                                AXX, ALU.add))
        dve.tensor_scalar(self.mean[:, :], self.both[:, :, 1], 0.5, None, ALU.mult)
        after(dve.tensor_tensor(self.diff[:, :], self.stats[:, :, 1], self.stats[:, :, 4], ALU.subtract))
        dve.tensor_scalar(self.var[:, :], self.both[:, :, 2], 1.0 / D, LN_EPS, ALU.mult, ALU.add)
        after(dve.tensor_tensor(self.diff[:, :], self.diff[:, :], self.diff[:, :], ALU.mult))
        dve.scalar_tensor_tensor(out=self.var[:, :], in0=self.diff[:, :], scalar=0.25, in1=self.var[:, :],
                                 op0=ALU.mult, op1=ALU.add).then_inc(self.var_done, 1)

    def pool_constants(self, pool):
        pool.memset(self.minus_half[:, :], -0.5).then_inc(self.half_done, 1)
        pool.wait_ge(self.half_done, 1)

    def pool_root(self, pool, turn):
        pool.wait_ge(self.var_done, turn + 1)
        pool.tensor_tensor(self.rstd[:, :], self.var[:, :], self.minus_half[:, :], ALU.pow).then_inc(self.rstd_done, 1)

    def vector_scale(self, dve, turn, resid):
        dve.wait_ge(self.rstd_done, turn + 1)
        for j in range(NJ):
            dve.tensor_scalar(self.x[:, j, :], resid[:, bass.ds(turn * NJ + j, 1), :].rearrange("p a d -> p (a d)"),
                              self.mean[:, j:j + 1], self.rstd[:, j:j + 1], ALU.subtract, ALU.mult)\
                .then_inc(self.x_done, 1)


def transpose_sequence(pe, out, x, c, ident):
    for j in range(NJ):
        mm = pe.transpose(out[:, j * P:(j + 1) * P], x[:, j, c * P:(c + 1) * P], ident[:, :])
    return mm


def ahead(eng, count, first, body):
    if first is not None:
        first(0)
    with eng.Fori(0, count - 1) as t:
        body(t, t + 1)
    body(count - 1, None)


def attention_stage(nc, w, resid, ident):
    TURNS = B
    PAIRS = NH // 2
    VW = HD + 1
    with ExitStack() as ctx:
        def sb(name, shape, dt=F32):
            return ctx.enter_context(nc.sbuf_tensor(name, shape, dt))

        def sem(name):
            return ctx.enter_context(nc.semaphore(name))

        wqkv = sb("wqkv", [P, ND, 3 * D])
        wout = sb("wout", [P, ND, D])
        bqk = sb("bqk", [P, 4])
        bv = sb("bv", [P, D])
        bo = sb("bo", [P, D])
        sel32 = sb("sel32", [P, 4, 4, P])
        sel = sb("sel", [P, 4, 4, P], F32R)
        selm32 = sb("selm32", [NH, 2, PAIRS, P])
        selm = sb("selm", [NH, 2, PAIRS, P], F32R)
        onerow = sb("onerow", [P, 1])

        x_in = sb("x_in", [P, NJ, D])
        xT = sb("xT", [P, ND, S])
        qk32 = sb("qk32", [P, 4, S])
        qk_hi = sb("qk_hi", [P, 4, S], F32R)
        qk_lo = sb("qk_lo", [P, 4, S], F32R)
        v1 = sb("v1", [P, NJ, NH, VW])
        qstack = sb("qstack", [P, PAIRS, S], F32R)
        kstack = sb("kstack", [P, PAIRS, S], F32R)
        maxima = sb("maxima", [P, NJ, NH])
        max_hi = sb("max_hi", [NH, S], F32R)
        max_lo = sb("max_lo", [NH, S], F32R)
        probs = sb("probs", [P, 2, NJ, S])
        rsum = sb("rsum", [P, 2, NJ])
        vals = sb("vals", [P, NJ, D])
        valsT = sb("valsT", [P, ND, S])

        scores = ctx.enter_context(nc.psum_tensor("scores", [P, 2, 2, BANK], F32))
        heads_out = ctx.enter_context(nc.psum_tensor("heads_out", [P, 2, BANK], F32))
        work = ctx.enter_context(nc.psum_tensor("work", [P, 2, BANK], F32))

        weights_in = sem("a_weights_in")
        consts_done = sem("a_consts_done")
        x_loaded = sem("x_loaded")
        x_used = sem("x_used")
        qk_hi_done = sem("qk_hi_done")
        qk_lo_done = sem("qk_lo_done")
        own = sem("a_vector_order")
        even = ["xT0", "qk0", "qk2", "v0"] + [f"k{p}" for p in range(PAIRS)] + ["max"] + \
               [f"m{p}" for p in range(1, PAIRS, 2)] + ["vT0", "out0"]
        odd = ["xT1", "qk1", "qk3", "v1"] + [f"q{p}" for p in range(PAIRS)] + \
              [f"m{p}" for p in range(0, PAIRS, 2)] + ["vT1", "out1"]
        bank = [Handoff(ctx, nc, "work0", even), Handoff(ctx, nc, "work1", odd)]
        units = [("s", h, u) for h in range(NH) for u in range(2)] + \
                [("t", h, u) for h in range(NH) for u in range(2)]
        score = [Handoff(ctx, nc, f"score{k}", units[k::2]) for k in range(2)]
        head = [Handoff(ctx, nc, f"head{k}", range(k, NH, 2)) for k in range(2)]

        block = ctx.enter_context(nc.Block())

        @block.sync
        def _(sp):
            for h in (*bank, *score, *head):
                h.open(sp)
            sp.sem_inc(x_used, 1)
            sp.dma_start(wqkv[:, :, :], w["wqkvT"].rearrange("(c p) n -> p c n", p=P)).then_inc(weights_in, 16)
            sp.dma_start(sel32[:, :, :, :], w["sel"]).then_inc(weights_in, 16)
            sp.dma_start(bqk[:, :], w["bqk"]).then_inc(weights_in, 16)
            sp.dma_start(bv[:, :], w["bv"].partition_broadcast(P)).then_inc(weights_in, 16)
            sp.dma_start(onerow[:, :], w["onerow"]).then_inc(weights_in, 16)
            sp.dma_start(selm32[:, :, :, :], w["selm"]).then_inc(weights_in, 16)
            sp.dma_start(wout[:, :, :], w["woutT"].rearrange("(c p) n -> p c n", p=P)).then_inc(weights_in, 16)
            sp.dma_start(bo[:, :], w["bo"].partition_broadcast(P)).then_inc(weights_in, 16)
            with sp.Fori(0, TURNS) as b:
                sp.wait_ge(x_used, b + 1)
                sp.dma_start(x_in[:, :, :], w["x"][b].rearrange("(j p) d -> p j d", p=P)).then_inc(x_loaded, 16)

        @block.gpsimd
        def _(pool):
            pool.memset(v1[:, :, :, HD:VW], 1.0).then_inc(consts_done, 1)
            pool.wait_ge(weights_in, 8 * 16)
            pool.tensor_copy(sel[:, :, :, :], sel32[:, :, :, :]).then_inc(consts_done, 1)
            pool.tensor_copy(selm[:, :, :, :], selm32[:, :, :, :]).then_inc(consts_done, 1)

        @block.scalar
        def _(act):
            act.wait_ge(weights_in, 8 * 16)
            with act.Fori(0, TURNS) as b:
                for c in range(ND):
                    bank[c].wait_full(act, b, f"xT{c}")
                    act.activation(xT[:, c, :], work[:, c, :], ACT.Copy).then_inc(bank[c].free, 1)
                for m in range(4):
                    bank[m % 2].wait_emptied(act, b, f"qk{m}")
                    act.activation(qk_hi[:, m, :], qk32[:, m, :], ACT.Copy).then_inc(qk_hi_done, 1)
                for p in range(PAIRS):
                    bank[0].wait_full(act, b, f"k{p}")
                    act.activation(kstack[:, p, :], work[:, 0, :], ACT.Identity, bias=onerow[:, 0:1])\
                       .then_inc(bank[0].free, 1)
                for p in range(1, PAIRS, 2):
                    bank[0].wait_full(act, b, f"m{p}")
                    act.activation(qstack[:, p, :], work[:, 0, :], ACT.Copy).then_inc(bank[0].free, 1)
                for h in range(NH):
                    for u in range(2):
                        score[u].wait_full(act, b, ("t", h, u))
                        if u == 0:
                            if h >= 2:
                                head[h % 2].wait_full(act, b, h - 2)
                        act.activation(probs[:, h % 2, 2 * u:2 * u + 2, :], scores[:, u, :, :], ACT.Exp)\
                           .then_inc(score[u].free, 1)
                for c in range(ND):
                    bank[c].wait_full(act, b, f"vT{c}")
                    act.activation(valsT[:, c, :], work[:, c, :], ACT.Copy).then_inc(bank[c].free, 1)

        @block.vector
        def _(dve):
            per = 1 + NH
            dve.wait_ge(weights_in, 8 * 16)
            dve.wait_ge(consts_done, 3)
            with dve.Fori(0, TURNS) as b:
                after = Chain(own, per)
                for m in range(4):
                    k = m % 2
                    bank[k].wait_full(dve, b, f"qk{m}")
                    dve.tensor_scalar(qk32[:, m, :], work[:, k, :], bqk[:, m:m + 1], 0.25 if m < 2 else 1.0,
                                      ALU.add, ALU.mult).then_inc(bank[k].free, 1)
                    dve.wait_ge(qk_hi_done, b * 4 + (m + 1))
                    dve.tensor_tensor(qk_lo[:, m, :], qk32[:, m, :], qk_hi[:, m, :].bitcast(F32), ALU.subtract)\
                       .then_inc(qk_lo_done, 1)
                for c in range(2):
                    bank[c].wait_full(dve, b, f"v{c}")
                    dve.tensor_tensor(v1[:, 2 * c:2 * c + 2, :, 0:HD],
                                      work[:, c, :].rearrange("p (j h e) -> p j h e", j=2, h=NH),
                                      bv[:, :].rearrange("p (h e) -> p h e", h=NH).unsqueeze(1)
                                      .broadcast_to([P, 2, NH, HD]), ALU.add).then_inc(bank[c].free, 1)
                for p in range(PAIRS):
                    bank[1].wait_full(dve, b, f"q{p}")
                    dve.tensor_copy(qstack[:, p, :], work[:, 1, :]).then_inc(bank[1].free, 1)
                for h in range(NH):
                    for u in range(2):
                        score[u].wait_full(dve, b, ("s", h, u))
                        dve.tensor_reduce(maxima[:, 2 * u:2 * u + 2, h], scores[:, u, :, :], AXX, ALU.max)\
                           .then_inc(score[u].free, 1)
                bank[0].wait_full(dve, b, "max")
                after(dve, b, dve.tensor_copy(max_hi[:, :], work[0:NH, 0, :]))
                dve.tensor_tensor(max_lo[:, :], work[0:NH, 0, :], max_hi[:, :].bitcast(F32), ALU.subtract)\
                   .then_inc(bank[0].free, 1)
                for p in range(0, PAIRS, 2):
                    bank[1].wait_full(dve, b, f"m{p}")
                    dve.tensor_copy(qstack[:, p, :], work[:, 1, :]).then_inc(bank[1].free, 1)
                for h in range(NH):
                    k = h % 2
                    head[k].wait_full(dve, b, h)
                    o = heads_out[:, k, 0:NJ * VW].rearrange("p (j e) -> p j e", j=NJ)
                    after(dve, b, dve.reciprocal(rsum[:, k, :], o[:, :, HD]))
                    dve.tensor_tensor(vals[:, :, h * HD:(h + 1) * HD], o[:, :, 0:HD],
                                      bcast(rsum[:, k, :], [P, NJ, HD]), ALU.mult).then_inc(head[k].free, 1)
                for c in range(2):
                    bank[c].wait_full(dve, b, f"out{c}")
                    dve.tensor_tensor(resid[:, bass.ds(b * NJ + 2 * c, 2), :],
                                      work[:, c, :].rearrange("p (j d) -> p j d", j=2),
                                      bo[:, :].unsqueeze(1).broadcast_to([P, 2, D]), ALU.add)\
                       .then_inc(bank[c].free, 1)
                after.close()

        @block.tensor
        def _(pe):
            def select(out, kind, part, tile, c, start, stop):
                return pe.matmul(out, sel[:, c, kind, :], part[:, tile, :], start=start, stop=stop)

            def values(b, h):
                k = h % 2
                for u in range(2):
                    score[u].wait_emptied(pe, b, ("t", h, u))
                head[k].wait_free(pe, b, h)
                for j in range(NJ):
                    for t in range(NJ):
                        mm = pe.matmul(heads_out[:, k, j * VW:(j + 1) * VW], probs[:, k, t, j * P:(j + 1) * P],
                                       v1[:, t, h, :], start=(t == 0), stop=(t == NJ - 1))
                mm.then_inc(head[k].full, 1)

            pe.wait_ge(weights_in, 8 * 16)
            pe.wait_ge(consts_done, 3)
            with pe.Fori(0, TURNS) as b:
                pe.wait_ge(x_loaded, b * 16 + 16)
                for c in range(ND):
                    bank[c].wait_free(pe, b, f"xT{c}")
                    for j in range(NJ):
                        mm = pe.transpose(work[:, c, j * P:(j + 1) * P], x_in[:, j, c * P:(c + 1) * P], ident[:, :])
                    mm.then_inc(bank[c].full, 1)
                pe.wait_ge(x_loaded, b * 16 + 16)
                for c in range(ND):
                    bank[c].wait_emptied(pe, b, f"xT{c}")
                pe.sem_inc(x_used, 1)
                for m in range(4):
                    k = m % 2
                    bank[k].wait_free(pe, b, f"qk{m}")
                    for c in range(ND):
                        mm = pe.matmul(work[:, k, :], wqkv[:, c, m * P:(m + 1) * P], xT[:, c, :],
                                       start=(c == 0), stop=(c == ND - 1))
                    mm.then_inc(bank[k].full, 1)
                for k in range(2):
                    bank[k].wait_free(pe, b, f"v{k}")
                    for j in range(2):
                        for c in range(ND):
                            mm = pe.matmul(work[:, k, j * D:(j + 1) * D],
                                           xT[:, c, (2 * k + j) * P:(2 * k + j + 1) * P], wqkv[:, c, 2 * D:3 * D],
                                           start=(c == 0), stop=(c == ND - 1))
                    mm.then_inc(bank[k].full, 1)
                for p in range(PAIRS):
                    m, c = p // 4, p % 4
                    pe.wait_ge(qk_lo_done, b * 4 + (m + 3))
                    for k, kind, name in ((0, 2, "k"), (1, 0, "q")):
                        bank[k].wait_free(pe, b, f"{name}{p}")
                        tile = m + 2 if name == "k" else m
                        select(work[:, k, :], kind, qk_hi, tile, c, True, False)
                        select(work[:, k, :], kind + 1, qk_lo, tile, c, False, True).then_inc(bank[k].full, 1)
                for h in range(NH):
                    p, r = h // 2, 64 * (h % 2)
                    bank[0].wait_emptied(pe, b, f"k{p}")
                    bank[1].wait_emptied(pe, b, f"q{p}")
                    for u in range(2):
                        score[u].wait_free(pe, b, ("s", h, u))
                        for j in range(2):
                            t = 2 * u + j
                            mm = pe.matmul(scores[:, u, j, :], qstack[r:r + 64, p, t * P:(t + 1) * P],
                                           kstack[r:r + 64, p, :], start=True, stop=True)
                        mm.then_inc(score[u].full, 1)
                for u in range(2):
                    score[u].wait_emptied(pe, b, ("s", NH - 1, u))
                bank[0].wait_free(pe, b, "max")
                for j in range(NJ):
                    mm = pe.transpose(work[0:NH, 0, j * P:(j + 1) * P], maxima[:, j, :], ident[:, :])
                mm.then_inc(bank[0].full, 1)
                bank[0].wait_emptied(pe, b, "max")
                for p in range(PAIRS):
                    m, c, k = p // 4, p % 4, (p + 1) % 2
                    bank[k].wait_free(pe, b, f"m{p}")
                    select(work[:, k, :], 0, qk_hi, m, c, True, False)
                    select(work[:, k, :], 1, qk_lo, m, c, False, False)
                    pe.matmul(work[:, k, :], selm[:, 0, p, :], max_hi[:, :], start=False, stop=False)
                    pe.matmul(work[:, k, :], selm[:, 1, p, :], max_lo[:, :], start=False, stop=True)\
                      .then_inc(bank[k].full, 1)
                for h in range(NH):
                    p, r = h // 2, 64 * (h % 2)
                    bank[(p + 1) % 2].wait_emptied(pe, b, f"m{p}")
                    for u in range(2):
                        score[u].wait_free(pe, b, ("t", h, u))
                        for j in range(2):
                            t = 2 * u + j
                            mm = pe.matmul(scores[:, u, j, :], kstack[r:r + 64, p, t * P:(t + 1) * P],
                                           qstack[r:r + 64, p, :], start=True, stop=True)
                        mm.then_inc(score[u].full, 1)
                    if h > 0:
                        values(b, h - 1)
                values(b, NH - 1)
                for k in range(2):
                    head[k].wait_emptied(pe, b, NH - 2 + k)
                for c in range(ND):
                    bank[c].wait_free(pe, b, f"vT{c}")
                    for j in range(NJ):
                        mm = pe.transpose(work[:, c, j * P:(j + 1) * P], vals[:, j, c * P:(c + 1) * P], ident[:, :])
                    mm.then_inc(bank[c].full, 1)
                for c in range(ND):
                    bank[c].wait_emptied(pe, b, f"vT{c}")
                for k in range(2):
                    bank[k].wait_free(pe, b, f"out{k}")
                    for j in range(2):
                        for c in range(ND):
                            mm = pe.matmul(work[:, k, j * D:(j + 1) * D],
                                           valsT[:, c, (2 * k + j) * P:(2 * k + j + 1) * P], wout[:, c, :],
                                           start=(c == 0), stop=(c == ND - 1))
                    mm.then_inc(bank[k].full, 1)


def delta_stage(nc, w, resid, ident):
    TURNS = NT
    LEVELS = 7
    HG = 4
    G = GH // HG
    HW = HG * P
    with ExitStack() as ctx:
        def sb(name, shape, dt=F32):
            return ctx.enter_context(nc.sbuf_tensor(name, shape, dt))

        def sem(name):
            return ctx.enter_context(nc.semaphore(name))

        wq4 = sb("wq4", [P, ND, 4, GD])
        wab = sb("wab", [P, ND, 2 * GH])
        wo = sb("wo", [P, GH, D])
        wfc = sb("wfc", [P, ND, FF])
        wproj = sb("wproj", [P, FF // P, D])
        dtb = sb("dtb", [P, GH])
        alog = sb("alog", [P, GH])
        expa = sb("expa", [P, GH])
        onw = sb("onw", [P, DK])
        upto = sb("upto", [P, P])
        beyond = sb("beyond", [P, P])
        ones = sb("ones", [P, P])
        level = sb("level", [P, LEVELS, P])
        keep = sb("keep", [P, NT])

        stats = sb("stats", [P, 6])
        both = sb("both", [P, 3])
        mv = sb("mv", [P, 2])
        var = sb("var", [P, 4])
        rs = sb("rs", [P, 4])
        minus_half = sb("minus_half", [P, 2, GH])
        Xn = sb("Xn", [P, D])
        X = sb("X", [P, D])
        Rn = sb("Rn", [P, D])
        RT = sb("RT", [P, ND, P])
        M = sb("M", [P, D])
        MT = sb("MT", [P, ND, P])
        qkvg = sb("qkvg", [P, 4, GH, DK])
        ab = sb("ab", [P, 2 * GH])
        ex = sb("ex", [P, 2 * GH])
        t1 = sb("t1", [P, GH])
        t2 = sb("t2", [P, GH])
        t3 = sb("t3", [P, GH])
        g = sb("g", [P, GH])
        beta = sb("beta", [P, GH])
        eg = sb("eg", [P, 3, GH])
        egk = sb("egk", [P, GH])
        egc = sb("egc", [P, GH])
        nbe = sb("nbe", [P, GH])
        norm = sb("norm", [P, 2, GH])
        rnorm = sb("rnorm", [P, 2, GH])
        gu = sb("gu", [P, GH, P])
        E = sb("E", [P, GH, P])
        nat = sb("nat", [P, 7, GH, DK])
        tra = sb("tra", [P, 5, GH, P])
        sq = tra[:, 0:2]
        sqo = tra[:, 3]
        mp = sb("mp", [P, GH, 2, P])
        T = sb("T", [P, GH, P])
        Y = sb("Y", [P, GH, P])
        Xl = sb("Xl", [P, GH, P])
        R = sb("R", [P, GH, DK])
        U = E
        O = sb("O", [P, GH, DK])
        St = sb("St", [P, GH, DK])
        og = T
        osum = sb("osum", [P, GH])
        ro = sb("ro", [P, GH])
        ogT = Xl
        X2 = sb("X2", [P, D])
        hid, hT = gu, R
        y = sb("y", [P, D])

        front = ctx.enter_context(nc.psum_tensor("g_front", [P, 2, BANK], F32))
        stateb = ctx.enter_context(nc.psum_tensor("g_state", [P, 2, BANK], F32))
        tri = ctx.enter_context(nc.psum_tensor("g_tri", [P, 4, BANK], F32))

        weights_in = sem("g_weights_in")
        vec_front = sem("g_vector_order_front")
        vec = sem("g_vector_order")
        expa_done = sem("g_expa_done")
        cleared = sem("g_cleared")
        half_done = sem("g_half_done")
        root_f = Handoff(ctx, nc, "g_root_front", ["ln", "rms", "qk"], depth=0)
        root = Handoff(ctx, nc, "g_root", ["o", "rms2"], depth=0)
        gate = Handoff(ctx, nc, "g_gate", depth=0)
        fb = [Handoff(ctx, nc, f"g_front{f}", [("RT", "ab")[f]] + [("proj", n, f) for n in range(4)])
              for f in range(2)]
        place = {}
        tri_uses = [[], [], [], []]

        def uses(bank, *names):
            for name in names:
                place[name] = bank
                tri_uses[bank].append(name)

        TRANSPOSED = (0, 3, 1, 2, 4)
        for k in range(G):
            uses(G + k, ("decay", k))
        for i, n in enumerate(TRANSPOSED):
            for k in range(G):
                uses(G * (i % 2) + k, ("tra", n, k))
        for i in range(4):
            uses((i + G) % 4, ("mp", i))
        for k in range(G):
            uses(k, ("t", 0, k))
            for l in range(1, LEVELS):
                uses(k, ("a", l, k))
                uses(G + k, ("b", l, k))
                if l < LEVELS - 1:
                    uses(k, ("t", l, k))
            uses(k, ("ogT", k))
        uses(2, ("mT",))
        uses(3, ("hid", 0))
        uses(0, ("hid", 1))
        tb = [Handoff(ctx, nc, f"g_tri{k}", tri_uses[k]) for k in range(4)]
        sbk = [Handoff(ctx, nc, f"g_state{k}", (["cum"] if k == 0 else []) + ["ks", "u", "o", "s"] +
                       (["wo"] if k == 0 else ["down"])) for k in range(2)]
        squares = sem("g_squares")
        squares_o = sem("g_squares_o")
        pool_gu = sem("g_pool_gu")
        pool_gate = sem("g_pool_gate")
        pool_E = sem("g_pool_E")
        pool_nat = sem("g_pool_nat")
        pool_og = sem("g_pool_og")
        dve_beta = sem("g_beta_done")
        dve_g = sem("g_g_done")
        dve_scal = sem("g_scalars_done")
        dve_nat = sem("g_vector_nat")
        Y_done = [sem(f"g_Y{k}") for k in range(G)]
        og_done = sem("g_og_done")
        rn_done = sem("g_rn_done")
        m_done = sem("g_m_done")
        hid_relu = sem("g_hid_relu")

        block = ctx.enter_context(nc.Block())

        def heads(ap, k):
            return ap[:, HG * k:HG * (k + 1), :]

        def split(bank):
            return bank.rearrange("p (h e) -> p h e", h=HG)

        def grp(ap, k):
            return split(ap[:, k, :])

        @block.sync
        def _(sp):
            for h in (*fb, *sbk, *tb):
                h.open(sp)
            for n, name in enumerate(("Wq", "Wk", "Wv", "Wg")):
                sp.dma_start(wq4[:, :, n, :], w[name].rearrange("(c p) n -> p c n", p=P)).then_inc(weights_in, 16)
            sp.dma_start(wab[:, :, :], w["wab"].rearrange("(c p) n -> p c n", p=P)).then_inc(weights_in, 16)
            sp.dma_start(wo[:, :, :], w["Wo"].rearrange("(c p) n -> p c n", p=P)).then_inc(weights_in, 16)
            sp.dma_start(wfc[:, :, :], w["Wfc"].rearrange("(c p) n -> p c n", p=P)).then_inc(weights_in, 16)
            sp.dma_start(wproj[:, :, :], w["Wproj"].rearrange("(c p) n -> p c n", p=P)).then_inc(weights_in, 16)
            sp.dma_start(dtb[:, :], w["dtb"].partition_broadcast(P)).then_inc(weights_in, 16)
            sp.dma_start(alog[:, :], w["alog"].partition_broadcast(P)).then_inc(weights_in, 16)
            sp.dma_start(onw[:, :], w["onw"].partition_broadcast(P)).then_inc(weights_in, 16)
            sp.dma_start(upto[:, :], w["upto"]).then_inc(weights_in, 16)
            sp.dma_start(beyond[:, :], w["beyond"]).then_inc(weights_in, 16)
            sp.dma_start(level[:, :, :], w["level"]).then_inc(weights_in, 16)
            sp.dma_start(keep[:, :], w["keep"].partition_broadcast(P)).then_inc(weights_in, 16)
            sp.dma_start(ones[:, :], w["ones"]).then_inc(weights_in, 16)
        IN = 16 * 16

        def bank_of(eng, t, use, wait):
            k = place[use]
            (tb[k].wait_free if wait == "free" else tb[k].wait_full)(eng, t, use)
            return tri[:, k, :], tb[k]

        def emptied(eng, t, use):
            tb[place[use]].wait_emptied(eng, t, use)

        @block.gpsimd
        def _(pool):
            def inv_root(hand, turn, use, out, x, half):
                hand.wait_full(pool, turn, use)
                pool.tensor_tensor(out, x, half, ALU.pow).then_inc(hand.free, 1)

            def roots_ln(u):
                inv_root(root_f, u, "ln", rs[:, 0:1], var[:, 0:1], minus_half[:, 0, 0:1])
                inv_root(root_f, u, "rms", rs[:, 1:2], var[:, 1:2], minus_half[:, 0, 0:1])

            def front_rest(u):
                pool.wait_ge(dve_g, u + 1)
                pool.tensor_tensor(gu[:, :, :], upto[:, :].unsqueeze(1).broadcast_to([P, GH, P]),
                                   bcast(g[:, :], [P, GH, P]), ALU.mult).then_inc(pool_gu, 1)
                inv_root(root_f, u, "qk", rnorm[:, :, :], norm[:, :, :], minus_half[:, :, :])
                for f in range(2):
                    fb[f].wait_emptied(pool, u, ("proj", 3, f))
                pool.tensor_tensor(qkvg[:, 3, :, :], qkvg[:, 3, :, :],
                                   onw[:, :].unsqueeze(1).broadcast_to([P, GH, DK]), ALU.mult)\
                    .then_inc(pool_gate, 1)

            def first(u):
                roots_ln(u)
                front_rest(u)

            def body(t, u):
                for k in range(G):
                    emptied(pool, t, ("decay", k))
                pool.tensor_tensor(E[:, :, :], E[:, :, :], upto[:, :].unsqueeze(1).broadcast_to([P, GH, P]),
                                   ALU.mult).then_inc(pool_E, 1)
                pool.wait_ge(dve_scal, t + 1)
                pool.wait_ge(dve_nat, t * 5 + 1)
                pool.tensor_tensor(nat[:, 5, :, :], nat[:, 0, :, :], bcast(eg[:, 1, :], [P, GH, DK]),
                                   ALU.mult).then_inc(pool_nat, 1)
                pool.tensor_tensor(nat[:, 6, :, :], qkvg[:, 2, :, :], bcast(beta[:, :], [P, GH, DK]),
                                   ALU.mult).then_inc(pool_nat, 1)
                if u is not None:
                    roots_ln(u)
                for k in range(G):
                    sbk[k].wait_emptied(pool, t, "o")
                pool.wait_ge(pool_gate, t + 1)
                pool.tensor_tensor(og[:, :, :], O[:, :, :], qkvg[:, 3, :, :], ALU.mult).then_inc(pool_og, 1)
                inv_root(root, t, "o", ro[:, :], osum[:, :], minus_half[:, 0, :])
                inv_root(root, t, "rms2", rs[:, 2:3], var[:, 2:3], minus_half[:, 0, 0:1])
                if u is not None:
                    for k in range(2):
                        emptied(pool, t, ("hid", k))
                    front_rest(u)

            pool.wait_ge(weights_in, IN)
            pool.memset(minus_half[:, :, :], -0.5).then_inc(half_done, 1)
            pool.wait_ge(half_done, 1)
            ahead(pool, TURNS, first, body)

        @block.scalar
        def _(act):
            def project(u, n, f):
                fb[f].wait_full(act, u, ("proj", n, f))
                act.activation(qkvg[:, n, HG * f:HG * (f + 1), :], grp(front, f), ACT.Silu).then_inc(fb[f].free, 1)

            def square(u, n):
                for f in range(2):
                    fb[f].wait_emptied(act, u, ("proj", n, f))
                for f in range(2):
                    ins = act.activation(heads(sq[:, n], f), heads(qkvg[:, n], f), ACT.Square)
                ins.then_inc(squares, 1)

            def front_start(u):
                fb[0].wait_full(act, u, "RT")
                act.activation(RT[:, :, :], front[:, 0, 0:D].rearrange("p (c t) -> p c t", c=ND), ACT.Copy)\
                   .then_inc(fb[0].free, 1)
                act.preload_act_table_set("exp_and_others")
                gate.wait_full(act, u)
                act.activation(ex[:, :], ab[:, :], ACT.Exp).then_inc(gate.free, 1)
                act.preload_act_table_set("silu_and_others")
                project(u, 0, 0)
                project(u, 0, 1)
                project(u, 1, 0)

            def front_middle(u):
                square(u, 0)
                project(u, 1, 1)
                project(u, 2, 0)

            def front_late(u):
                square(u, 1)
                project(u, 2, 1)

            def front_gates(u):
                for f in range(2):
                    project(u, 3, f)

            def first(u):
                front_start(u)
                front_middle(u)
                front_late(u)
                front_gates(u)

            def body(t, u):
                act.preload_act_table_set("exp_and_others")
                sbk[0].wait_full(act, t, "cum")
                act.activation(eg[:, :, :], stateb[:, 0, 0:3 * GH].rearrange("p (a h) -> p a h", a=3), ACT.Exp)\
                   .then_inc(sbk[0].free, 1)
                for k in range(G):
                    bank, h = bank_of(act, t, ("decay", k), "full")
                    act.activation(heads(E, k), split(bank), ACT.Exp).then_inc(h.free, 1)
                for n in TRANSPOSED:
                    bank, h = bank_of(act, t, ("tra", n, 0), "full")
                    act.activation(heads(tra[:, n], 0), split(bank), ACT.Copy).then_inc(h.free, 1)
                for l in range(LEVELS - 1):
                    for k in range(G):
                        bank, h = bank_of(act, t, ("t", l, k), "full")
                        act.activation(heads(T, k), split(bank), ACT.Copy).then_inc(h.free, 1)
                for k in range(G):
                    sbk[k].wait_full(act, t, "u")
                    act.activation(heads(U, k), grp(stateb, k), ACT.Copy).then_inc(sbk[k].free, 1)
                for k in range(G):
                    sbk[k].wait_full(act, t, "o")
                    act.activation(heads(sqo, k), grp(stateb, k), ACT.Square).then_inc(squares_o, 1)
                    act.activation(heads(O, k), grp(stateb, k), ACT.Copy).then_inc(sbk[k].free, 1)
                if u is not None:
                    front_start(u)
                for k in range(G):
                    bank, h = bank_of(act, t, ("ogT", k), "full")
                    act.activation(heads(ogT, k), split(bank), ACT.Copy).then_inc(h.free, 1)
                if u is not None:
                    front_middle(u)
                bank, h = bank_of(act, t, ("mT",), "full")
                act.activation(MT[:, :, :], bank[:, 0:D].rearrange("p (c t) -> p c t", c=ND), ACT.Copy)\
                   .then_inc(h.free, 1)
                for k in range(2):
                    bank, h = bank_of(act, t, ("hid", k), "full")
                    act.activation(heads(hid, k), split(bank), ACT.Relu).then_inc(hid_relu, 1)
                if u is not None:
                    front_late(u)
                    act.wait_ge(pool_og, u)
                    front_gates(u)

            act.wait_ge(weights_in, IN)
            act.activation(expa[:, :], alog[:, :], ACT.Exp).then_inc(expa_done, 1)
            ahead(act, TURNS, first, body)

        @block.vector
        def _(dve):
            def mean_square(after, turn, x, col, hand, use, out, done):
                after(dve, turn, dve.tensor_tensor_reduce(out=y[:, :], in0=x, in1=x, scale=1.0 / D, scalar=0.0,
                                                          op0=ALU.mult, op1=ALU.add, accum_out=var[:, 3:4]))
                dve.tensor_scalar(var[:, col:col + 1], var[:, 3:4], RMS_EPS, None, ALU.add)\
                   .then_inc(hand.full, 1)
                hand.wait_emptied(dve, turn, use)
                dve.tensor_scalar(out, x, rs[:, col:col + 1], None, ALU.mult).then_inc(done, 1)

            def row(t):
                return resid[:, bass.ds(t, 1), :].rearrange("p a d -> p (a d)")

            def layer_norm(u, order):
                def after(ins):
                    order(dve, u, ins)

                after(dve.bn_stats(stats[:, :], row(u)))
                after(dve.tensor_reduce(both[:, :], stats[:, :].rearrange("p (a b) -> p b a", a=2), AXX, ALU.add))
                after(dve.tensor_tensor(mv[:, 1:2], stats[:, 1:2], stats[:, 4:5], ALU.subtract))
                after(dve.tensor_tensor(mv[:, 1:2], mv[:, 1:2], mv[:, 1:2], ALU.mult))
                after(dve.tensor_scalar(var[:, 3:4], both[:, 2:3], 1.0 / D, LN_EPS, ALU.mult, ALU.add))
                dve.tensor_scalar(mv[:, 0:1], both[:, 1:2], 0.5, None, ALU.mult)
                dve.scalar_tensor_tensor(out=var[:, 0:1], in0=mv[:, 1:2], scalar=0.25, in1=var[:, 3:4],
                                         op0=ALU.mult, op1=ALU.add).then_inc(root_f.full, 1)
                root_f.wait_emptied(dve, u, "ln")
                after(dve.tensor_scalar(Xn[:, :], row(u), mv[:, 0:1], rs[:, 0:1], ALU.subtract, ALU.mult))
                mean_square(order, u, Xn[:, :], 1, root_f, "rms", Rn[:, :], rn_done)

            def gate_inputs(u, order):
                fb[1].wait_full(dve, u, "ab")
                order(dve, u, dve.tensor_tensor(t1[:, :], front[:, 1, GH:2 * GH], dtb[:, :], ALU.add))
                dve.tensor_scalar(ab[:, 0:GH], front[:, 1, 0:GH], -1.0, None, ALU.mult).then_inc(fb[1].free, 1)
                order(dve, u, dve.scalar_tensor_tensor(out=ab[:, GH:2 * GH], in0=t1[:, :], scalar=-1.0,
                                                       in1=t1[:, :], op0=ALU.mult, op1=ALU.min))
                dve.tensor_scalar(t1[:, :], t1[:, :], 0.0, None, ALU.max).then_inc(gate.full, 1)

            def gates(u, order):
                def after(ins):
                    order(dve, u, ins)

                gate.wait_emptied(dve, u)
                after(dve.tensor_scalar(beta[:, :], ex[:, 0:GH], 1.0, None, ALU.add))
                dve.reciprocal(beta[:, :], beta[:, :]).then_inc(dve_beta, 1)
                after(dve.tensor_scalar(t2[:, :], ex[:, GH:2 * GH], 2.0, None, ALU.add))
                after(dve.reciprocal(t2[:, :], t2[:, :]))
                after(dve.tensor_tensor(t2[:, :], t2[:, :], ex[:, GH:2 * GH], ALU.mult))
                after(dve.tensor_tensor(t3[:, :], t2[:, :], t2[:, :], ALU.mult))
                after(dve.tensor_scalar(g[:, :], t3[:, :], 1.0 / 17, 1.0 / 15, ALU.mult, ALU.add))
                for n in (13, 11, 9, 7, 5, 3, 1):
                    after(dve.tensor_tensor(g[:, :], g[:, :], t3[:, :], ALU.mult))
                    after(dve.tensor_scalar(g[:, :], g[:, :], 1.0 / n, None, ALU.add))
                after(dve.tensor_tensor(g[:, :], g[:, :], t2[:, :], ALU.mult))
                after(dve.scalar_tensor_tensor(out=g[:, :], in0=g[:, :], scalar=2.0, in1=t1[:, :],
                                               op0=ALU.mult, op1=ALU.add))
                after(dve.scalar_tensor_tensor(out=g[:, :], in0=g[:, :], scalar=-1.0, in1=expa[:, :],
                                               op0=ALU.mult, op1=ALU.mult))
                dve.tensor_scalar(g[:, :], g[:, :], -200.0, None, ALU.max).then_inc(dve_g, 1)

            def norm_of(u, order, n):
                dve.wait_ge(squares, u * 2 + (n + 1))
                order(dve, u, dve.tensor_reduce(norm[:, n, :], sq[:, n, :, :], AXX, ALU.add))

            def scaled(n, src, by):
                dve.tensor_tensor(nat[:, n, :, :], src, bcast(by, [P, GH, DK]), ALU.mult).then_inc(dve_nat, 1)

            def ask_norms(u):
                dve.tensor_scalar(norm[:, :, :], norm[:, :, :], RMS_EPS, None, ALU.add).then_inc(root_f.full, 1)

            def normalise(u, order):
                root_f.wait_emptied(dve, u, "qk")
                order(dve, u, dve.tensor_scalar(rnorm[:, 0, :], rnorm[:, 0, :], DK ** -0.5, None, ALU.mult))
                scaled(0, qkvg[:, 1, :, :], rnorm[:, 1, :])
                scaled(3, qkvg[:, 0, :, :], rnorm[:, 0, :])
                dve.wait_ge(dve_nat, u * 5 + 2)
                dve.wait_ge(dve_beta, u + 1)
                scaled(1, nat[:, 0, :, :], beta[:, :])

            FRONT_STEPS, STEPS = 36, 7

            def first(u):
                order = Chain(vec_front, FRONT_STEPS)
                layer_norm(u, order)
                order(dve, u, dve.tensor_copy(X[:, :], Xn[:, :]))
                gate_inputs(u, order)
                gates(u, order)
                norm_of(u, order, 0)
                norm_of(u, order, 1)
                ask_norms(u)
                normalise(u, order)
                order.close()

            def body(t, u):
                inner = Chain(vec, STEPS)
                order = Chain(vec_front, FRONT_STEPS)

                def after(ins):
                    inner(dve, t, ins)

                sbk[0].wait_emptied(dve, t, "cum")
                after(dve.tensor_scalar(egk[:, :], eg[:, 0, :], keep[:, bass.ds(t, 1)], None, ALU.mult))
                dve.tensor_scalar(egc[:, :], eg[:, 2, :], keep[:, bass.ds(t, 1)], None, ALU.mult)\
                   .then_inc(dve_scal, 1)
                after(dve.scalar_tensor_tensor(out=nbe[:, :], in0=egk[:, :], scalar=-1.0, in1=beta[:, :],
                                               op0=ALU.mult, op1=ALU.mult))

                def transposed(n):
                    bank, h = bank_of(dve, t, ("tra", n, 1), "full")
                    dve.tensor_copy(heads(tra[:, n], 1), split(bank)).then_inc(h.free, 1)

                transposed(0)
                scaled(2, nat[:, 0, :, :], nbe[:, :])
                transposed(3)
                scaled(4, nat[:, 3, :, :], egk[:, :])
                transposed(1)
                transposed(2)
                transposed(4)
                dve.wait_ge(pool_E, t + 1)
                for k in range(GH // 2):
                    bank, h = bank_of(dve, t, ("mp", k), "full")
                    dve.tensor_tensor(mp[:, 2 * k:2 * k + 2, :, :],
                                      bank.rearrange("p (h a e) -> p h a e", h=2, a=2),
                                      E[:, 2 * k:2 * k + 2, :].unsqueeze(2).broadcast_to([P, 2, 2, P]),
                                      ALU.mult).then_inc(h.free, 1)
                for k in range(G):
                    for i in (2 * k + 1, 2 * k):
                        emptied(dve, t, ("mp", i))
                    after(dve.tensor_tensor(heads(Xl, k), mp[:, HG * k:HG * (k + 1), 0, :],
                                            level[:, 0, :].unsqueeze(1).broadcast_to([P, HG, P]), ALU.mult))
                    dve.tensor_tensor(heads(Y, k), ident[:, :].unsqueeze(1).broadcast_to([P, HG, P]),
                                      heads(Xl, k), ALU.subtract).then_inc(Y_done[k], 1)
                for l in range(1, LEVELS):
                    for k in range(G):
                        bank, h = bank_of(dve, t, ("a", l, k), "full")
                        dve.tensor_tensor(heads(Xl, k), split(bank),
                                          level[:, l, :].unsqueeze(1).broadcast_to([P, HG, P]), ALU.mult)\
                           .then_inc(h.free, 1)
                    for k in range(G):
                        bank, h = bank_of(dve, t, ("b", l, k), "full")
                        dve.tensor_tensor(heads(Y, k), heads(Y, k), split(bank), ALU.subtract)\
                           .then_inc(h.free, 1)
                dve.wait_ge(pool_nat, t * 2 + 2)
                for k in range(G):
                    sbk[k].wait_full(dve, t, "ks")
                    dve.tensor_tensor(heads(R, k), grp(stateb, k), heads(nat[:, 6], k), ALU.add)\
                       .then_inc(sbk[k].free, 1)
                if u is not None:
                    layer_norm(u, order)
                for k in range(G):
                    sbk[k].wait_full(dve, t, "s")
                    for h in range(HG):
                        ins = dve.scalar_tensor_tensor(out=St[:, HG * k + h, :], in0=St[:, HG * k + h, :],
                                                       scalar=egc[:, HG * k + h:HG * k + h + 1],
                                                       in1=stateb[:, k, h * P:(h + 1) * P],
                                                       op0=ALU.mult, op1=ALU.add)
                    ins.then_inc(sbk[k].free, 1)
                dve.wait_ge(squares_o, t * 2 + 2)
                after(dve.tensor_reduce(osum[:, :], sqo, AXX, ALU.add))
                dve.tensor_scalar(osum[:, :], osum[:, :], 1.0 / DK, RMS_EPS, ALU.mult, ALU.add)\
                   .then_inc(root.full, 1)
                if u is not None:
                    gate_inputs(u, order)
                root.wait_emptied(dve, t, "o")
                dve.wait_ge(pool_og, t + 1)
                dve.tensor_tensor(og[:, :, :], og[:, :, :], bcast(ro[:, :], [P, GH, DK]), ALU.mult)\
                   .then_inc(og_done, 1)
                if u is not None:
                    gates(u, order)
                    norm_of(u, order, 0)
                sbk[0].wait_full(dve, t, "wo")
                dve.tensor_tensor(X2[:, :], stateb[:, 0, 0:D], X[:, :], ALU.add).then_inc(sbk[0].free, 1)
                sbk[0].wait_emptied(dve, t, "wo")
                mean_square(inner, t, X2[:, :], 2, root, "rms2", M[:, :], m_done)
                if u is not None:
                    order(dve, u, dve.tensor_copy(X[:, :], Xn[:, :]))
                for k in range(2):
                    bank, h = bank_of(dve, t, ("hid", k), "full")
                    dve.wait_ge(hid_relu, t * 2 + (k + 1))
                    dve.tensor_tensor(heads(hT, k), split(bank), heads(hid, k), ALU.mult).then_inc(h.free, 1)
                if u is not None:
                    norm_of(u, order, 1)
                    ask_norms(u)
                sbk[1].wait_full(dve, t, "down")
                dve.tensor_tensor(y[:, :], stateb[:, 1, 0:D], X2[:, :], ALU.add).then_inc(sbk[1].free, 1)
                sbk[1].wait_emptied(dve, t, "down")
                after(dve.tensor_tensor(row(t), row(t), y[:, :], ALU.add))
                if u is not None:
                    normalise(u, order)
                    order.close()
                inner.close()

            dve.wait_ge(weights_in, IN)
            dve.memset(St[:, :, :], 0.0).then_inc(cleared, 1)
            dve.wait_ge(cleared, 1)
            dve.wait_ge(expa_done, 1)
            ahead(dve, TURNS, first, body)

        @block.tensor
        def _(pe):
            def transposes(out, src, n):
                for i in range(n):
                    mm = pe.transpose(out[:, i * P:(i + 1) * P], src(i), ident[:, :])
                return mm

            def project(u, n, f):
                fb[f].wait_free(pe, u, ("proj", n, f))
                for c in range(ND):
                    mm = pe.matmul(front[:, f, :], RT[:, c, :], wq4[:, c, n, f * BANK:(f + 1) * BANK],
                                   start=(c == 0), stop=(c == ND - 1))
                mm.then_inc(fb[f].full, 1)

            def front_start(u):
                pe.wait_ge(rn_done, u + 1)
                fb[0].wait_free(pe, u, "RT")
                transposes(front[:, 0, :], lambda i: Rn[:, i * P:(i + 1) * P], ND).then_inc(fb[0].full, 1)
                fb[0].wait_emptied(pe, u, "RT")
                fb[1].wait_free(pe, u, "ab")
                for c in range(ND):
                    mm = pe.matmul(front[:, 1, 0:2 * GH], RT[:, c, :], wab[:, c, :], start=(c == 0),
                                   stop=(c == ND - 1))
                mm.then_inc(fb[1].full, 1)
                project(u, 0, 0)
                project(u, 0, 1)
                project(u, 1, 0)

            def front_middle(u):
                project(u, 1, 1)
                project(u, 2, 0)

            def first(u):
                front_start(u)
                front_middle(u)
                project(u, 2, 1)
                project(u, 3, 0)
                project(u, 3, 1)

            def body(t, u):
                pe.wait_ge(dve_g, t + 1)
                sbk[0].wait_free(pe, t, "cum")
                for n, mask in enumerate((upto, beyond, ones)):
                    mm = pe.matmul(stateb[:, 0, n * GH:(n + 1) * GH], mask[:, :], g[:, :], start=True, stop=True)
                mm.then_inc(sbk[0].full, 1)
                pe.wait_ge(pool_gu, t + 1)
                for k in range(G):
                    out, h = bank_of(pe, t, ("decay", k), "free")
                    pe.matmul(out, beyond[:, :], heads(gu, k), start=True, stop=True).then_inc(h.full, 1)
                for i, n in enumerate(TRANSPOSED):
                    pe.wait_ge(dve_nat, t * 5 + (1, 2, 3, 4, 5)[i])
                    for k in range(G):
                        out, h = bank_of(pe, t, ("tra", n, k), "free")
                        transposes(out, lambda i: nat[:, n, HG * k + i, :], HG).then_inc(h.full, 1)
                for k in range(GH // 2):
                    for n in (3, 1):
                        emptied(pe, t, ("tra", n, k // 2))
                    out, hand = bank_of(pe, t, ("mp", k), "free")
                    for i in range(2):
                        h = 2 * k + i
                        pe.matmul(out[:, 2 * i * P:(2 * i + 1) * P], tra[:, 0, h, :], tra[:, 1, h, :],
                                  start=True, stop=True)
                        mm = pe.matmul(out[:, (2 * i + 1) * P:(2 * i + 2) * P], tra[:, 0, h, :], tra[:, 3, h, :],
                                       start=True, stop=True)
                    mm.then_inc(hand.full, 1)
                for l in range(LEVELS):
                    for k in range(G):
                        if l == 0:
                            pe.wait_ge(Y_done[k], t + 1)
                        else:
                            emptied(pe, t, ("t", l - 1, k))
                            out, hand = bank_of(pe, t, ("a", l, k), "free")
                            for h in range(HG):
                                mm = pe.matmul(out[:, h * P:(h + 1) * P], mp[:, HG * k + h, 0, :],
                                               T[:, HG * k + h, :], start=True, stop=True)
                            mm.then_inc(hand.full, 1)
                    if l > 0:
                        for k in range(G):
                            emptied(pe, t, ("a", l, k))
                            out, hand = bank_of(pe, t, ("b", l, k), "free")
                            for h in range(HG):
                                mm = pe.matmul(out[:, h * P:(h + 1) * P], Xl[:, HG * k + h, :],
                                               Y[:, HG * k + h, :], start=True, stop=True)
                            mm.then_inc(hand.full, 1)
                    if l < LEVELS - 1:
                        for k in range(G):
                            if l > 0:
                                emptied(pe, t, ("b", l, k))
                            out, hand = bank_of(pe, t, ("t", l, k), "free")
                            transposes(out, lambda i: Y[:, HG * k + i, :], HG).then_inc(hand.full, 1)
                for k in range(G):
                    emptied(pe, t, ("tra", 2, k))
                    sbk[k].wait_free(pe, t, "ks")
                    for h in range(HG):
                        mm = pe.matmul(stateb[:, k, h * P:(h + 1) * P], tra[:, 2, HG * k + h, :],
                                       St[:, HG * k + h, :], start=True, stop=True)
                    mm.then_inc(sbk[k].full, 1)
                for k in range(G):
                    emptied(pe, t, ("b", LEVELS - 1, k))
                    sbk[k].wait_emptied(pe, t, "ks")
                    for h in range(HG):
                        mm = pe.matmul(stateb[:, k, h * P:(h + 1) * P], Y[:, HG * k + h, :],
                                       R[:, HG * k + h, :], start=True, stop=True)
                    mm.then_inc(sbk[k].full, 1)
                for k in range(G):
                    emptied(pe, t, ("tra", 4, k))
                    sbk[k].wait_emptied(pe, t, "u")
                    for h in range(HG):
                        out = stateb[:, k, h * P:(h + 1) * P]
                        pe.matmul(out, tra[:, 4, HG * k + h, :], St[:, HG * k + h, :], start=True, stop=False)
                        mm = pe.matmul(out, mp[:, HG * k + h, 1, :], U[:, HG * k + h, :], start=False, stop=True)
                    mm.then_inc(sbk[k].full, 1)
                pe.wait_ge(pool_nat, t * 2 + 1)
                for k in range(G):
                    sbk[k].wait_emptied(pe, t, "o")
                    for h in range(HG):
                        mm = pe.matmul(stateb[:, k, h * P:(h + 1) * P], nat[:, 5, HG * k + h, :],
                                       U[:, HG * k + h, :], start=True, stop=True)
                    mm.then_inc(sbk[k].full, 1)
                if u is not None:
                    front_start(u)
                pe.wait_ge(og_done, t + 1)
                for k in range(G):
                    out, h = bank_of(pe, t, ("ogT", k), "free")
                    transposes(out, lambda i: og[:, HG * k + i, :], HG).then_inc(h.full, 1)
                sbk[0].wait_free(pe, t, "wo")
                for h in range(GH):
                    if h % HG == 0:
                        emptied(pe, t, ("ogT", h // HG))
                    mm = pe.matmul(stateb[:, 0, 0:D], ogT[:, h, :], wo[:, h, :], start=(h == 0), stop=(h == GH - 1))
                mm.then_inc(sbk[0].full, 1)
                if u is not None:
                    front_middle(u)
                pe.wait_ge(m_done, t + 1)
                out, h = bank_of(pe, t, ("mT",), "free")
                transposes(out, lambda i: M[:, i * P:(i + 1) * P], ND).then_inc(h.full, 1)
                emptied(pe, t, ("mT",))
                for k in range(2):
                    out, h = bank_of(pe, t, ("hid", k), "free")
                    for f in range(4):
                        for c in range(ND):
                            mm = pe.matmul(out[:, f * P:(f + 1) * P], wfc[:, c, (4 * k + f) * P:(4 * k + f + 1) * P],
                                           MT[:, c, :], start=(c == 0), stop=(c == ND - 1))
                    mm.then_inc(h.full, 1)
                if u is not None:
                    project(u, 2, 1)
                sbk[1].wait_free(pe, t, "down")
                for f in range(FF // P):
                    if f % 4 == 0:
                        emptied(pe, t, ("hid", f // 4))
                    mm = pe.matmul(stateb[:, 1, 0:D], hT[:, f, :], wproj[:, f, :], start=(f == 0),
                                   stop=(f == FF // P - 1))
                mm.then_inc(sbk[1].full, 1)
                if u is not None:
                    for f in range(2):
                        project(u, 3, f)

            pe.wait_ge(weights_in, IN)
            ahead(pe, TURNS, first, body)


def experts_stage(nc, w, resid, ident):
    TURNS = B
    NX = NE + 1
    SIZES = [128, 128, EH - 256]
    NM = len(SIZES)
    with ExitStack() as ctx:
        def sb(name, shape, dt=F32):
            return ctx.enter_context(nc.sbuf_tensor(name, shape, dt))

        def sem(name):
            return ctx.enter_context(nc.semaphore(name))

        norm = Norm(ctx, nc, "m")
        gw = sb("gw", [P, ND, NE])
        gb = sb("gb", [P, NE])
        before = sb("before", [P, NE, NE])
        w13 = sb("w13", [P, NX, 2, ND, EH])
        b13 = sb("b13", [P, NX, 2, NM])
        w2 = sb("w2", [P, NX, NM, D])
        XT = sb("m_XT", [P, ND, S])
        lg = sb("lg", [P, NJ, NE])
        eq = sb("eq", [P, NJ, NE, NE])
        gt = sb("gt", [P, NJ, NE, NE])
        small = sb("small", [P, NJ])
        score = sb("score", [P, NJ, NE])
        biased = sb("biased", [P, NJ, NE])
        rank = sb("rank", [P, NJ, NE])
        rw = sb("rw", [P, NJ, NX])
        up = sb("up", [P, 2, S])
        pre = sb("pre", [P, 2, S])
        hT = sb("m_hT", [P, 2, NM, S])

        ups = ctx.enter_context(nc.psum_tensor("m_ups", [P, 2, 2, BANK], F32))
        outs = ctx.enter_context(nc.psum_tensor("m_outs", [P, 2, 2, BANK], F32))

        tiles = [(e, m) for e in range(NX) for m in range(NM)]
        first = [["XT0", "gate"], ["XT1"]]
        hb = [Handoff(ctx, nc, f"m_up{k}", first[k] + [x for n, x in enumerate(tiles) if n % 2 == k]) for k in range(2)]
        hid_done = sem("m_hid_done")
        ob = [Handoff(ctx, nc, f"m_out{k}", range(k, NX, 2)) for k in range(2)]
        up_done = sem("m_up_done")
        small_in = sem("m_small_in")
        w_in = [sem(f"m_w_in{e}") for e in range(NX)]
        vec_norm = sem("m_vector_order_norm")
        vec = sem("m_vector_order")
        ones_done = sem("m_ones_done")
        lg_done = sem("m_logits")
        lg_exp = sem("m_exps")

        block = ctx.enter_context(nc.Block())

        @block.sync
        def _(sp):
            for h in (*hb, *ob):
                h.open(sp)
            sp.dma_start(gw[:, :, :], w["gw"].rearrange("(c p) n -> p c n", p=P)).then_inc(small_in, 16)
            sp.dma_start(gb[:, :], w["gb"].partition_broadcast(P)).then_inc(small_in, 16)
            sp.dma_start(before[:, :, :], w["before"].partition_broadcast(P)
                         .rearrange("p a (e f) -> p (a e) f", e=NE)).then_inc(small_in, 16)
            sp.dma_start(b13[:, :, :, :], w["b13"]).then_inc(small_in, 16)
            for e in range(NX):
                sp.dma_start(w13[:, e, :, :, :], w["w13"][e]).then_inc(w_in[e], 16)
                sp.dma_start(w2[:, e, 0:2, :], w["w2a"][e]).then_inc(w_in[e], 16)
                sp.dma_start(w2[0:SIZES[2] + 1, e, 2, :], w["w2b"][e]).then_inc(w_in[e], 16)

        @block.gpsimd
        def _(pool):
            pool.memset(hT[SIZES[2]:SIZES[2] + 1, :, NM - 1, :], 1.0).then_inc(ones_done, 1)
            pool.wait_ge(ones_done, 1)
            pool.memset(rw[:, :, NE:NX], 1.0).then_inc(ones_done, 1)
            pool.wait_ge(ones_done, 2)
            norm.pool_constants(pool)
            with pool.Fori(0, TURNS) as t:
                norm.pool_root(pool, t)

        @block.scalar
        def _(act):
            act.wait_ge(small_in, 4 * 16)
            with act.Fori(0, TURNS) as t:
                for c in range(ND):
                    hb[c].wait_full(act, t, f"XT{c}")
                    act.activation(XT[:, c, :], ups[:, c, 0, :], ACT.Copy).then_inc(hb[c].free, 1)
                act.wait_ge(lg_done, t + 1)
                act.activation(lg[:, :, :], lg[:, :, :], ACT.Exp).then_inc(lg_exp, 1)

                def silu(n):
                    e, m = tiles[n]
                    s, k = SIZES[m], n % 2
                    hb[k].wait_emptied(act, t, (e, m))
                    if e >= 2:
                        ob[e % 2].wait_full(act, t, e - 2)
                    act.activation(hT[0:s, e % 2, m, :], pre[0:s, k, :], ACT.Silu).then_inc(hid_done, 1)

                for n, (e, m) in enumerate(tiles):
                    s, k = SIZES[m], n % 2
                    hb[k].wait_full(act, t, (e, m))
                    act.activation(up[0:s, k, :], ups[0:s, k, 0, :], ACT.Identity, bias=b13[0:s, e, 0, m:m + 1])\
                       .then_inc(up_done, 1)
                    if n > 0:
                        silu(n - 1)
                silu(len(tiles) - 1)

        @block.vector
        def _(dve):
            dve.wait_ge(small_in, 4 * 16)
            dve.wait_ge(ones_done, 2)

            def normalise(u):
                order = Chain(vec_norm, Norm.DVE_STEPS)
                norm.vector_statistics(dve, u, lambda ins: order(dve, u, ins), resid)
                norm.vector_scale(dve, u, resid)
                order.close()

            def body(t, u):
                order = Chain(vec, 10)

                def after(ins):
                    order(dve, t, ins)

                hb[0].wait_full(dve, t, "gate")
                logits = ups[:, 0, 0, 0:NJ * NE].rearrange("p (j e) -> p j e", j=NJ)
                after(dve.tensor_reduce(small[:, :], logits, AXX, ALU.max))
                dve.tensor_tensor(lg[:, :, :], logits, bcast(small[:, :], [P, NJ, NE]), ALU.subtract)\
                    .then_inc(hb[0].free, 1)
                hb[0].wait_emptied(dve, t, "gate")
                dve.sem_inc(lg_done, 1)
                dve.wait_ge(lg_exp, t + 1)
                after(dve.tensor_reduce(small[:, :], lg[:, :, :], AXX, ALU.add))
                after(dve.reciprocal(small[:, :], small[:, :]))
                after(dve.tensor_tensor(score[:, :, :], lg[:, :, :], bcast(small[:, :], [P, NJ, NE]), ALU.mult))
                after(dve.tensor_tensor(biased[:, :, :], score[:, :, :],
                                        gb[:, :].unsqueeze(1).broadcast_to([P, NJ, NE]), ALU.add))
                mine = bcast(biased[:, :, :], [P, NJ, NE, NE])
                other = biased[:, :, :].unsqueeze(2).broadcast_to([P, NJ, NE, NE])
                dve.tensor_tensor(gt[:, :, :, :], other, mine, ALU.is_gt)
                after(dve.tensor_tensor(eq[:, :, :, :], other, mine, ALU.is_equal))
                after(dve.tensor_tensor(eq[:, :, :, :], eq[:, :, :, :],
                                        before[:, :, :].unsqueeze(1).broadcast_to([P, NJ, NE, NE]), ALU.mult))
                after(dve.tensor_tensor(gt[:, :, :, :], gt[:, :, :, :], eq[:, :, :, :], ALU.add))
                after(dve.tensor_reduce(rank[:, :, :], gt[:, :, :, :], AXX, ALU.add))
                after(dve.scalar_tensor_tensor(out=rw[:, :, 0:NE], in0=rank[:, :, :], scalar=float(TOPK) - 0.5,
                                               in1=score[:, :, :], op0=ALU.is_lt, op1=ALU.mult))

                def combine(e):
                    ob[e % 2].wait_full(dve, t, e)
                    if e >= 1:
                        ob[(e - 1) % 2].wait_emptied(dve, t, e - 1)
                    for j in range(NJ):
                        row = resid[:, bass.ds(t * NJ + j, 1), :].rearrange("p a d -> p (a d)")
                        ins = dve.scalar_tensor_tensor(
                            out=row, in0=outs[:, e % 2, j // 2, (j % 2) * D:(j % 2 + 1) * D],
                            scalar=rw[:, j, e:e + 1], in1=row, op0=ALU.mult, op1=ALU.add)
                    ins.then_inc(ob[e % 2].free, 1)

                for n, (e, m) in enumerate(tiles):
                    s, k = SIZES[m], n % 2
                    dve.wait_ge(up_done, t * len(tiles) + (n + 1))
                    dve.scalar_tensor_tensor(out=pre[0:s, k, :], in0=ups[0:s, k, 1, :],
                                             scalar=b13[0:s, e, 1, m:m + 1], in1=up[0:s, k, :],
                                             op0=ALU.add, op1=ALU.mult).then_inc(hb[k].free, 1)
                    if e >= 1 and m == NM - 1:
                        combine(e - 1)
                    if u is not None and n == len(tiles) - 2:
                        normalise(u)
                combine(NX - 1)
                order.close()

            ahead(dve, TURNS, normalise, body)

        @block.tensor
        def _(pe):
            pe.wait_ge(small_in, 4 * 16)
            pe.wait_ge(ones_done, 2)
            with pe.Fori(0, TURNS) as t:
                pe.wait_ge(norm.x_done, t * NJ + NJ)
                for c in range(ND):
                    hb[c].wait_free(pe, t, f"XT{c}")
                    transpose_sequence(pe, ups[:, c, 0, :], norm.x, c, ident).then_inc(hb[c].full, 1)
                for c in range(ND):
                    hb[c].wait_emptied(pe, t, f"XT{c}")
                hb[0].wait_free(pe, t, "gate")
                for j in range(NJ):
                    for c in range(ND):
                        mm = pe.matmul(ups[:, 0, 0, j * NE:(j + 1) * NE], XT[:, c, j * P:(j + 1) * P], gw[:, c, :],
                                       start=(c == 0), stop=(c == ND - 1))
                mm.then_inc(hb[0].full, 1)

                def down(e):
                    k = e % 2
                    pe.wait_ge(hid_done, t * len(tiles) + (e + 1) * NM)
                    ob[k].wait_free(pe, t, e)
                    for j in range(NJ):
                        for m, s in enumerate(SIZES):
                            rows = s + (m == NM - 1)
                            mm = pe.matmul(outs[:, k, j // 2, (j % 2) * D:(j % 2 + 1) * D],
                                           hT[0:rows, k, m, j * P:(j + 1) * P], w2[0:rows, e, m, :],
                                           start=(m == 0), stop=(m == NM - 1))
                    mm.then_inc(ob[k].full, 1)

                for n, (e, m) in enumerate(tiles):
                    s, k = SIZES[m], n % 2
                    if m == 0:
                        pe.wait_ge(w_in[e], 3 * 16)
                    hb[k].wait_free(pe, t, (e, m))
                    for i in range(2):
                        for c in range(ND):
                            mm = pe.matmul(ups[0:s, k, i, :], w13[:, e, i, c, m * P:m * P + s], XT[:, c, :],
                                           start=(c == 0), stop=(c == ND - 1))
                    mm.then_inc(hb[k].full, 1)
                    if e >= 1 and m == 1:
                        down(e - 1)
                down(NX - 1)


def convolution_stage(nc, w, resid, ident):
    LA, LB = 32, 16
    ROWS = 2 * MODES
    GROUPS = D // 4
    NFT = NF // P
    HALF = NFT // 2
    TURNS = B
    with ExitStack() as outer:
        fwd = outer.enter_context(nc.sbuf_tensor("fwd", [P, NJ, NF], F32))
        inv = outer.enter_context(nc.sbuf_tensor("inv", [P, NFT, S], F32))
        ka = outer.enter_context(nc.sbuf_tensor("ka", [P, HALF, 2, D], F32))
        kb = outer.enter_context(nc.sbuf_tensor("kb", [P, HALF, 2, D], F32))
        mats_in = outer.enter_context(nc.semaphore("mats_in"))
        convolution_kernel(nc, w, fwd, inv, ka, kb, mats_in, LA, LB, ROWS, GROUPS, NFT, HALF)

        with ExitStack() as ctx:
            def sb(name, shape, dt=F32):
                return ctx.enter_context(nc.sbuf_tensor(name, shape, dt))

            def sem(name):
                return ctx.enter_context(nc.semaphore(name))

            norm = Norm(ctx, nc, "c")
            pa = sb("pa", [P, 2, 2, D])
            pb = sb("pb", [P, 2, 2, D])
            ys = sb("ys", [P, HALF, 2, D])
            spec = ctx.enter_context(nc.psum_tensor("spec", [P, HALF, 2, D], F32))
            back = ctx.enter_context(nc.psum_tensor("back", [P, 2, 2, D], F32))
            sp_h = [Handoff(ctx, nc, f"c_spec{k}") for k in range(HALF)]
            pr_h = [Handoff(ctx, nc, f"c_prod{k}", range(k, HALF, 2)) for k in range(2)]
            back_h = [Handoff(ctx, nc, f"c_back{k}") for k in range(2)]
            ys_done = sem("c_ys_done")
            vec = sem("c_vector_order")

            block = ctx.enter_context(nc.Block())

            @block.sync
            def _(sp):
                for h in (*sp_h, *pr_h, *back_h):
                    h.open(sp)

            @block.gpsimd
            def _(pool):
                def body(t, u):
                    for m in range(HALF):
                        sp_h[m].wait_emptied(pool, t)
                        pool.tensor_tensor(ys[:, m, :, :], pa[:, m % 2, :, :], pb[:, m % 2, :, :], ALU.add)\
                            .then_inc(pr_h[m % 2].free, 1)
                    if u is not None:
                        norm.pool_root(pool, u)

                norm.pool_constants(pool)
                ahead(pool, TURNS, lambda u: norm.pool_root(pool, u), body)

            @block.vector
            def _(dve):
                def normalise(u):
                    order = Chain(vec, Norm.DVE_STEPS)
                    norm.vector_statistics(dve, u, lambda ins: order(dve, u, ins), resid)
                    norm.vector_scale(dve, u, resid)
                    order.close()

                def body(t, u):
                    for m in range(HALF):
                        sp_h[m].wait_full(dve, t)
                        pr_h[m % 2].wait_free(dve, t, m)
                        dve.tensor_tensor(pa[:, m % 2, :, :], spec[:, m, 0, :].unsqueeze(1).broadcast_to([P, 2, D]),
                                          ka[:, m, :, :], ALU.mult)
                        dve.tensor_tensor(pb[:, m % 2, :, :], spec[:, m, 1, :].unsqueeze(1).broadcast_to([P, 2, D]),
                                          kb[:, m, :, :], ALU.mult).then_inc(sp_h[m].free, 1)
                    if u is not None:
                        normalise(u)
                    for k in range(2):
                        back_h[k].wait_full(dve, t)
                        rows = resid[:, bass.ds(t * NJ + 2 * k, 2), :]
                        dve.tensor_tensor(rows, rows, back[:, k, :, :], ALU.add).then_inc(back_h[k].free, 1)

                ahead(dve, TURNS, normalise, body)

            @block.tensor
            def _(pe):
                with pe.Fori(0, TURNS) as t:
                    pe.wait_ge(norm.x_done, t * NJ + NJ)
                    for m in range(HALF):
                        sp_h[m].wait_free(pe, t)
                        for part in range(2):
                            f = (part * HALF + m) * P
                            for j in range(NJ):
                                mm = pe.matmul(spec[:, m, part, :], fwd[:, j, f:f + P], norm.x[:, j, :],
                                               start=(j == 0), stop=(j == NJ - 1))
                        mm.then_inc(sp_h[m].full, 1)
                    for m in (HALF - 2, HALF - 1):
                        pr_h[m % 2].wait_emptied(pe, t, m)
                    for j in range(NJ):
                        if j % 2 == 0:
                            back_h[j // 2].wait_free(pe, t)
                        for f in range(NFT):
                            mm = pe.matmul(back[:, j // 2, j % 2, :], inv[:, f, j * P:(j + 1) * P],
                                           ys[:, f % HALF, f // HALF, :], start=(f == 0), stop=(f == NFT - 1))
                        if j % 2 == 1:
                            mm.then_inc(back_h[j // 2].full, 1)


def convolution_kernel(nc, w, fwd, inv, ka, kb, mats_in, LA, LB, ROWS, GROUPS, NFT, HALF):
    CH = 8
    NCA, NCB = LA // CH, LB // CH
    MAGIC = 1.5 * 2.0 ** 23
    TWO_PI_HI = 6.28125
    TWO_PI_LO = 2 * np.pi - TWO_PI_HI
    PI = 3.1415925
    with ExitStack() as ctx:
        def sb(name, shape, dt=F32):
            return ctx.enter_context(nc.sbuf_tensor(name, shape, dt))

        def sem(name):
            return ctx.enter_context(nc.semaphore(name))

        par = sb("par", [ROWS, 5, D])
        lv = sb("lv", [ROWS, LA + LB])
        names = ("dt", "are", "dre", "dim", "em1", "er", "sn", "cs", "hs", "nr", "ni", "wr", "wi",
                 "den", "u", "v", "al", "be")
        v = {n: sb("k_" + n, [ROWS, D]) for n in names}
        th = sb("th", [ROWS, CH, D])
        kk = sb("kk", [ROWS, CH, D])
        mg = sb("mg", [ROWS, CH, D])
        arg = sb("arg", [ROWS, CH, D])
        cz = sb("cz", [ROWS, CH, D])
        q = sb("q", [ROWS, GROUPS, 4, LA])
        pz = sb("pz", [ROWS, LB, D])
        kl = sb("kl", [P, LB, GROUPS])
        kt = sb("kt", [P, NJ, D])
        drow = sb("drow", [1, D])
        scratch = nc.dram_tensor("k_scratch", (S, D), F32).ap()
        kp = ctx.enter_context(nc.psum_tensor("kp", [P, 8, 8, 64], F32))

        params_in = sem("params_in")
        vec = sem("k_vector_order")
        tables_done = sem("k_tables_done")
        ask = sem("k_ask")
        ans = sem("k_answer")
        products = sem("k_products")
        gathered = sem("k_gathered")
        stored = sem("k_stored")
        loaded = sem("k_loaded")
        row_done = sem("k_row_done")
        spectra = sem("k_spectra")

        block = ctx.enter_context(nc.Block())

        @block.sync
        def _(sp):
            for half in range(2):
                rows = slice(MODES * half, MODES * (half + 1))
                sp.dma_start(par[rows, 0, :], w["log_dt"].partition_broadcast(MODES)
                             .rearrange("p a h -> p (a h)")).then_inc(params_in, 16)
                sp.dma_start(par[rows, 1:5, :], w["modes"]).then_inc(params_in, 16)
            sp.dma_start(lv[:, :], w["lvals"].partition_broadcast(ROWS)
                         .rearrange("p a l -> p (a l)")).then_inc(params_in, 16)
            sp.dma_start(drow[:, :], w["skip"]).then_inc(params_in, 16)
            sp.dma_start(fwd[:, :, :], w["fwd"].rearrange("(j p) f -> p j f", p=P)).then_inc(mats_in, 16)
            sp.dma_start(inv[:, :, :], w["inv"].rearrange("(m p) l -> p m l", p=P)).then_inc(mats_in, 16)
            sp.wait_ge(gathered, 8)
            dst = scratch.rearrange("(a b) (j g) -> j a b g", b=LB, j=4)
            for j in range(4):
                sp.dma_start(dst[j], kl[32 * j:32 * j + 32, :, :]).then_inc(stored, 16)
            sp.wait_ge(stored, 4 * 16)
            sp.dma_start(kt[:, :, :], scratch.rearrange("(t p) h -> p t h", p=P)).then_inc(loaded, 16)

        asked = [(ACT.Exp, v["dt"], par[:, 0, :], 1.0), (ACT.Exp, v["are"], par[:, 1, :], 1.0),
                 (ACT.Tanh, v["em1"], v["dre"][:, :], 0.5)]
        trig = [(v["sn"], v["sn"]), (v["cs"], v["cs"]), (v["hs"], v["hs"])]

        @block.scalar
        def _(act):
            act.wait_ge(params_in, 6 * 16)
            for n, (f, out, src, scale) in enumerate(asked):
                if n == 2:
                    act.wait_ge(ask, 1)
                act.activation(out[:, :], src, f, scale=scale).then_inc(ans, 1)
            act.wait_ge(ask, 2)
            for out, src in trig:
                act.activation(out[:, :], src[:, :], ACT.Sin).then_inc(ans, 1)
            for n in range(NCA + NCB):
                act.wait_ge(ask, 3 + n)
                act.activation(mg[:, :, :], mg[:, :, :], ACT.Exp).then_inc(ans, 1)
                act.activation(arg[:, :, :], arg[:, :, :], ACT.Sin).then_inc(ans, 1)
                if n >= NCA:
                    act.activation(cz[:, :, :], cz[:, :, :], ACT.Sin).then_inc(ans, 1)

        @block.vector
        def _(dve):
            count = [0]

            def after(ins):
                count[0] += 1
                ins.then_inc(vec, 1)
                dve.wait_ge(vec, count[0])

            def tt(o, a, b, op):
                after(dve.tensor_tensor(v[o][:, :], v[a][:, :], v[b][:, :], op))

            def stt(o, a, s, b, op0, op1):
                after(dve.scalar_tensor_tensor(out=v[o][:, :], in0=v[a][:, :], scalar=s, in1=v[b][:, :],
                                               op0=op0, op1=op1))

            def ts(o, a, s1, s2, op0, op1):
                after(dve.tensor_scalar(v[o][:, :], v[a][:, :], s1, s2, op0, op1))

            def reduce_angle(angle, turns):
                after(dve.tensor_scalar(turns, angle, 1 / (2 * np.pi), MAGIC, ALU.mult, ALU.add))
                after(dve.tensor_scalar(turns, turns, -MAGIC, None, ALU.add))
                after(dve.scalar_tensor_tensor(out=angle, in0=turns, scalar=-TWO_PI_HI, in1=angle,
                                               op0=ALU.mult, op1=ALU.add))
                after(dve.scalar_tensor_tensor(out=angle, in0=turns, scalar=-TWO_PI_LO, in1=angle,
                                               op0=ALU.mult, op1=ALU.add))
                after(dve.tensor_scalar(angle, angle, PI, -PI, ALU.min, ALU.max))

            def cosine_angle(out, angle):
                after(dve.scalar_tensor_tensor(out=out, in0=angle, scalar=-1.0, in1=angle,
                                               op0=ALU.mult, op1=ALU.min))
                after(dve.tensor_scalar(out, out, float(np.pi / 2), None, ALU.add))

            M, A_, S_ = ALU.mult, ALU.add, ALU.subtract
            dve.wait_ge(params_in, 6 * 16)
            dve.wait_ge(ans, 2)
            ts("are", "are", -1.0, None, M, ALU.bypass)
            tt("dre", "are", "dt", M)
            after(dve.tensor_tensor(v["dim"][:, :], par[:, 2, :], v["dt"][:, :], M))
            dve.sem_inc(ask, 1)
            after(dve.tensor_copy(v["sn"][:, :], v["dim"][:, :]))
            reduce_angle(v["sn"][:, :], v["u"][:, :])
            cosine_angle(v["cs"][:, :], v["sn"][:, :])
            ts("hs", "sn", 0.5, None, M, ALU.bypass)
            dve.sem_inc(ask, 1)
            dve.wait_ge(ans, 6)
            ts("u", "em1", -1.0, 1.0, M, A_)
            after(dve.reciprocal(v["u"][:, :], v["u"][:, :]))
            stt("em1", "em1", 2.0, "u", M, M)
            ts("er", "em1", 1.0, None, A_, ALU.bypass)
            tt("nr", "em1", "cs", M)
            tt("hs", "hs", "hs", M)
            stt("nr", "hs", -2.0, "nr", M, A_)
            tt("ni", "er", "sn", M)
            after(dve.tensor_tensor(v["wr"][:, :], par[:, 3, :], v["nr"][:, :], M))
            after(dve.tensor_tensor(v["u"][:, :], par[:, 4, :], v["ni"][:, :], M))
            tt("wr", "wr", "u", S_)
            after(dve.tensor_tensor(v["wi"][:, :], par[:, 3, :], v["ni"][:, :], M))
            after(dve.tensor_tensor(v["u"][:, :], par[:, 4, :], v["nr"][:, :], M))
            tt("wi", "wi", "u", A_)
            tt("den", "are", "are", M)
            after(dve.tensor_tensor(v["u"][:, :], par[:, 2, :], par[:, 2, :], M))
            tt("den", "den", "u", A_)
            after(dve.reciprocal(v["den"][:, :], v["den"][:, :]))
            tt("u", "wr", "are", M)
            after(dve.tensor_tensor(v["v"][:, :], v["wi"][:, :], par[:, 2, :], M))
            tt("u", "u", "v", A_)
            tt("u", "u", "den", M)
            tt("v", "wi", "are", M)
            after(dve.tensor_tensor(v["wr"][:, :], v["wr"][:, :], par[:, 2, :], M))
            tt("v", "v", "wr", S_)
            tt("v", "v", "den", M)
            re, im = slice(0, MODES), slice(MODES, ROWS)
            after(dve.tensor_scalar(v["al"][re, :], v["u"][re, :], 2.0, None, M))
            after(dve.tensor_scalar(v["be"][re, :], v["v"][re, :], -2.0, None, M))
            after(dve.tensor_scalar(v["al"][im, :], v["v"][im, :], -2.0, None, M))
            after(dve.tensor_scalar(v["be"][im, :], v["u"][im, :], -2.0, None, M))

            got = 6
            for n in range(NCA + NCB):
                steps = bcast(lv[:, CH * n:CH * (n + 1)], [ROWS, CH, D])
                after(dve.tensor_tensor(mg[:, :, :], steps, v["dre"][:, :].unsqueeze(1)
                                        .broadcast_to([ROWS, CH, D]), M))
                after(dve.tensor_tensor(th[:, :, :], steps, v["dim"][:, :].unsqueeze(1)
                                        .broadcast_to([ROWS, CH, D]), M))
                reduce_angle(th[:, :, :], kk[:, :, :])
                if n < NCA:
                    cosine_angle(arg[re, :, :], th[re, :, :])
                    after(dve.tensor_copy(arg[im, :, :], th[im, :, :]))
                else:
                    after(dve.tensor_copy(arg[:, :, :], th[:, :, :]))
                    cosine_angle(cz[:, :, :], th[:, :, :])
                dve.sem_inc(ask, 1)
                got += 2 if n < NCA else 3
                dve.wait_ge(ans, got)
                if n < NCA:
                    after(dve.tensor_tensor(q[:, :, :, CH * n:CH * (n + 1)].rearrange("r g j a -> r a j g"),
                                            mg[:, :, :].rearrange("r a (j g) -> r a j g", j=4),
                                            arg[:, :, :].rearrange("r a (j g) -> r a j g", j=4), M))
                else:
                    after(dve.tensor_tensor(cz[:, :, :], cz[:, :, :], v["al"][:, :].unsqueeze(1)
                                            .broadcast_to([ROWS, CH, D]), M))
                    after(dve.tensor_tensor(arg[:, :, :], arg[:, :, :], v["be"][:, :].unsqueeze(1)
                                            .broadcast_to([ROWS, CH, D]), M))
                    after(dve.tensor_tensor(cz[:, :, :], cz[:, :, :], arg[:, :, :], A_))
                    after(dve.tensor_tensor(pz[:, CH * (n - NCA):CH * (n - NCA + 1), :], mg[:, :, :],
                                            cz[:, :, :], M))
            dve.sem_inc(tables_done, 1)
            for k in range(8):
                dve.wait_ge(products, k + 1)
                for j in range(4):
                    rows = slice(32 * j, 32 * j + 32)
                    ins = dve.tensor_copy(kl[rows, :, 8 * k:8 * k + 8],
                                          kp[rows, k, :, LB * j:LB * (j + 1)].rearrange("p g b -> p b g"))
                ins.then_inc(gathered, 1)
            dve.wait_ge(loaded, 16)
            dve.tensor_tensor(kt[0:1, 0, :], kt[0:1, 0, :], drow[:, :], A_).then_inc(row_done, 1)
            dve.wait_ge(spectra, HALF)
            for m in range(HALF):
                kr, ki = kp[:, m, 0:4, :].rearrange("p a b -> p (a b)"), kp[:, m, 4:8, :].rearrange("p a b -> p (a b)")
                dve.tensor_copy(ka[:, m, 0, :], kr)
                dve.tensor_copy(ka[:, m, 1, :], ki)
                dve.tensor_scalar(kb[:, m, 0, :], ki, -1.0, None, M)
                after(dve.tensor_copy(kb[:, m, 1, :], kr))
            first = kp[0:1, 0, 4:8, :].rearrange("p a b -> p (a b)")
            dve.tensor_scalar(ka[0:1, 0, 1, :], first, 0.0, None, M)
            dve.tensor_scalar(kb[0:1, 0, 0, :], first, 0.0, None, M)
            after(dve.tensor_copy(kb[0:1, 0, 1, :], first))

        @block.tensor
        def _(pe):
            pe.wait_ge(tables_done, 1)
            qv = q[:, :, :, :].rearrange("r g j a -> r g (j a)")
            pv = pz[:, :, :].rearrange("r b (j g) -> r g j b", j=4)
            for k in range(8):
                for i in range(8):
                    grp = 8 * k + i
                    mm = pe.matmul(kp[:, k, i, :], qv[:, grp, :], pv[:, grp, :, :], start=True, stop=True)
                mm.then_inc(products, 1)
            pe.wait_ge(row_done, 1)
            pe.wait_ge(mats_in, 2 * 16)
            pe.wait_ge(gathered, 8)
            for m in range(HALF):
                for part in range(2):
                    f = (part * HALF + m) * P
                    for j in range(NJ):
                        mm = pe.matmul(kp[:, m, 4 * part:4 * part + 4, :], fwd[:, j, f:f + P], kt[:, j, :],
                                       start=(j == 0), stop=(j == NJ - 1))
                mm.then_inc(spectra, 1)


def low_rank_stage(nc, w, resid, ident, out):
    TURNS = B
    NFT = FF // P
    with ExitStack() as ctx:
        def sb(name, shape, dt=F32):
            return ctx.enter_context(nc.sbuf_tensor(name, shape, dt))

        def sem(name):
            return ctx.enter_context(nc.semaphore(name))

        norm = Norm(ctx, nc, "f")
        u1 = sb("u1", [P, ND, RANK])
        v1 = sb("f_v1", [RANK, FF])
        b1 = sb("b1", [P, NFT])
        u2 = sb("u2", [P, NFT, RANK])
        v2 = sb("v2", [RANK + 1, D])
        XT = sb("f_XT", [P, ND, S])
        PT = sb("PT", [RANK, S])
        H = sb("H", [P, NFT, S])
        QT = sb("QT", [RANK + 1, S])
        y = sb("f_y", [P, NJ, D])

        xb = ctx.enter_context(nc.psum_tensor("f_xps", [P, 2, BANK], F32))
        hb = ctx.enter_context(nc.psum_tensor("f_hps", [P, 2, BANK], F32))
        rb = ctx.enter_context(nc.psum_tensor("f_r", [P, 2, BANK], F32))
        yb = ctx.enter_context(nc.psum_tensor("f_y_out", [P, 2, BANK], F32))
        x_h = [Handoff(ctx, nc, f"f_x{k}") for k in range(2)]
        h_h = [Handoff(ctx, nc, f"f_h{k}", range(k, NFT, 2)) for k in range(2)]
        r_h = [Handoff(ctx, nc, f"f_r{k}") for k in range(2)]
        y_h = [Handoff(ctx, nc, f"f_yb{k}") for k in range(2)]
        weights_in = sem("f_weights_in")
        ones_done = sem("f_ones_done")
        vec = sem("f_vector_order")
        stored = sem("f_stored")
        block = ctx.enter_context(nc.Block())

        @block.sync
        def _(sp):
            for h in (*x_h, *h_h, *r_h, *y_h):
                h.open(sp)
            sp.sem_inc(stored, 1)
            sp.dma_start(u1[:, :, :], w["U1"].rearrange("(c p) r -> p c r", p=P)).then_inc(weights_in, 16)
            sp.dma_start(v1[:, :], w["V1"]).then_inc(weights_in, 16)
            sp.dma_start(b1[:, :], w["fb1"]).then_inc(weights_in, 16)
            sp.dma_start(u2[:, :, :], w["U2"].rearrange("(c p) r -> p c r", p=P)).then_inc(weights_in, 16)
            sp.dma_start(v2[:, :], w["V2"]).then_inc(weights_in, 16)
            with sp.Fori(0, TURNS) as t:
                for k in range(2):
                    y_h[k].wait_emptied(sp, t)
                sp.dma_start(out[t].rearrange("(j p) d -> p j d", p=P), y[:, :, :]).then_inc(stored, 16)
            sp.wait_ge(stored, TURNS * 16 + 1)

        @block.gpsimd
        def _(pool):
            pool.memset(QT[RANK:RANK + 1, :], 1.0).then_inc(ones_done, 1)
            pool.wait_ge(ones_done, 1)
            norm.pool_constants(pool)
            with pool.Fori(0, TURNS) as t:
                norm.pool_root(pool, t)

        @block.scalar
        def _(act):
            act.wait_ge(weights_in, 5 * 16)
            act.preload_act_table_set("gelu_apprx_tanh_and_others")
            with act.Fori(0, TURNS) as t:
                for c in range(ND):
                    x_h[c].wait_full(act, t)
                    act.activation(XT[:, c, :], xb[:, c, :], ACT.Copy).then_inc(x_h[c].free, 1)
                r_h[0].wait_full(act, t)
                act.activation(PT[:, :], rb[0:RANK, 0, :], ACT.Copy).then_inc(r_h[0].free, 1)
                for f in range(NFT):
                    h_h[f % 2].wait_full(act, t, f)
                    act.activation(H[:, f, :], hb[:, f % 2, :], ACT.Gelu_apprx_tanh, bias=b1[:, f:f + 1])\
                       .then_inc(h_h[f % 2].free, 1)
                r_h[1].wait_full(act, t)
                act.activation(QT[0:RANK, :], rb[0:RANK, 1, :], ACT.Copy).then_inc(r_h[1].free, 1)

        @block.vector
        def _(dve):
            def normalise(u):
                order = Chain(vec, Norm.DVE_STEPS)
                norm.vector_statistics(dve, u, lambda ins: order(dve, u, ins), resid)
                norm.vector_scale(dve, u, resid)
                order.close()

            def body(t, u):
                if u is not None:
                    x_h[1].wait_emptied(dve, t)
                    normalise(u)
                dve.wait_ge(stored, t * 16 + 1)
                for k in range(2):
                    y_h[k].wait_full(dve, t)
                    dve.tensor_tensor(y[:, 2 * k:2 * k + 2, :], resid[:, bass.ds(t * NJ + 2 * k, 2), :],
                                      yb[:, k, :].rearrange("p (j d) -> p j d", j=2), ALU.add)\
                        .then_inc(y_h[k].free, 1)

            ahead(dve, TURNS, normalise, body)

        @block.tensor
        def _(pe):
            pe.wait_ge(weights_in, 5 * 16)
            pe.wait_ge(ones_done, 1)
            with pe.Fori(0, TURNS) as t:
                pe.wait_ge(norm.x_done, t * NJ + NJ)
                for c in range(ND):
                    x_h[c].wait_free(pe, t)
                    transpose_sequence(pe, xb[:, c, :], norm.x, c, ident).then_inc(x_h[c].full, 1)
                for c in range(ND):
                    x_h[c].wait_emptied(pe, t)
                r_h[0].wait_free(pe, t)
                for c in range(ND):
                    mm = pe.matmul(rb[0:RANK, 0, :], u1[:, c, :], XT[:, c, :], start=(c == 0), stop=(c == ND - 1))
                mm.then_inc(r_h[0].full, 1)
                r_h[0].wait_emptied(pe, t)
                for f in range(NFT):
                    h_h[f % 2].wait_free(pe, t, f)
                    pe.matmul(hb[:, f % 2, :], v1[:, f * P:(f + 1) * P], PT[:, :], start=True, stop=True)\
                      .then_inc(h_h[f % 2].full, 1)
                r_h[1].wait_free(pe, t)
                for f in range(NFT):
                    h_h[f % 2].wait_emptied(pe, t, f)
                    mm = pe.matmul(rb[0:RANK, 1, :], u2[:, f, :], H[:, f, :], start=(f == 0), stop=(f == NFT - 1))
                mm.then_inc(r_h[1].full, 1)
                r_h[1].wait_emptied(pe, t)
                for k in range(2):
                    y_h[k].wait_free(pe, t)
                    for j in range(2):
                        mm = pe.matmul(yb[:, k, j * D:(j + 1) * D], QT[:, (2 * k + j) * P:(2 * k + j + 1) * P],
                                       v2[:, :], start=True, stop=True)
                    mm.then_inc(y_h[k].full, 1)


def identity_into(nc, ident):
    with ExitStack() as ctx:
        made = ctx.enter_context(nc.semaphore("ident_made"))
        block = ctx.enter_context(nc.Block())

        @block.gpsimd
        def _(pool):
            pool.memset(ident[:, :], 0.0).then_inc(made, 1)
            pool.wait_ge(made, 1)
            pool.affine_select(out=ident[:, :], in_=ident[:, :], compare_op=ALU.not_equal, fill=1.0,
                               base=0, pattern=[[-1, P]], channel_multiplier=1).then_inc(made, 1)
            pool.wait_ge(made, 2)


def tower(nc, w, out):
    with ExitStack() as ctx:
        resid = ctx.enter_context(nc.sbuf_tensor("resid", [P, NT, D], F32))
        ident = ctx.enter_context(nc.sbuf_tensor("ident", [P, P], F32))
        identity_into(nc, ident)
        attention_stage(nc, w, resid, ident)
        delta_stage(nc, w, resid, ident)
        experts_stage(nc, w, resid, ident)
        convolution_stage(nc, w, resid, ident)
        low_rank_stage(nc, w, resid, ident, out)


def layout(i):
    c = np.ascontiguousarray
    w = {}
    w["x"] = c(i["x"].reshape(B, S, D))
    w["wqkvT"] = c(i["L0_tok_w_qkv"].reshape(NH, 3, HD, D).transpose(3, 1, 0, 2).reshape(D, 3 * D))
    b = i["L0_tok_b_qkv"].reshape(NH, 3, HD).transpose(1, 0, 2).reshape(3, D)
    w["bqk"] = c(b[0:2].reshape(4, P).T)
    w["bv"] = c(b[2:3])
    w["woutT"] = c(i["L0_tok_w_out"].T)
    w["bo"] = c(i["L0_tok_b_out"].reshape(1, D))
    w.update(attention_constants())
    for name in ("Wq", "Wk", "Wv", "Wg", "Wo"):
        w[name] = c(i["L0_attn_" + name])
    w["wab"] = c(np.concatenate([i["L0_attn_Wb"], i["L0_attn_Wa"]], axis=1))
    w["Wfc"], w["Wproj"] = c(i["L0_attn_W_fc"]), c(i["L0_attn_W_proj"])
    w["dtb"], w["alog"], w["onw"] = (c(i["L0_attn_" + n][None]) for n in ("dt_bias", "A_log", "o_norm_w"))
    w.update(delta_constants())
    w["gw"], w["gb"] = c(i["L0_ffn_gate_w"].T), c(i["L0_ffn_gate_b"][None])
    at = np.arange(NE)
    w["before"] = (at[None, :] < at[:, None]).astype(np.float32).reshape(1, NE * NE)
    w1 = np.concatenate([i["L0_ffn_w1"], i["L0_ffn_sw1"][None]])
    w3 = np.concatenate([i["L0_ffn_w3"], i["L0_ffn_sw3"][None]])
    w13 = np.stack([w1, w3], axis=1)
    w["w13"] = c(w13.reshape(NE + 1, 2, ND, P, EH).transpose(0, 3, 1, 2, 4))
    b1 = np.concatenate([i["L0_ffn_b1"], i["L0_ffn_sb1"][None]])
    b3 = np.concatenate([i["L0_ffn_b3"], i["L0_ffn_sb3"][None]])
    b13 = np.zeros((NE + 1, 2, 3 * P), np.float32)
    b13[:, :, :EH] = np.stack([b1, b3], axis=1)
    w["b13"] = c(b13.reshape(NE + 1, 2, 3, P).transpose(3, 0, 1, 2))
    w2 = np.concatenate([i["L0_ffn_w2"], i["L0_ffn_sw2"][None]])
    b2 = np.concatenate([i["L0_ffn_b2"], i["L0_ffn_sb2"][None]])
    w["w2a"] = c(w2[:, :2 * P].reshape(NE + 1, 2, P, D).transpose(0, 2, 1, 3))
    w["w2b"] = c(np.concatenate([w2[:, 2 * P:], b2[:, None]], axis=1))
    w["log_dt"] = c(i["L1_attn_log_dt"][None])
    w["modes"] = c(np.stack([i["L1_attn_log_A_real"].T, i["L1_attn_A_imag"].T,
                             i["L1_attn_C"][:, :, 0].T, i["L1_attn_C"][:, :, 1].T], axis=1))
    w["skip"] = c(i["L1_attn_D"][None])
    w.update(fourier_constants())
    w["U1"], w["V1"], w["U2"] = c(i["L1_ffn_U1"]), c(i["L1_ffn_V1"]), c(i["L1_ffn_U2"])
    w["fb1"] = c(i["L1_ffn_b1"].reshape(FF // P, P).T)
    w["V2"] = c(np.concatenate([i["L1_ffn_V2"], i["L1_ffn_b2"][None]]))
    return w


def fourier_constants():
    l, f = np.arange(S)[:, None], np.arange(S)[None, :]
    angle = 2 * np.pi * (l * f % NF) / NF
    alternating = (-1.0) ** np.arange(S)
    fwd = np.concatenate([np.cos(angle), -np.sin(angle)], axis=1)
    fwd[:, S] = alternating
    weight = np.where(np.arange(S) == 0, 1.0, 2.0)[:, None] / NF
    inv = np.concatenate([weight * np.cos(angle.T), -weight * np.sin(angle.T)])
    inv[S] = alternating / NF
    return {"fwd": fwd.astype(np.float32), "inv": inv.astype(np.float32),
            "lvals": np.concatenate([16 * np.arange(32), np.arange(16)]).astype(np.float32)[None]}


def delta_constants():
    at = np.arange(P)
    level = np.zeros((P, 7, P), np.float32)
    for l in range(7):
        m = 1 << l
        under = (at[:, None] // (2 * m) == at // (2 * m)) & (at[:, None] // m % 2 == 1) & (at // m % 2 == 0)
        level[:, l, :] = under.T if l == 0 else under
    return {
        "upto": (at[:, None] <= at).astype(np.float32),
        "beyond": (at[:, None] > at).astype(np.float32),
        "ones": np.ones((P, P), np.float32),
        "level": level,
        "keep": (np.arange(NT) % NJ != 0).astype(np.float32)[None],
    }


def attention_constants():
    sel = np.zeros((P, 4, 4, P), np.float32)
    for kind, starts in enumerate(((0, 16), (32,), (0, 32), (16,))):
        for start in starts:
            for head in range(2):
                for e in range(HD):
                    for pair in range(4):
                        sel[32 * pair + head * HD + e, pair, kind, 64 * head + start + e] = 1.0
    selm = np.zeros((NH, 2, NH // 2, P), np.float32)
    onerow = np.zeros((P, 1), np.float32)
    for h in range(NH):
        for part in range(2):
            selm[h, part, h // 2, 64 * (h % 2) + 48 + part] = -1.0
            onerow[64 * (h % 2) + 48 + part] = 1.0
    return {"sel": sel, "selm": selm, "onerow": onerow}


def kernel(**inputs):
    from concourse.bacc import Bacc
    from concourse.bass_utils import run_bass_kernel_spmd

    nc = Bacc("TRN2", target_bir_lowering=False, num_devices=1)
    arrays = layout({k: np.asarray(v) for k, v in inputs.items()})
    w = {}
    for name, a in arrays.items():
        w[name] = nc.dram_tensor("in_" + name, a.shape, mybir.dt.from_np(a.dtype), kind="ExternalInput").ap()
    out = nc.dram_tensor("out", (B, S, D), F32, kind="ExternalOutput").ap()
    tower(nc, w, out)
    result = run_bass_kernel_spmd(nc, [{"in_" + k: a for k, a in arrays.items()}], core_ids=[0])
    return result.results[0]["out"]
```

```python
from contextlib import ExitStack

import numpy as np

import concourse.bass as bass
from concourse import mybir

F32 = mybir.dt.float32
F32R = mybir.dt.float32r
ACT = mybir.ActivationFunctionType
ALU = mybir.AluOpType
AXX = mybir.AxisListType.X

P = 128
B = 8
S = 512
D = 256
NJ = S // P
NT = B * NJ
ND = D // P
BANK = 512

NH, HD = 16, 16
GH, DK = 8, 128
GD = GH * DK
FF = 1024
NE, TOPK, EH = 8, 2, 352
RANK = 64
MODES = 32
NF = 2 * S
LN_EPS, RMS_EPS = 1e-5, 1e-6


class Handoff:

    def __init__(self, ctx, nc, name, uses=("x",), depth=1):
        self.depth = depth
        self.full = ctx.enter_context(nc.semaphore(name + "_full"))
        self.free = ctx.enter_context(nc.semaphore(name + "_free"))
        self.at = {u: k for k, u in enumerate(uses)}
        self.n = len(self.at)

    def open(self, eng):
        eng.sem_inc(self.free, self.depth)

    def wait_full(self, eng, turn, use="x"):
        eng.wait_ge(self.full, turn * self.n + (self.at[use] + 1))

    def wait_free(self, eng, turn, use="x"):
        eng.wait_ge(self.free, turn * self.n + (self.at[use] + 1))

    def wait_emptied(self, eng, turn, use="x"):
        eng.wait_ge(self.free, turn * self.n + (self.at[use] + 1 + self.depth))


class Chain:

    def __init__(self, sem, per):
        self.sem, self.per, self.k = sem, per, 0

    def __call__(self, eng, turn, ins):
        self.k += 1
        ins.then_inc(self.sem, 1)
        eng.wait_ge(self.sem, turn * self.per + self.k)

    def close(self):
        assert self.k == self.per, (self.k, self.per)


def bcast(ap, shape):
    while len(ap.shape) < len(shape):
        ap = ap.unsqueeze(len(ap.shape))
    return ap.broadcast_to(shape)


class Norm:

    STEPS = 4

    def __init__(self, ctx, nc, minus_half):
        def sb(n, shape):
            return ctx.enter_context(nc.sbuf_tensor("norm_" + n, shape, F32))

        self.x = sb("x", [P, NJ, D])
        self.stats, self.both = sb("stats", [P, NJ, 6]), sb("both", [P, NJ, 3])
        self.diff, self.mean = sb("diff", [P, NJ]), sb("mean", [P, NJ])
        self.var, self.rstd = sb("var", [P, NJ]), sb("rstd", [P, NJ])
        self.minus_half = minus_half[:, 0, 0:NJ]
        self.order = ctx.enter_context(nc.semaphore("norm_vector_order"))
        self.var_done = ctx.enter_context(nc.semaphore("norm_var_done"))
        self.rstd_done = ctx.enter_context(nc.semaphore("norm_rstd_done"))
        self.x_done = ctx.enter_context(nc.semaphore("norm_x_done"))
        self.before = -B

    def next_stage(self):
        self.before += B

    def vector(self, dve, turn, resid):
        def rows(j):
            return resid[:, bass.ds(turn * NJ + j, 1), :].rearrange("p a d -> p (a d)")

        n = turn + self.before
        chain = Chain(self.order, self.STEPS)
        for j in range(NJ):
            ins = dve.bn_stats(self.stats[:, j, :], rows(j))
        chain(dve, n, ins)
        chain(dve, n, dve.tensor_reduce(self.both[:, :, :], self.stats[:, :, :].rearrange("p j (a b) -> p j b a", a=2),
                                        AXX, ALU.add))
        dve.tensor_scalar(self.mean[:, :], self.both[:, :, 1], 0.5, None, ALU.mult)
        chain(dve, n, dve.tensor_tensor(self.diff[:, :], self.stats[:, :, 1], self.stats[:, :, 4], ALU.subtract))
        dve.tensor_scalar(self.var[:, :], self.both[:, :, 2], 1.0 / D, LN_EPS, ALU.mult, ALU.add)
        chain(dve, n, dve.tensor_tensor(self.diff[:, :], self.diff[:, :], self.diff[:, :], ALU.mult))
        dve.scalar_tensor_tensor(out=self.var[:, :], in0=self.diff[:, :], scalar=0.25, in1=self.var[:, :],
                                 op0=ALU.mult, op1=ALU.add).then_inc(self.var_done, 1)
        dve.wait_ge(self.rstd_done, n + 1)
        for j in range(NJ):
            dve.tensor_scalar(self.x[:, j, :], rows(j), self.mean[:, j:j + 1], self.rstd[:, j:j + 1],
                              ALU.subtract, ALU.mult).then_inc(self.x_done, 1)
        chain.close()

    def pool_root(self, pool, turn):
        pool.wait_ge(self.var_done, turn + (self.before + 1))
        pool.tensor_tensor(self.rstd[:, :], self.var[:, :], self.minus_half, ALU.pow).then_inc(self.rstd_done, 1)

    def wait(self, eng, turn):
        eng.wait_ge(self.x_done, turn * NJ + (self.before + 1) * NJ)


def transpose_sequence(pe, out, x, c, ident):
    for j in range(NJ):
        mm = pe.transpose(out[:, j * P:(j + 1) * P], x[:, j, c * P:(c + 1) * P], ident[:, :])
    return mm


def ahead(eng, count, first, body):
    if first is not None:
        first(0)
    with eng.Fori(0, count - 1) as t:
        body(t, t + 1)
    body(count - 1, None)


def attention_stage(nc, w, ident, result):
    TURNS = B
    PAIRS = NH // 2
    QUADS = NH // 4
    SKEW = P + HD
    with ExitStack() as ctx:
        def sb(name, shape, dt=F32):
            return ctx.enter_context(nc.sbuf_tensor(name, shape, dt))

        def sem(name):
            return ctx.enter_context(nc.semaphore(name))

        wqkv = sb("wqkv", [P, ND, 3 * D])
        wout = sb("wout", [P, ND, D])
        bqk = sb("bqk", [P, 4])
        bv = sb("bv", [P, D])
        bo = sb("bo", [P, D])
        sel32 = sb("sel32", [P, 4, 4, P])
        sel = sb("sel", [P, 4, 4, P], F32R)
        selm32 = sb("selm32", [2, 2, P])
        selm = sb("selm", [2, 2, P], F32R)
        onerow = sb("onerow", [P, 1])

        x_in = sb("x_in", [P, NJ, D])
        xT = sb("xT", [P, ND, S])
        qk32 = sb("qk32", [P, 4, S])
        qk_hi = sb("qk_hi", [P, 4, S], F32R)
        qk_lo = sb("qk_lo", [P, 4, S], F32R)
        vpad = sb("vpad", [P, NJ, QUADS, 4, SKEW])
        qstack = sb("qstack", [P, PAIRS, S], F32R)
        kstack = sb("kstack", [P, PAIRS, S], F32R)
        maxima = sb("maxima", [P, NJ, NH])
        max_hi = sb("max_hi", [2, S], F32R)
        max_lo = sb("max_lo", [2, S], F32R)
        probs = sb("probs", [P, 2, NJ, S])
        rsum = sb("rsum", [P, S])
        valsT = sb("valsT", [P, ND, S])
        y = sb("a_y", [P, NJ, D])

        scores = ctx.enter_context(nc.psum_tensor("scores", [P, 2, BANK], F32))
        scoresT = ctx.enter_context(nc.psum_tensor("scoresT", [P, 2, BANK], F32))
        heads_out = ctx.enter_context(nc.psum_tensor("heads_out", [P, 2, BANK], F32))
        work = ctx.enter_context(nc.psum_tensor("work", [P, 2, BANK], F32))

        weights_in = sem("a_weights_in")
        consts_done = sem("a_consts_done")
        x_loaded = sem("x_loaded")
        x_used = sem("x_used")
        qk_hi_done = sem("qk_hi_done")
        qk_lo_done = sem("qk_lo_done")
        own = sem("a_vector_order")
        probs_used = sem("probs_used")
        stored = sem("a_stored")
        even, odd = ["xT0", "qk0", "qk2", "v0"], ["xT1", "qk1", "qk3", "v1"]
        for p in range(PAIRS + 1):
            even += ([f"k{p}"] if p < PAIRS else []) + ([f"max{p - 1}"] if p >= 1 else [])
            odd += ([f"q{p}"] if p < PAIRS else []) + ([f"m{p - 1}"] if p >= 1 else [])
        bank = [Handoff(ctx, nc, "work0", even + ["out0"]), Handoff(ctx, nc, "work1", odd + ["out1"])]
        units = [(h, t) for h in range(NH) for t in range(NJ)]
        score = [Handoff(ctx, nc, f"score{k}", units[k::2]) for k in range(2)]
        scoreT = [Handoff(ctx, nc, f"scoreT{k}", units[k::2]) for k in range(2)]
        head = [Handoff(ctx, nc, f"head{k}", range(k, QUADS, 2)) for k in range(2)]

        def window(t, h):
            return vpad[:, t, h // 4, :, :].rearrange("p i e -> p (i e)")[:, (h % 4) * P:(h % 4 + 1) * P]

        def value_rows(quad):
            return 64 * (quad % 2)

        block = ctx.enter_context(nc.Block())

        @block.sync
        def _(sp):
            for h in (*bank, *score, *scoreT, *head):
                h.open(sp)
            sp.sem_inc(x_used, 1)
            sp.sem_inc(stored, 1)
            sp.dma_start(wqkv[:, :, :], w["wqkvT"].rearrange("(c p) n -> p c n", p=P)).then_inc(weights_in, 16)
            sp.dma_start(sel32[:, :, :, :], w["sel"]).then_inc(weights_in, 16)
            sp.dma_start(bqk[:, :], w["bqk"]).then_inc(weights_in, 16)
            sp.dma_start(bv[:, :], w["bv"].partition_broadcast(P)).then_inc(weights_in, 16)
            sp.dma_start(onerow[:, :], w["onerow"]).then_inc(weights_in, 16)
            sp.dma_start(selm32[:, :, :], w["selm"]).then_inc(weights_in, 16)
            sp.dma_start(wout[:, :, :], w["woutT"].rearrange("(c p) n -> p c n", p=P)).then_inc(weights_in, 16)
            sp.dma_start(bo[:, :], w["bo"].partition_broadcast(P)).then_inc(weights_in, 16)
            with sp.Fori(0, TURNS) as b:
                sp.wait_ge(x_used, b + 1)
                sp.dma_start(x_in[:, :, :], w["x"][b].rearrange("(j p) d -> p j d", p=P)).then_inc(x_loaded, 16)

        @block.gpsimd
        def _(pool):
            pool.memset(vpad[:, :, :, :, :], 0.0).then_inc(consts_done, 1)
            pool.wait_ge(consts_done, 1)
            for g in range(QUADS):
                ones = 64 - value_rows(g)
                pool.memset(vpad[:, :, g, :, ones:ones + HD], 1.0).then_inc(consts_done, 1)
            pool.wait_ge(weights_in, 8 * 16)
            pool.tensor_copy(sel[:, :, :, :], sel32[:, :, :, :]).then_inc(consts_done, 1)
            pool.tensor_copy(selm[:, :, :], selm32[:, :, :]).then_inc(consts_done, 1)

        @block.scalar
        def _(act):
            act.preload_act_table_set("exp_and_others")
            act.wait_ge(weights_in, 8 * 16)
            with act.Fori(0, TURNS) as b:
                for c in range(ND):
                    bank[c].wait_full(act, b, f"xT{c}")
                    act.activation(xT[:, c, :], work[:, c, :], ACT.Copy).then_inc(bank[c].free, 1)
                for m in range(4):
                    bank[m % 2].wait_emptied(act, b, f"qk{m}")
                    act.activation(qk_hi[:, m, :], qk32[:, m, :], ACT.Copy).then_inc(qk_hi_done, 1)
                def stack_k(p):
                    bank[0].wait_full(act, b, f"k{p}")
                    act.activation(kstack[:, p, :], work[:, 0, :], ACT.Identity, bias=onerow[:, 0:1])\
                       .then_inc(bank[0].free, 1)

                stack_k(0)
                for s in range(PAIRS + 2):
                    for i in range(2 * NJ):
                        if i == 2 and 1 <= s <= PAIRS:
                            bank[1].wait_full(act, b, f"m{s - 1}")
                            act.activation(qstack[:, s - 1, :], work[:, 1, :], ACT.Copy).then_inc(bank[1].free, 1)
                        if i == 5 and s + 1 < PAIRS:
                            stack_k(s + 1)
                        if s >= 2:
                            h, t = 2 * (s - 2) + i // NJ, i % NJ
                            scoreT[t % 2].wait_full(act, b, (h, t))
                            if t == 0 and h >= 2:
                                act.wait_ge(probs_used, b * NH + (h - 1))
                            act.activation(probs[:, h % 2, t, :], scoresT[:, t % 2, :], ACT.Exp)\
                               .then_inc(scoreT[t % 2].free, 1)
                for c in range(2):
                    bank[c].wait_emptied(act, b, f"out{c}")
                act.dma_start(result[b].rearrange("(j p) d -> p j d", p=P), y[:, :, :]).then_inc(stored, 16)
            act.wait_ge(stored, B * 16 + 1)

        @block.vector
        def _(dve):
            per = PAIRS + QUADS
            dve.wait_ge(weights_in, 8 * 16)
            dve.wait_ge(consts_done, 3 + QUADS)
            with dve.Fori(0, TURNS) as b:
                after = Chain(own, per)

                def cut(m):
                    dve.wait_ge(qk_hi_done, b * 4 + (m + 1))
                    dve.tensor_tensor(qk_lo[:, m, :], qk32[:, m, :], qk_hi[:, m, :].bitcast(F32), ALU.subtract)\
                       .then_inc(qk_lo_done, 1)

                for m in range(4):
                    k = m % 2
                    bank[k].wait_full(dve, b, f"qk{m}")
                    dve.tensor_scalar(qk32[:, m, :], work[:, k, :], bqk[:, m:m + 1], 0.25 if m < 2 else 1.0,
                                      ALU.add, ALU.mult).then_inc(bank[k].free, 1)
                    if m > 0:
                        cut(m - 1)
                cut(3)
                for c in range(2):
                    bank[c].wait_full(dve, b, f"v{c}")
                    for g in range(QUADS):
                        at = value_rows(g)
                        ins = dve.tensor_tensor(
                            vpad[:, 2 * c:2 * c + 2, g, :, at:at + HD],
                            work[:, c, :].rearrange("p (j g i e) -> p j g i e", j=2, g=QUADS, i=4)[:, :, g, :, :],
                            bv[:, :].rearrange("p (g i e) -> p g i e", g=QUADS, i=4)[:, g, :, :].unsqueeze(1)
                            .broadcast_to([P, 2, 4, HD]), ALU.add)
                    ins.then_inc(bank[c].free, 1)

                def stack_q(p):
                    bank[1].wait_full(dve, b, f"q{p}")
                    dve.tensor_copy(qstack[:, p, :], work[:, 1, :]).then_inc(bank[1].free, 1)

                def normalise(g):
                    k, at = g % 2, value_rows(g)
                    rows, sums = slice(at, at + 64), slice(64 - at, 128 - at)
                    head[k].wait_full(dve, b, g)
                    after(dve, b, dve.reciprocal(rsum[rows, :], heads_out[sums, k, :]))
                    dve.tensor_tensor(valsT[rows, g // 2, :], heads_out[rows, k, :], rsum[rows, :], ALU.mult)\
                       .then_inc(head[k].free, 1)

                stack_q(0)
                for s in range(PAIRS + 2):
                    if 1 <= s <= PAIRS:
                        bank[0].wait_full(dve, b, f"max{s - 1}")
                        after(dve, b, dve.tensor_copy(max_hi[:, :], work[0:2, 0, :]))
                        dve.tensor_tensor(max_lo[:, :], work[0:2, 0, :], max_hi[:, :].bitcast(F32), ALU.subtract)\
                           .then_inc(bank[0].free, 1)
                    for i in range(2 * NJ):
                        if i == 5 and s + 1 < PAIRS:
                            stack_q(s + 1)
                        if s < PAIRS:
                            h, t = 2 * s + i // NJ, i % NJ
                            score[t % 2].wait_full(dve, b, (h, t))
                            dve.tensor_reduce(maxima[:, t, h:h + 1], scores[:, t % 2, :], AXX, ALU.max)\
                               .then_inc(score[t % 2].free, 1)
                        if i == NJ - 1 and s >= 4 and s % 2 == 0:
                            normalise((s - 4) // 2)
                normalise(QUADS - 1)
                dve.wait_ge(stored, b * 16 + 1)
                for c in range(2):
                    bank[c].wait_full(dve, b, f"out{c}")
                    dve.tensor_tensor(y[:, 2 * c:2 * c + 2, :],
                                      work[:, c, :].rearrange("p (j d) -> p j d", j=2),
                                      bo[:, :].unsqueeze(1).broadcast_to([P, 2, D]), ALU.add)\
                       .then_inc(bank[c].free, 1)
                after.close()

        @block.tensor
        def _(pe):
            def select(out, kind, part, tile, c, start, stop):
                return pe.matmul(out, sel[:, c, kind, :], part[:, tile, :], start=start, stop=stop)

            pe.wait_ge(weights_in, 8 * 16)
            pe.wait_ge(consts_done, 3 + QUADS)
            with pe.Fori(0, TURNS) as b:
                pe.wait_ge(x_loaded, b * 16 + 16)
                for c in range(ND):
                    bank[c].wait_free(pe, b, f"xT{c}")
                    for j in range(NJ):
                        mm = pe.transpose(work[:, c, j * P:(j + 1) * P], x_in[:, j, c * P:(c + 1) * P], ident[:, :])
                    mm.then_inc(bank[c].full, 1)
                pe.wait_ge(x_loaded, b * 16 + 16)
                for c in range(ND):
                    bank[c].wait_emptied(pe, b, f"xT{c}")
                pe.sem_inc(x_used, 1)
                for m in range(4):
                    k = m % 2
                    bank[k].wait_free(pe, b, f"qk{m}")
                    for c in range(ND):
                        mm = pe.matmul(work[:, k, :], wqkv[:, c, m * P:(m + 1) * P], xT[:, c, :],
                                       start=(c == 0), stop=(c == ND - 1))
                    mm.then_inc(bank[k].full, 1)
                for k in range(2):
                    bank[k].wait_free(pe, b, f"v{k}")
                    for j in range(2):
                        for c in range(ND):
                            mm = pe.matmul(work[:, k, j * D:(j + 1) * D],
                                           xT[:, c, (2 * k + j) * P:(2 * k + j + 1) * P], wqkv[:, c, 2 * D:3 * D],
                                           start=(c == 0), stop=(c == ND - 1))
                    mm.then_inc(bank[k].full, 1)
                def stack(p):
                    m, c = p // 4, p % 4
                    pe.wait_ge(qk_lo_done, b * 4 + (m + 3))
                    for k, kind, name in ((0, 2, "k"), (1, 0, "q")):
                        bank[k].wait_free(pe, b, f"{name}{p}")
                        tile = m + 2 if name == "k" else m
                        select(work[:, k, :], kind, qk_hi, tile, c, True, False)
                        select(work[:, k, :], kind + 1, qk_lo, tile, c, False, True).then_inc(bank[k].full, 1)

                def stack_with_maxima(p):
                    m, c = p // 4, p % 4
                    bank[0].wait_emptied(pe, b, f"max{p}")
                    bank[1].wait_free(pe, b, f"m{p}")
                    select(work[:, 1, :], 0, qk_hi, m, c, True, False)
                    select(work[:, 1, :], 1, qk_lo, m, c, False, False)
                    pe.matmul(work[:, 1, :], selm[:, 0, :], max_hi[:, :], start=False, stop=False)
                    pe.matmul(work[:, 1, :], selm[:, 1, :], max_lo[:, :], start=False, stop=True)\
                      .then_inc(bank[1].full, 1)

                def maxima_of(p):
                    for t in (NJ - 2, NJ - 1):
                        score[t % 2].wait_emptied(pe, b, (2 * p + 1, t))
                    bank[0].wait_free(pe, b, f"max{p}")
                    for j in range(NJ):
                        mm = pe.transpose(work[0:2, 0, j * P:(j + 1) * P], maxima[:, j, 2 * p:2 * p + 2], ident[:, :])
                    mm.then_inc(bank[0].full, 1)

                def scores_of(h, t):
                    p, r = h // 2, 64 * (h % 2)
                    score[t % 2].wait_free(pe, b, (h, t))
                    pe.matmul(scores[:, t % 2, :], qstack[r:r + 64, p, t * P:(t + 1) * P], kstack[r:r + 64, p, :],
                              start=True, stop=True).then_inc(score[t % 2].full, 1)

                def scoresT_of(h, t):
                    p, r = h // 2, 64 * (h % 2)
                    scoreT[t % 2].wait_free(pe, b, (h, t))
                    pe.matmul(scoresT[:, t % 2, :], kstack[r:r + 64, p, t * P:(t + 1) * P], qstack[r:r + 64, p, :],
                              start=True, stop=True).then_inc(scoreT[t % 2].full, 1)

                def values(h, t):
                    g = h // 4
                    scoreT[t % 2].wait_emptied(pe, b, (h, t))
                    if h % 4 == 0 and t == 0:
                        head[g % 2].wait_free(pe, b, g)
                    mm = pe.matmul(heads_out[:, g % 2, :], window(t, h), probs[:, h % 2, t, :],
                                   start=(h % 4 == 0 and t == 0), stop=(h % 4 == 3 and t == NJ - 1))
                    if t == NJ - 1:
                        mm.then_inc(probs_used, 1)
                        if h % 4 == 3:
                            pe.wait_ge(probs_used, b * NH + (h + 1))
                            pe.sem_inc(head[g % 2].full, 1)

                stack(0)
                for s in range(PAIRS + 2):
                    if 1 <= s <= PAIRS:
                        maxima_of(s - 1)
                    if s < PAIRS:
                        bank[0].wait_emptied(pe, b, f"k{s}")
                        bank[1].wait_emptied(pe, b, f"q{s}")
                    for i in range(2 * NJ):
                        if i == 2 and 1 <= s <= PAIRS:
                            stack_with_maxima(s - 1)
                        if i == 5 and s + 1 < PAIRS:
                            stack(s + 1)
                        if s < PAIRS:
                            scores_of(2 * s + i // NJ, i % NJ)
                        if s >= 2:
                            if i == 0:
                                bank[1].wait_emptied(pe, b, f"m{s - 2}")
                            h, t = 2 * (s - 2) + i // NJ, i % NJ
                            scoresT_of(h, t)
                            if h > 0:
                                values(h - 1, t)
                for t in range(NJ):
                    values(NH - 1, t)
                for k in range(2):
                    head[k].wait_emptied(pe, b, QUADS - 2 + k)
                for k in range(2):
                    bank[k].wait_free(pe, b, f"out{k}")
                    for j in range(2):
                        for c in range(ND):
                            mm = pe.matmul(work[:, k, j * D:(j + 1) * D],
                                           valsT[:, c, (2 * k + j) * P:(2 * k + j + 1) * P], wout[:, c, :],
                                           start=(c == 0), stop=(c == ND - 1))
                    mm.then_inc(bank[k].full, 1)


def delta_stage(nc, w, ident, minus_half, source, result):
    TURNS = NT
    LEVELS = 7
    HG = 4
    G = GH // HG
    HW = HG * P
    with ExitStack() as ctx:
        def sb(name, shape, dt=F32):
            return ctx.enter_context(nc.sbuf_tensor(name, shape, dt))

        def sem(name):
            return ctx.enter_context(nc.semaphore(name))

        wq_hi = sb("wq_hi", [P, 4, ND, GD], F32R)
        wq_lo = sb("wq_lo", [P, 4, ND, GD], F32R)
        wab = sb("wab", [P, ND, 2 * GH])
        wo = sb("wo", [P, GH, D])
        wfc = sb("wfc", [P, ND, FF])
        wproj = sb("wproj", [P, FF // P, D])
        dtb = sb("dtb", [P, GH])
        alog = sb("alog", [P, GH])
        expa = sb("expa", [P, GH])
        onw = sb("onw", [P, DK])
        upto = sb("upto", [P, P])
        beyond = sb("beyond", [P, P])
        ones = sb("ones", [P, P])
        level0 = sb("level0", [P, P])
        level = sb("level", [P, LEVELS, P])
        keep = sb("keep", [P, NT])

        stats = sb("stats", [P, 6])
        both = sb("both", [P, 3])
        mv = sb("mv", [P, 2])
        var = sb("var", [P, 4])
        rs = sb("rs", [P, 4])
        Xn = sb("Xn", [P, D])
        X = sb("X", [P, D])
        Rn = sb("Rn", [P, D])
        RT = sb("RT", [P, ND, P])
        RT_hi = sb("RT_hi", [P, ND, P], F32R)
        RT_lo = sb("RT_lo", [P, ND, P], F32R)
        row_next = sb("row_next", [P, D])
        row = sb("row", [P, D])
        row_out = sb("row_out", [P, D])
        M, MT = Rn, RT
        qkvg = sb("qkvg", [P, 4, GH, DK])
        ab = sb("ab", [P, 2 * GH])
        ex = sb("ex", [P, 2 * GH])
        t1 = sb("t1", [P, GH])
        t2 = sb("t2", [P, GH])
        t3 = sb("t3", [P, GH])
        g = sb("g", [P, GH])
        beta = sb("beta", [P, GH])
        eg = sb("eg", [P, 3, GH])
        egk = sb("egk", [P, GH])
        egc = sb("egc", [P, GH])
        nbe = sb("nbe", [P, GH])
        norm = sb("norm", [P, 2, GH])
        rnorm = sb("rnorm", [P, 2, GH])
        gu = sb("gu", [P, GH, P])
        E = sb("E", [P, GH, P])
        nat = sb("nat", [P, 7, GH, DK])
        tra = sb("tra", [P, 5, GH, P])
        sq = tra[:, 0:2]
        sqo = tra[:, 3]
        mp = sb("mp", [P, GH, 2, P])
        T = sb("T", [P, GH, P])
        Y = sb("Y", [P, GH, P])
        Xl = sb("Xl", [P, GH, P])
        R = sb("R", [P, GH, DK])
        U = E
        O = gu
        St = sb("St", [P, GH, DK])
        og = T
        osum = sb("osum", [P, GH])
        ro = sb("ro", [P, GH])
        ogT = Xl
        X2 = sb("X2", [P, D])
        hid, hT = gu, R
        y = sb("y", [P, D])

        front = ctx.enter_context(nc.psum_tensor("g_front", [P, 2, BANK], F32))
        stateb = ctx.enter_context(nc.psum_tensor("g_state", [P, 2, BANK], F32))
        tri = ctx.enter_context(nc.psum_tensor("g_tri", [P, 4, BANK], F32))

        weights_in = sem("g_weights_in")
        late_in = sem("g_late_weights_in")
        vec_front = sem("g_vector_order_front")
        vec = sem("g_vector_order")
        expa_done = sem("g_expa_done")
        cleared = sem("g_cleared")
        row_in = sem("g_row_in")
        row_taken = sem("g_row_taken")
        row_done = sem("g_row_done")
        stored = sem("g_stored")
        wq_hi_done = sem("g_wq_hi_done")
        wq_cut = sem("g_wq_cut")
        rt_cut = sem("g_rt_cut")
        root_f = Handoff(ctx, nc, "g_root_front", ["ln", "rms", "qk"], depth=0)
        root = Handoff(ctx, nc, "g_root", ["o", "rms2"], depth=0)
        gate = Handoff(ctx, nc, "g_gate", depth=0)
        fb = [Handoff(ctx, nc, f"g_front{f}", [("RT", "ab")[f]] + [("proj", n, f) for n in range(4)])
              for f in range(2)]
        place = {}
        tri_uses = [[], [], [], []]

        def uses(bank, *names):
            for name in names:
                place[name] = bank
                tri_uses[bank].append(name)

        TRANSPOSED = (0, 3, 1, 2, 4)
        for k in range(G):
            uses(G + k, ("decay", k))
        for i, n in enumerate(TRANSPOSED):
            for k in range(G):
                uses(G * (i % 2) + k, ("tra", n, k))
        for i in range(4):
            uses((i + G) % 4, ("mp", i))
        for k in range(G):
            uses(k, ("t", 0, k))
            for l in range(1, LEVELS):
                uses(k, ("a", l, k))
                uses(G + k, ("b", l, k), ("t", l, k))
            uses(k, ("ogT", k))
        uses(2, ("mT",))
        uses(3, ("hid", 0))
        uses(0, ("hid", 1))
        tb = [Handoff(ctx, nc, f"g_tri{k}", tri_uses[k]) for k in range(4)]
        sbk = [Handoff(ctx, nc, f"g_state{k}", (["cum"] if k == 0 else []) + ["ks", "u", "o", "s"] +
                       (["wo"] if k == 0 else ["down"])) for k in range(2)]
        squares = sem("g_squares")
        squares_o = sem("g_squares_o")
        pool_gu = sem("g_pool_gu")
        pool_gate = sem("g_pool_gate")
        pool_E = sem("g_pool_E")
        pool_nat = sem("g_pool_nat")
        pool_og = sem("g_pool_og")
        dve_beta = sem("g_beta_done")
        dve_g = sem("g_g_done")
        dve_scal = sem("g_scalars_done")
        dve_nat = sem("g_vector_nat")
        X_done = [sem(f"g_X{k}") for k in range(G)]
        Y_done = [sem(f"g_Y{k}") for k in range(G)]
        og_done = sem("g_og_done")
        rn_done = sem("g_rn_done")
        m_done = sem("g_m_done")
        hid_relu = sem("g_hid_relu")

        block = ctx.enter_context(nc.Block())

        def heads(ap, k):
            return ap[:, HG * k:HG * (k + 1), :]

        def split(bank):
            return bank.rearrange("p (h e) -> p h e", h=HG)

        def grp(ap, k):
            return split(ap[:, k, :])

        def halves(ap, l):
            return ap.rearrange("p h (b two m) -> p h b two m", two=2, m=1 << l)

        def wq_whole(n):
            room = nat[:, 2 * n:2 * n + 2, :, :] if n < 3 else tra[:, 0:2, :, :]
            return room.rearrange("p c h e -> p c (h e)")

        def chunk_of(h, t):
            return h.rearrange("b (j p) d -> (b j) p d", p=P)[bass.ds(t, 1)].rearrange("a p d -> p (a d)")

        def load_store(sp, t, load):
            if load:
                sp.wait_ge(row_taken, t + 1)
                sp.dma_start(row_next[:, :], chunk_of(source, t + 1)).then_inc(row_in, 16)
            sp.wait_ge(row_done, t + 1)
            sp.dma_start(chunk_of(result, t), row_out[:, :]).then_inc(stored, 16)

        def level_zero(eng, t, k):
            for i in (2 * k + 1, 2 * k):
                emptied(eng, t, ("mp", i))
            eng.tensor_tensor(heads(Xl, k), mp[:, HG * k:HG * (k + 1), 0, :],
                              level0[:, :].unsqueeze(1).broadcast_to([P, HG, P]), ALU.mult).then_inc(X_done[k], 1)
            eng.wait_ge(X_done[k], t + 1)
            eng.tensor_tensor(heads(Y, k), ident[:, :].unsqueeze(1).broadcast_to([P, HG, P]),
                              heads(Xl, k), ALU.subtract).then_inc(Y_done[k], 1)

        @block.sync
        def _(sp):
            for h in (*fb, *sbk, *tb):
                h.open(sp)
            sp.sem_inc(stored, 1)
            sp.dma_start(row_next[:, :], chunk_of(source, 0)).then_inc(row_in, 16)
            for n, name in enumerate(("Wq", "Wk", "Wv", "Wg")):
                sp.dma_start(wq_whole(n), w[name].rearrange("(c p) n -> p c n", p=P)).then_inc(weights_in, 16)
            sp.dma_start(wab[:, :, :], w["wab"].rearrange("(c p) n -> p c n", p=P)).then_inc(weights_in, 16)
            sp.dma_start(dtb[:, :], w["dtb"].partition_broadcast(P)).then_inc(weights_in, 16)
            sp.dma_start(alog[:, :], w["alog"].partition_broadcast(P)).then_inc(weights_in, 16)
            sp.dma_start(onw[:, :], w["onw"].partition_broadcast(P)).then_inc(weights_in, 16)
            sp.dma_start(upto[:, :], w["upto"]).then_inc(weights_in, 16)
            sp.dma_start(beyond[:, :], w["beyond"]).then_inc(weights_in, 16)
            sp.dma_start(level[:, :, :], w["level"]).then_inc(weights_in, 16)
            sp.dma_start(level0[:, :], w["level0"]).then_inc(weights_in, 16)
            sp.dma_start(keep[:, :], w["keep"].partition_broadcast(P)).then_inc(weights_in, 16)
            sp.dma_start(ones[:, :], w["ones"]).then_inc(weights_in, 16)
            for to, name in ((wo, "Wo"), (wfc, "Wfc"), (wproj, "Wproj")):
                sp.dma_start(to[:, :, :], w[name].rearrange("(c p) n -> p c n", p=P)).then_inc(late_in, 16)
            with sp.Fori(0, TURNS - 2) as t:
                load_store(sp, t, True)
            load_store(sp, TURNS - 2, True)
            load_store(sp, TURNS - 1, False)
            sp.wait_ge(stored, TURNS * 16 + 1)
        IN = 14 * 16

        def bank_of(eng, t, use, wait):
            k = place[use]
            (tb[k].wait_free if wait == "free" else tb[k].wait_full)(eng, t, use)
            return tri[:, k, :], tb[k]

        def emptied(eng, t, use):
            tb[place[use]].wait_emptied(eng, t, use)

        @block.gpsimd
        def _(pool):
            def inv_root(hand, turn, use, out, x, half):
                hand.wait_full(pool, turn, use)
                pool.tensor_tensor(out, x, half, ALU.pow).then_inc(hand.free, 1)

            def roots_ln(u):
                inv_root(root_f, u, "ln", rs[:, 0:1], var[:, 0:1], minus_half[:, 0, 0:1])
                inv_root(root_f, u, "rms", rs[:, 1:2], var[:, 1:2], minus_half[:, 0, 0:1])

            def front_rest(u):
                pool.wait_ge(dve_g, u + 1)
                pool.tensor_tensor(gu[:, :, :], upto[:, :].unsqueeze(1).broadcast_to([P, GH, P]),
                                   bcast(g[:, :], [P, GH, P]), ALU.mult).then_inc(pool_gu, 1)
                inv_root(root_f, u, "qk", rnorm[:, :, :], norm[:, :, :], minus_half[:, :, :])
                for f in range(2):
                    fb[f].wait_emptied(pool, u, ("proj", 3, f))
                pool.tensor_tensor(qkvg[:, 3, :, :], qkvg[:, 3, :, :],
                                   onw[:, :].unsqueeze(1).broadcast_to([P, GH, DK]), ALU.mult)\
                    .then_inc(pool_gate, 1)

            def first(u):
                roots_ln(u)
                front_rest(u)

            def body(t, u):
                for k in range(G):
                    emptied(pool, t, ("decay", k))
                pool.tensor_tensor(E[:, :, :], E[:, :, :], upto[:, :].unsqueeze(1).broadcast_to([P, GH, P]),
                                   ALU.mult).then_inc(pool_E, 1)
                pool.wait_ge(dve_scal, t + 1)
                pool.wait_ge(dve_nat, t * 5 + 1)
                pool.tensor_tensor(nat[:, 5, :, :], nat[:, 0, :, :], bcast(eg[:, 1, :], [P, GH, DK]),
                                   ALU.mult).then_inc(pool_nat, 1)
                pool.tensor_tensor(nat[:, 6, :, :], qkvg[:, 2, :, :], bcast(beta[:, :], [P, GH, DK]),
                                   ALU.mult).then_inc(pool_nat, 1)
                level_zero(pool, t, 0)
                if u is not None:
                    roots_ln(u)
                for k in range(G):
                    sbk[k].wait_emptied(pool, t, "o")
                pool.wait_ge(pool_gate, t + 1)
                pool.tensor_tensor(og[:, :, :], O[:, :, :], qkvg[:, 3, :, :], ALU.mult).then_inc(pool_og, 1)
                inv_root(root, t, "o", ro[:, :], osum[:, :], minus_half[:, 0, :])
                inv_root(root, t, "rms2", rs[:, 2:3], var[:, 2:3], minus_half[:, 0, 0:1])
                if u is not None:
                    for k in range(2):
                        emptied(pool, t, ("hid", k))
                    front_rest(u)

            pool.wait_ge(weights_in, IN)
            ahead(pool, TURNS, first, body)

        @block.scalar
        def _(act):
            def project(u, n, f):
                fb[f].wait_full(act, u, ("proj", n, f))
                act.activation(qkvg[:, n, HG * f:HG * (f + 1), :], grp(front, f), ACT.Silu).then_inc(fb[f].free, 1)

            def square(u, n):
                for f in range(2):
                    fb[f].wait_emptied(act, u, ("proj", n, f))
                for f in range(2):
                    ins = act.activation(heads(sq[:, n], f), heads(qkvg[:, n], f), ACT.Square)
                ins.then_inc(squares, 1)

            def front_start(u):
                fb[0].wait_full(act, u, "RT")
                for to in (RT_hi, RT):
                    ins = act.activation(to[:, :, :], front[:, 0, 0:D].rearrange("p (c t) -> p c t", c=ND), ACT.Copy)
                ins.then_inc(fb[0].free, 1)
                gate.wait_full(act, u)
                act.activation(ex[:, :], ab[:, :], ACT.Exp).then_inc(gate.free, 1)
                act.preload_act_table_set("silu_and_others")
                project(u, 0, 0)
                project(u, 0, 1)
                project(u, 1, 0)

            def front_middle(u):
                square(u, 0)
                project(u, 1, 1)
                project(u, 2, 0)

            def front_late(u):
                square(u, 1)

            def front_gates(u):
                for f in range(2):
                    project(u, 3, f)

            def first(u):
                front_start(u)
                front_middle(u)
                project(u, 2, 1)
                front_late(u)
                front_gates(u)

            def body(t, u):
                act.preload_act_table_set("exp_and_others")
                sbk[0].wait_full(act, t, "cum")
                act.activation(eg[:, :, :], stateb[:, 0, 0:3 * GH].rearrange("p (a h) -> p a h", a=3), ACT.Exp)\
                   .then_inc(sbk[0].free, 1)
                for k in range(G):
                    bank, h = bank_of(act, t, ("decay", k), "full")
                    act.activation(heads(E, k), split(bank), ACT.Exp).then_inc(h.free, 1)
                for n in TRANSPOSED:
                    bank, h = bank_of(act, t, ("tra", n, 0), "full")
                    act.activation(heads(tra[:, n], 0), split(bank), ACT.Copy).then_inc(h.free, 1)
                for l in range(LEVELS):
                    for k in range(G):
                        bank, h = bank_of(act, t, ("t", l, k), "full")
                        act.activation(heads(T if l == 0 else Y, k), split(bank), ACT.Copy).then_inc(h.free, 1)
                for k in range(G):
                    sbk[k].wait_full(act, t, "u")
                    act.activation(heads(U, k), grp(stateb, k), ACT.Copy).then_inc(sbk[k].free, 1)
                for k in range(G):
                    sbk[k].wait_full(act, t, "o")
                    act.activation(heads(sqo, k), grp(stateb, k), ACT.Square).then_inc(squares_o, 1)
                    act.activation(heads(O, k), grp(stateb, k), ACT.Copy).then_inc(sbk[k].free, 1)
                if u is not None:
                    front_start(u)
                for k in range(G):
                    bank, h = bank_of(act, t, ("ogT", k), "full")
                    act.activation(heads(ogT, k), split(bank), ACT.Copy).then_inc(h.free, 1)
                if u is not None:
                    front_middle(u)
                bank, h = bank_of(act, t, ("mT",), "full")
                act.activation(MT[:, :, :], bank[:, 0:D].rearrange("p (c t) -> p c t", c=ND), ACT.Copy)\
                   .then_inc(h.free, 1)
                if u is not None:
                    project(u, 2, 1)
                for k in range(2):
                    bank, h = bank_of(act, t, ("hid", k), "full")
                    act.activation(heads(hid, k), split(bank), ACT.Relu).then_inc(hid_relu, 1)
                if u is not None:
                    front_late(u)
                    act.wait_ge(pool_og, u)
                    front_gates(u)

            act.wait_ge(weights_in, IN)
            act.activation(expa[:, :], alog[:, :], ACT.Exp).then_inc(expa_done, 1)
            for n in range(4):
                act.activation(wq_hi[:, n, :, :], wq_whole(n), ACT.Copy).then_inc(wq_hi_done, 1)
            ahead(act, TURNS, first, body)

        @block.vector
        def _(dve):
            def mean_square(after, turn, x, col, hand, use, out, done):
                after(dve, turn, dve.tensor_tensor_reduce(out=y[:, :], in0=x, in1=x, scale=1.0 / D, scalar=0.0,
                                                          op0=ALU.mult, op1=ALU.add, accum_out=var[:, 3:4]))
                dve.tensor_scalar(var[:, col:col + 1], var[:, 3:4], RMS_EPS, None, ALU.add)\
                   .then_inc(hand.full, 1)
                hand.wait_emptied(dve, turn, use)
                dve.tensor_scalar(out, x, rs[:, col:col + 1], None, ALU.mult).then_inc(done, 1)

            def cut_input(u):
                fb[0].wait_emptied(dve, u, "RT")
                dve.tensor_tensor(RT_lo[:, :, :], RT[:, :, :], RT_hi[:, :, :].bitcast(F32), ALU.subtract)\
                   .then_inc(rt_cut, 1)

            def take_row(u, order):
                order(dve, u, dve.tensor_copy(row[:, :], row_next[:, :]))
                dve.sem_inc(row_taken, 1)

            def layer_norm(u, order):
                def after(ins):
                    order(dve, u, ins)

                dve.wait_ge(row_in, u * 16 + 16)
                after(dve.bn_stats(stats[:, :], row_next[:, :]))
                after(dve.tensor_reduce(both[:, :], stats[:, :].rearrange("p (a b) -> p b a", a=2), AXX, ALU.add))
                after(dve.tensor_tensor(mv[:, 1:2], stats[:, 1:2], stats[:, 4:5], ALU.subtract))
                after(dve.tensor_tensor(mv[:, 1:2], mv[:, 1:2], mv[:, 1:2], ALU.mult))
                after(dve.tensor_scalar(var[:, 3:4], both[:, 2:3], 1.0 / D, LN_EPS, ALU.mult, ALU.add))
                dve.tensor_scalar(mv[:, 0:1], both[:, 1:2], 0.5, None, ALU.mult)
                dve.scalar_tensor_tensor(out=var[:, 0:1], in0=mv[:, 1:2], scalar=0.25, in1=var[:, 3:4],
                                         op0=ALU.mult, op1=ALU.add).then_inc(root_f.full, 1)
                root_f.wait_emptied(dve, u, "ln")
                after(dve.tensor_scalar(Xn[:, :], row_next[:, :], mv[:, 0:1], rs[:, 0:1], ALU.subtract, ALU.mult))
                mean_square(order, u, Xn[:, :], 1, root_f, "rms", Rn[:, :], rn_done)

            def gate_inputs(u, order):
                fb[1].wait_full(dve, u, "ab")
                order(dve, u, dve.tensor_tensor(t1[:, :], front[:, 1, GH:2 * GH], dtb[:, :], ALU.add))
                dve.tensor_scalar(ab[:, 0:GH], front[:, 1, 0:GH], -1.0, None, ALU.mult).then_inc(fb[1].free, 1)
                order(dve, u, dve.scalar_tensor_tensor(out=ab[:, GH:2 * GH], in0=t1[:, :], scalar=-1.0,
                                                       in1=t1[:, :], op0=ALU.mult, op1=ALU.min))
                dve.tensor_scalar(t1[:, :], t1[:, :], 0.0, None, ALU.max).then_inc(gate.full, 1)

            def gates(u, order):
                def after(ins):
                    order(dve, u, ins)

                gate.wait_emptied(dve, u)
                after(dve.tensor_scalar(beta[:, :], ex[:, 0:GH], 1.0, None, ALU.add))
                dve.reciprocal(beta[:, :], beta[:, :]).then_inc(dve_beta, 1)
                after(dve.tensor_scalar(t2[:, :], ex[:, GH:2 * GH], 2.0, None, ALU.add))
                after(dve.reciprocal(t2[:, :], t2[:, :]))
                after(dve.tensor_tensor(t2[:, :], t2[:, :], ex[:, GH:2 * GH], ALU.mult))
                after(dve.tensor_tensor(t3[:, :], t2[:, :], t2[:, :], ALU.mult))
                after(dve.tensor_scalar(g[:, :], t3[:, :], 1.0 / 17, 1.0 / 15, ALU.mult, ALU.add))
                for n in (13, 11, 9, 7, 5, 3, 1):
                    after(dve.tensor_tensor(g[:, :], g[:, :], t3[:, :], ALU.mult))
                    after(dve.tensor_scalar(g[:, :], g[:, :], 1.0 / n, None, ALU.add))
                after(dve.tensor_tensor(g[:, :], g[:, :], t2[:, :], ALU.mult))
                after(dve.scalar_tensor_tensor(out=g[:, :], in0=g[:, :], scalar=2.0, in1=t1[:, :],
                                               op0=ALU.mult, op1=ALU.add))
                after(dve.scalar_tensor_tensor(out=g[:, :], in0=g[:, :], scalar=-1.0, in1=expa[:, :],
                                               op0=ALU.mult, op1=ALU.mult))
                dve.tensor_scalar(g[:, :], g[:, :], -200.0, None, ALU.max).then_inc(dve_g, 1)

            def norm_of(u, order, n):
                dve.wait_ge(squares, u * 2 + (n + 1))
                order(dve, u, dve.tensor_reduce(norm[:, n, :], sq[:, n, :, :], AXX, ALU.add))

            def scaled(n, src, by):
                dve.tensor_tensor(nat[:, n, :, :], src, bcast(by, [P, GH, DK]), ALU.mult).then_inc(dve_nat, 1)

            def ask_norms(u):
                dve.tensor_scalar(norm[:, :, :], norm[:, :, :], RMS_EPS, None, ALU.add).then_inc(root_f.full, 1)

            def normalise(u, order):
                root_f.wait_emptied(dve, u, "qk")
                order(dve, u, dve.tensor_scalar(rnorm[:, 0, :], rnorm[:, 0, :], DK ** -0.5, None, ALU.mult))
                scaled(0, qkvg[:, 1, :, :], rnorm[:, 1, :])
                scaled(3, qkvg[:, 0, :, :], rnorm[:, 0, :])
                dve.wait_ge(dve_nat, u * 5 + 2)
                dve.wait_ge(dve_beta, u + 1)
                scaled(1, nat[:, 0, :, :], beta[:, :])

            FRONT_STEPS, STEPS = 37, 4

            def first(u):
                order = Chain(vec_front, FRONT_STEPS)
                layer_norm(u, order)
                dve.wait_ge(weights_in, IN)
                for n in range(4):
                    dve.wait_ge(wq_hi_done, n + 1)
                    dve.tensor_tensor(wq_lo[:, n, :, :], wq_whole(n), wq_hi[:, n, :, :].bitcast(F32), ALU.subtract)\
                       .then_inc(wq_cut, 1)
                order(dve, u, dve.tensor_copy(X[:, :], Xn[:, :]))
                take_row(u, order)
                cut_input(u)
                gate_inputs(u, order)
                gates(u, order)
                norm_of(u, order, 0)
                norm_of(u, order, 1)
                ask_norms(u)
                normalise(u, order)
                order.close()

            def body(t, u):
                inner = Chain(vec, STEPS)
                order = Chain(vec_front, FRONT_STEPS)

                def after(ins):
                    inner(dve, t, ins)

                sbk[0].wait_emptied(dve, t, "cum")
                after(dve.tensor_scalar(egk[:, :], eg[:, 0, :], keep[:, bass.ds(t, 1)], None, ALU.mult))
                dve.tensor_scalar(egc[:, :], eg[:, 2, :], keep[:, bass.ds(t, 1)], None, ALU.mult)\
                   .then_inc(dve_scal, 1)
                after(dve.scalar_tensor_tensor(out=nbe[:, :], in0=egk[:, :], scalar=-1.0, in1=beta[:, :],
                                               op0=ALU.mult, op1=ALU.mult))

                def transposed(n):
                    bank, h = bank_of(dve, t, ("tra", n, 1), "full")
                    dve.tensor_copy(heads(tra[:, n], 1), split(bank)).then_inc(h.free, 1)

                transposed(0)
                scaled(2, nat[:, 0, :, :], nbe[:, :])
                transposed(3)
                scaled(4, nat[:, 3, :, :], egk[:, :])
                transposed(1)
                transposed(2)
                transposed(4)
                dve.wait_ge(pool_E, t + 1)
                for k in range(G):
                    for i in (2 * k, 2 * k + 1):
                        bank, h = bank_of(dve, t, ("mp", i), "full")
                        dve.tensor_tensor(mp[:, 2 * i:2 * i + 2, :, :],
                                          bank.rearrange("p (h a e) -> p h a e", h=2, a=2),
                                          E[:, 2 * i:2 * i + 2, :].unsqueeze(2).broadcast_to([P, 2, 2, P]),
                                          ALU.mult).then_inc(h.free, 1)
                level_zero(dve, t, G - 1)
                for l in range(1, LEVELS):
                    for k in range(G):
                        bank, h = bank_of(dve, t, ("a", l, k), "full")
                        dve.tensor_tensor(halves(heads(Xl, k), l)[:, :, :, 0, :], halves(split(bank), l)[:, :, :, 0, :],
                                          halves(level[:, l, :].unsqueeze(1).broadcast_to([P, HG, P]), l)
                                          [:, :, :, 0, :], ALU.mult).then_inc(h.free, 1)
                    for k in range(G):
                        bank, h = bank_of(dve, t, ("b", l, k), "full")
                        cols = halves(heads(T, k), l)[:, :, :, 0, :]
                        dve.tensor_tensor(cols, cols, halves(split(bank), l)[:, :, :, 0, :], ALU.subtract)\
                           .then_inc(h.free, 1)
                dve.wait_ge(pool_nat, t * 2 + 2)
                for k in range(G):
                    sbk[k].wait_full(dve, t, "ks")
                    dve.tensor_tensor(heads(R, k), grp(stateb, k), heads(nat[:, 6], k), ALU.add)\
                       .then_inc(sbk[k].free, 1)
                if u is not None:
                    layer_norm(u, order)
                dve.wait_ge(squares_o, t * 2 + 2)
                after(dve.tensor_reduce(osum[:, :], sqo, AXX, ALU.add))
                dve.tensor_scalar(osum[:, :], osum[:, :], 1.0 / DK, RMS_EPS, ALU.mult, ALU.add)\
                   .then_inc(root.full, 1)
                if u is not None:
                    cut_input(u)
                for k in range(G):
                    sbk[k].wait_full(dve, t, "s")
                    for h in range(HG):
                        ins = dve.scalar_tensor_tensor(out=St[:, HG * k + h, :], in0=St[:, HG * k + h, :],
                                                       scalar=egc[:, HG * k + h:HG * k + h + 1],
                                                       in1=stateb[:, k, h * P:(h + 1) * P],
                                                       op0=ALU.mult, op1=ALU.add)
                    ins.then_inc(sbk[k].free, 1)
                if u is not None:
                    gate_inputs(u, order)
                root.wait_emptied(dve, t, "o")
                dve.wait_ge(pool_og, t + 1)
                dve.tensor_tensor(og[:, :, :], og[:, :, :], bcast(ro[:, :], [P, GH, DK]), ALU.mult)\
                   .then_inc(og_done, 1)
                if u is not None:
                    gates(u, order)
                    norm_of(u, order, 0)
                sbk[0].wait_full(dve, t, "wo")
                dve.tensor_tensor(X2[:, :], stateb[:, 0, 0:D], X[:, :], ALU.add).then_inc(sbk[0].free, 1)
                sbk[0].wait_emptied(dve, t, "wo")
                mean_square(inner, t, X2[:, :], 2, root, "rms2", M[:, :], m_done)
                if u is not None:
                    order(dve, u, dve.tensor_copy(X[:, :], Xn[:, :]))
                for k in range(2):
                    bank, h = bank_of(dve, t, ("hid", k), "full")
                    dve.wait_ge(hid_relu, t * 2 + (k + 1))
                    dve.tensor_tensor(heads(hT, k), split(bank), heads(hid, k), ALU.mult).then_inc(h.free, 1)
                if u is not None:
                    norm_of(u, order, 1)
                    ask_norms(u)
                sbk[1].wait_full(dve, t, "down")
                dve.tensor_tensor(y[:, :], stateb[:, 1, 0:D], X2[:, :], ALU.add).then_inc(sbk[1].free, 1)
                sbk[1].wait_emptied(dve, t, "down")
                dve.wait_ge(stored, t * 16 + 1)
                dve.tensor_tensor(row_out[:, :], row[:, :], y[:, :], ALU.add).then_inc(row_done, 1)
                if u is not None:
                    dve.wait_ge(row_done, t + 1)
                    take_row(u, order)
                    normalise(u, order)
                    order.close()
                inner.close()

            dve.memset(St[:, :, :], 0.0).then_inc(cleared, 1)
            dve.wait_ge(cleared, 1)
            dve.wait_ge(expa_done, 1)
            ahead(dve, TURNS, first, body)

        @block.tensor
        def _(pe):
            def transposes(out, src, n):
                for i in range(n):
                    mm = pe.transpose(out[:, i * P:(i + 1) * P], src(i), ident[:, :])
                return mm

            def project(u, n, f):
                fb[f].wait_free(pe, u, ("proj", n, f))
                products = ((RT_hi, wq_hi), (RT_hi, wq_lo), (RT_lo, wq_hi))
                for i, (x, wq) in enumerate(products):
                    for c in range(ND):
                        mm = pe.matmul(front[:, f, :], x[:, c, :], wq[:, n, c, f * BANK:(f + 1) * BANK],
                                       start=(i == 0 and c == 0), stop=(i == 2 and c == ND - 1))
                mm.then_inc(fb[f].full, 1)

            def front_input(u):
                pe.wait_ge(rn_done, u + 1)
                fb[0].wait_free(pe, u, "RT")
                transposes(front[:, 0, :], lambda i: Rn[:, i * P:(i + 1) * P], ND).then_inc(fb[0].full, 1)

            def front_start(u):
                fb[0].wait_emptied(pe, u, "RT")
                fb[1].wait_free(pe, u, "ab")
                for c in range(ND):
                    mm = pe.matmul(front[:, 1, 0:2 * GH], RT[:, c, :], wab[:, c, :], start=(c == 0),
                                   stop=(c == ND - 1))
                mm.then_inc(fb[1].full, 1)
                pe.wait_ge(rt_cut, u + 1)
                project(u, 0, 0)
                project(u, 0, 1)
                project(u, 1, 0)

            def front_middle(u):
                project(u, 1, 1)
                project(u, 2, 0)

            def first(u):
                front_input(u)
                front_start(u)
                front_middle(u)
                project(u, 2, 1)
                project(u, 3, 0)
                project(u, 3, 1)

            def body(t, u):
                pe.wait_ge(dve_g, t + 1)
                sbk[0].wait_free(pe, t, "cum")
                for n, mask in enumerate((upto, beyond, ones)):
                    mm = pe.matmul(stateb[:, 0, n * GH:(n + 1) * GH], mask[:, :], g[:, :], start=True, stop=True)
                mm.then_inc(sbk[0].full, 1)
                pe.wait_ge(pool_gu, t + 1)
                for k in range(G):
                    out, h = bank_of(pe, t, ("decay", k), "free")
                    pe.matmul(out, beyond[:, :], heads(gu, k), start=True, stop=True).then_inc(h.full, 1)
                for i, n in enumerate(TRANSPOSED):
                    pe.wait_ge(dve_nat, t * 5 + (1, 2, 3, 4, 5)[i])
                    for k in range(G):
                        out, h = bank_of(pe, t, ("tra", n, k), "free")
                        transposes(out, lambda i: nat[:, n, HG * k + i, :], HG).then_inc(h.full, 1)
                for k in range(GH // 2):
                    for n in (3, 1):
                        emptied(pe, t, ("tra", n, k // 2))
                    out, hand = bank_of(pe, t, ("mp", k), "free")
                    for i in range(2):
                        h = 2 * k + i
                        pe.matmul(out[:, 2 * i * P:(2 * i + 1) * P], tra[:, 0, h, :], tra[:, 1, h, :],
                                  start=True, stop=True)
                        mm = pe.matmul(out[:, (2 * i + 1) * P:(2 * i + 2) * P], tra[:, 0, h, :], tra[:, 3, h, :],
                                       start=True, stop=True)
                    mm.then_inc(hand.full, 1)
                def transpose_level(l, k, src):
                    out, hand = bank_of(pe, t, ("t", l, k), "free")
                    transposes(out, lambda i: src[:, HG * k + i, :], HG).then_inc(hand.full, 1)

                for k in range(G):
                    emptied(pe, t, ("tra", 2, k))
                    sbk[k].wait_free(pe, t, "ks")
                    for h in range(HG):
                        mm = pe.matmul(stateb[:, k, h * P:(h + 1) * P], tra[:, 2, HG * k + h, :],
                                       St[:, HG * k + h, :], start=True, stop=True)
                    mm.then_inc(sbk[k].full, 1)
                for k in range(G):
                    pe.wait_ge(Y_done[k], t + 1)
                    transpose_level(0, k, Y)
                for l in range(1, LEVELS):
                    for k in range(G):
                        emptied(pe, t, ("t", 0, k) if l == 1 else ("b", l - 1, k))
                        out, hand = bank_of(pe, t, ("a", l, k), "free")
                        for h in range(HG):
                            mm = pe.matmul(out[:, h * P:(h + 1) * P], mp[:, HG * k + h, 0, :],
                                           T[:, HG * k + h, :], start=True, stop=True)
                        mm.then_inc(hand.full, 1)
                        if l > 1:
                            transpose_level(l - 1, k, T)
                    for k in range(G):
                        emptied(pe, t, ("a", l, k))
                        if l > 1:
                            emptied(pe, t, ("t", l - 1, k))
                        out, hand = bank_of(pe, t, ("b", l, k), "free")
                        for h in range(HG):
                            mm = pe.matmul(out[:, h * P:(h + 1) * P], Y[:, HG * k + h, :],
                                           Xl[:, HG * k + h, :], start=True, stop=True)
                        mm.then_inc(hand.full, 1)
                for k in range(G):
                    emptied(pe, t, ("b", LEVELS - 1, k))
                    transpose_level(LEVELS - 1, k, T)
                for k in range(G):
                    emptied(pe, t, ("t", LEVELS - 1, k))
                    sbk[k].wait_emptied(pe, t, "ks")
                    for h in range(HG):
                        mm = pe.matmul(stateb[:, k, h * P:(h + 1) * P], Y[:, HG * k + h, :],
                                       R[:, HG * k + h, :], start=True, stop=True)
                    mm.then_inc(sbk[k].full, 1)
                for k in range(G):
                    emptied(pe, t, ("tra", 4, k))
                    sbk[k].wait_emptied(pe, t, "u")
                    for h in range(HG):
                        out = stateb[:, k, h * P:(h + 1) * P]
                        pe.matmul(out, tra[:, 4, HG * k + h, :], St[:, HG * k + h, :], start=True, stop=False)
                        mm = pe.matmul(out, mp[:, HG * k + h, 1, :], U[:, HG * k + h, :], start=False, stop=True)
                    mm.then_inc(sbk[k].full, 1)
                if u is not None:
                    front_input(u)
                pe.wait_ge(pool_nat, t * 2 + 1)
                for k in range(G):
                    sbk[k].wait_emptied(pe, t, "o")
                    for h in range(HG):
                        mm = pe.matmul(stateb[:, k, h * P:(h + 1) * P], nat[:, 5, HG * k + h, :],
                                       U[:, HG * k + h, :], start=True, stop=True)
                    mm.then_inc(sbk[k].full, 1)
                if u is not None:
                    front_start(u)
                pe.wait_ge(og_done, t + 1)
                for k in range(G):
                    out, h = bank_of(pe, t, ("ogT", k), "free")
                    transposes(out, lambda i: og[:, HG * k + i, :], HG).then_inc(h.full, 1)
                pe.wait_ge(late_in, 3 * 16)
                sbk[0].wait_free(pe, t, "wo")
                for h in range(GH):
                    if h % HG == 0:
                        emptied(pe, t, ("ogT", h // HG))
                    mm = pe.matmul(stateb[:, 0, 0:D], ogT[:, h, :], wo[:, h, :], start=(h == 0), stop=(h == GH - 1))
                mm.then_inc(sbk[0].full, 1)
                if u is not None:
                    front_middle(u)
                pe.wait_ge(m_done, t + 1)
                out, h = bank_of(pe, t, ("mT",), "free")
                transposes(out, lambda i: M[:, i * P:(i + 1) * P], ND).then_inc(h.full, 1)
                if u is not None:
                    project(u, 2, 1)
                emptied(pe, t, ("mT",))
                for k in range(2):
                    out, h = bank_of(pe, t, ("hid", k), "free")
                    for f in range(4):
                        for c in range(ND):
                            mm = pe.matmul(out[:, f * P:(f + 1) * P], wfc[:, c, (4 * k + f) * P:(4 * k + f + 1) * P],
                                           MT[:, c, :], start=(c == 0), stop=(c == ND - 1))
                    mm.then_inc(h.full, 1)
                if u is not None:
                    project(u, 3, 0)
                sbk[1].wait_free(pe, t, "down")
                for f in range(FF // P):
                    if f % 4 == 0:
                        emptied(pe, t, ("hid", f // 4))
                    mm = pe.matmul(stateb[:, 1, 0:D], hT[:, f, :], wproj[:, f, :], start=(f == 0),
                                   stop=(f == FF // P - 1))
                mm.then_inc(sbk[1].full, 1)
                if u is not None:
                    project(u, 3, 1)

            pe.wait_ge(weights_in, IN)
            pe.wait_ge(wq_cut, 4)
            ahead(pe, TURNS, first, body)


def experts_stage(nc, w, resid, ident, norm, source):
    TURNS = B
    NX = NE + 1
    SIZES = [128, 128, EH - 256]
    NM = len(SIZES)
    with ExitStack() as ctx:
        def sb(name, shape, dt=F32):
            return ctx.enter_context(nc.sbuf_tensor(name, shape, dt))

        def sem(name):
            return ctx.enter_context(nc.semaphore(name))

        norm.next_stage()
        gw = sb("gw", [P, ND, NE])
        gb = sb("gb", [P, NE])
        before = sb("before", [P, NE, NE])
        w13_in = sb("w13_in", [P, 2, 2, ND, EH])
        w13_hi = sb("w13_hi", [P, NX, 2, ND, EH], F32R)
        w13_lo = sb("w13_lo", [P, NX, 2, ND, EH], F32R)
        b13 = sb("b13", [P, NX, 2, NM])
        w2 = sb("w2", [P, NX, NM, D])
        XT_hi = sb("m_XT_hi", [P, ND, S], F32R)
        XT_lo = sb("m_XT_lo", [P, ND, S], F32R)
        lg = sb("lg", [P, NJ, NE])
        eq = sb("eq", [P, NJ, NE, NE])
        gt = sb("gt", [P, NJ, NE, NE])
        small = sb("small", [P, NJ])
        score = sb("score", [P, NJ, NE])
        biased = sb("biased", [P, NJ, NE])
        rank = sb("rank", [P, NJ, NE])
        rw = sb("rw", [P, NJ, NX])
        up = sb("up", [P, 2, S])
        XT = up
        pre = sb("pre", [P, 2, S])
        hT = sb("m_hT", [P, 2, NM, S])

        ups = ctx.enter_context(nc.psum_tensor("m_ups", [P, 2, 2, BANK], F32))
        outs = ctx.enter_context(nc.psum_tensor("m_outs", [P, 2, 2, BANK], F32))

        tiles = [(e, m) for e in range(NX) for m in range(NM)]
        first = [["XT0", "gate"], ["XT1"]]
        hb = [Handoff(ctx, nc, f"m_up{k}", first[k] + [x for n, x in enumerate(tiles) if n % 2 == k]) for k in range(2)]
        hid_done = sem("m_hid_done")
        ob = [Handoff(ctx, nc, f"m_out{k}", range(k, NX, 2)) for k in range(2)]
        up_done = sem("m_up_done")
        small_in = sem("m_small_in")
        w13_here = [sem(f"m_w13_in{k}") for k in range(2)]
        w2_here = [sem(f"m_w2_in{k}") for k in range(2)]
        w13_cut = sem("m_w13_cut")
        x_hi_done = sem("m_x_hi_done")
        x_cut = sem("m_x_cut")
        resid_in = sem("m_resid_in")
        vec = sem("m_vector_order")
        ones_done = sem("m_ones_done")
        lg_done = sem("m_logits")
        lg_exp = sem("m_exps")

        block = ctx.enter_context(nc.Block())

        @block.sync
        def _(sp):
            for h in (*hb, *ob):
                h.open(sp)

            def load(e):
                sp.dma_start(w13_in[:, e % 2, :, :, :], w["w13"][e]).then_inc(w13_here[e % 2], 16)
                sp.dma_start(w2[:, e, 0:2, :], w["w2a"][e]).then_inc(w2_here[e % 2], 16)
                sp.dma_start(w2[0:SIZES[2] + 1, e, 2, :], w["w2b"][e]).then_inc(w2_here[e % 2], 16)

            rows = source.rearrange("b (j p) d -> p (b j) d", p=P)
            sp.dma_start(resid[:, 0:NJ, :], rows[:, 0:NJ, :]).then_inc(resid_in, 16)
            load(0)
            sp.dma_start(gw[:, :, :], w["gw"].rearrange("(c p) n -> p c n", p=P)).then_inc(small_in, 16)
            sp.dma_start(gb[:, :], w["gb"].partition_broadcast(P)).then_inc(small_in, 16)
            sp.dma_start(before[:, :, :], w["before"].partition_broadcast(P)
                         .rearrange("p a (e f) -> p (a e) f", e=NE)).then_inc(small_in, 16)
            sp.dma_start(b13[:, :, :, :], w["b13"]).then_inc(small_in, 16)
            sp.wait_ge(resid_in, 16)
            sp.dma_start(resid[:, NJ:NT, :], rows[:, NJ:NT, :]).then_inc(resid_in, 16)
            for e in range(1, NX):
                if e >= 2:
                    sp.wait_ge(w13_cut, 2 * (e - 1))
                    sp.wait_ge(w2_here[e % 2], e // 2 * 32)
                load(e)

        @block.gpsimd
        def _(pool):
            pool.memset(hT[SIZES[2]:SIZES[2] + 1, :, NM - 1, :], 1.0).then_inc(ones_done, 1)
            pool.wait_ge(ones_done, 1)
            pool.memset(rw[:, :, NE:NX], 1.0).then_inc(ones_done, 1)
            pool.wait_ge(ones_done, 2)
            norm.pool_root(pool, 0)
            for e in range(NX):
                pool.wait_ge(w13_here[e % 2], (e // 2 + 1) * 16)
                pool.tensor_copy(w13_hi[:, e, :, :, :], w13_in[:, e % 2, :, :, :]).then_inc(w13_cut, 1)
                pool.wait_ge(w13_cut, 2 * e + 1)
                pool.tensor_tensor(w13_lo[:, e, :, :, :], w13_in[:, e % 2, :, :, :],
                                   w13_hi[:, e, :, :, :].bitcast(F32), ALU.subtract).then_inc(w13_cut, 1)
            with pool.Fori(1, TURNS) as t:
                norm.pool_root(pool, t)

        @block.scalar
        def _(act):
            with act.Fori(0, TURNS) as t:
                for c in range(ND):
                    hb[c].wait_full(act, t, f"XT{c}")
                    act.activation(XT_hi[:, c, :], ups[:, c, 0, :], ACT.Copy).then_inc(x_hi_done, 1)
                    act.activation(XT[:, c, :], ups[:, c, 0, :], ACT.Copy).then_inc(hb[c].free, 1)
                act.wait_ge(small_in, 4 * 16)
                act.wait_ge(lg_done, t + 1)
                act.activation(lg[:, :, :], lg[:, :, :], ACT.Exp).then_inc(lg_exp, 1)

                def silu(n):
                    e, m = tiles[n]
                    s, k = SIZES[m], n % 2
                    hb[k].wait_emptied(act, t, (e, m))
                    if e >= 2:
                        ob[e % 2].wait_full(act, t, e - 2)
                    act.activation(hT[0:s, e % 2, m, :], pre[0:s, k, :], ACT.Silu).then_inc(hid_done, 1)

                for n, (e, m) in enumerate(tiles):
                    s, k = SIZES[m], n % 2
                    hb[k].wait_full(act, t, (e, m))
                    act.activation(up[0:s, k, :], ups[0:s, k, 0, :], ACT.Identity, bias=b13[0:s, e, 0, m:m + 1])\
                       .then_inc(up_done, 1)
                    if n > 0:
                        silu(n - 1)
                silu(len(tiles) - 1)

        @block.vector
        def _(dve):

            def normalise(u):
                norm.vector(dve, u, resid)

            def body(t, u):
                order = Chain(vec, 10)

                def after(ins):
                    order(dve, t, ins)

                for c in range(ND):
                    dve.wait_ge(x_hi_done, t * ND + (c + 1))
                    hb[c].wait_emptied(dve, t, f"XT{c}")
                    dve.tensor_tensor(XT_lo[:, c, :], XT[:, c, :], XT_hi[:, c, :].bitcast(F32), ALU.subtract)\
                       .then_inc(x_cut, 1)
                hb[0].wait_full(dve, t, "gate")
                logits = ups[:, 0, 0, 0:NJ * NE].rearrange("p (j e) -> p j e", j=NJ)
                after(dve.tensor_reduce(small[:, :], logits, AXX, ALU.max))
                dve.tensor_tensor(lg[:, :, :], logits, bcast(small[:, :], [P, NJ, NE]), ALU.subtract)\
                    .then_inc(hb[0].free, 1)
                hb[0].wait_emptied(dve, t, "gate")
                dve.sem_inc(lg_done, 1)
                dve.wait_ge(lg_exp, t + 1)
                after(dve.tensor_reduce(small[:, :], lg[:, :, :], AXX, ALU.add))
                after(dve.reciprocal(small[:, :], small[:, :]))
                after(dve.tensor_tensor(score[:, :, :], lg[:, :, :], bcast(small[:, :], [P, NJ, NE]), ALU.mult))
                after(dve.tensor_tensor(biased[:, :, :], score[:, :, :],
                                        gb[:, :].unsqueeze(1).broadcast_to([P, NJ, NE]), ALU.add))
                mine = bcast(biased[:, :, :], [P, NJ, NE, NE])
                other = biased[:, :, :].unsqueeze(2).broadcast_to([P, NJ, NE, NE])
                dve.tensor_tensor(gt[:, :, :, :], other, mine, ALU.is_gt)
                after(dve.tensor_tensor(eq[:, :, :, :], other, mine, ALU.is_equal))
                after(dve.tensor_tensor(eq[:, :, :, :], eq[:, :, :, :],
                                        before[:, :, :].unsqueeze(1).broadcast_to([P, NJ, NE, NE]), ALU.mult))
                after(dve.tensor_tensor(gt[:, :, :, :], gt[:, :, :, :], eq[:, :, :, :], ALU.add))
                after(dve.tensor_reduce(rank[:, :, :], gt[:, :, :, :], AXX, ALU.add))
                after(dve.scalar_tensor_tensor(out=rw[:, :, 0:NE], in0=rank[:, :, :], scalar=float(TOPK) - 0.5,
                                               in1=score[:, :, :], op0=ALU.is_lt, op1=ALU.mult))

                def combine(e):
                    ob[e % 2].wait_full(dve, t, e)
                    if e >= 1:
                        ob[(e - 1) % 2].wait_emptied(dve, t, e - 1)
                    for j in range(NJ):
                        row = resid[:, bass.ds(t * NJ + j, 1), :].rearrange("p a d -> p (a d)")
                        ins = dve.scalar_tensor_tensor(
                            out=row, in0=outs[:, e % 2, j // 2, (j % 2) * D:(j % 2 + 1) * D],
                            scalar=rw[:, j, e:e + 1], in1=row, op0=ALU.mult, op1=ALU.add)
                    ins.then_inc(ob[e % 2].free, 1)

                for n, (e, m) in enumerate(tiles):
                    s, k = SIZES[m], n % 2
                    dve.wait_ge(up_done, t * len(tiles) + (n + 1))
                    dve.scalar_tensor_tensor(out=pre[0:s, k, :], in0=ups[0:s, k, 1, :],
                                             scalar=b13[0:s, e, 1, m:m + 1], in1=up[0:s, k, :],
                                             op0=ALU.add, op1=ALU.mult).then_inc(hb[k].free, 1)
                    if e >= 1 and m == NM - 1:
                        combine(e - 1)
                    if u is not None and n == len(tiles) - 2:
                        dve.wait_ge(resid_in, 2 * 16)
                        normalise(u)
                combine(NX - 1)
                order.close()

            def first(u):
                dve.wait_ge(resid_in, 16)
                normalise(u)
                dve.wait_ge(small_in, 4 * 16)
                dve.wait_ge(ones_done, 2)

            ahead(dve, TURNS, first, body)

        @block.tensor
        def _(pe):
            pe.wait_ge(ones_done, 2)
            with pe.Fori(0, TURNS) as t:
                norm.wait(pe, t)
                for c in range(ND):
                    hb[c].wait_free(pe, t, f"XT{c}")
                    transpose_sequence(pe, ups[:, c, 0, :], norm.x, c, ident).then_inc(hb[c].full, 1)
                for c in range(ND):
                    hb[c].wait_emptied(pe, t, f"XT{c}")
                pe.wait_ge(small_in, 4 * 16)
                hb[0].wait_free(pe, t, "gate")
                for j in range(NJ):
                    for c in range(ND):
                        mm = pe.matmul(ups[:, 0, 0, j * NE:(j + 1) * NE], XT[:, c, j * P:(j + 1) * P], gw[:, c, :],
                                       start=(c == 0), stop=(c == ND - 1))
                mm.then_inc(hb[0].full, 1)

                def down(e):
                    k = e % 2
                    pe.wait_ge(hid_done, t * len(tiles) + (e + 1) * NM)
                    pe.wait_ge(w2_here[e % 2], (e // 2 + 1) * 32)
                    ob[k].wait_free(pe, t, e)
                    for j in range(NJ):
                        for m, s in enumerate(SIZES):
                            rows = s + (m == NM - 1)
                            mm = pe.matmul(outs[:, k, j // 2, (j % 2) * D:(j % 2 + 1) * D],
                                           hT[0:rows, k, m, j * P:(j + 1) * P], w2[0:rows, e, m, :],
                                           start=(m == 0), stop=(m == NM - 1))
                    mm.then_inc(ob[k].full, 1)

                for n, (e, m) in enumerate(tiles):
                    s, k = SIZES[m], n % 2
                    if m == 0:
                        pe.wait_ge(w13_cut, 2 * (e + 1))
                    if n == 0:
                        pe.wait_ge(x_cut, t * ND + ND)
                    hb[k].wait_free(pe, t, (e, m))
                    for i in range(2):
                        for c in range(ND):
                            cols = slice(m * P, m * P + s)
                            for a, b in ((w13_hi, XT_hi), (w13_hi, XT_lo), (w13_lo, XT_hi)):
                                mm = pe.matmul(ups[0:s, k, i, :], a[:, e, i, c, cols], b[:, c, :],
                                               start=(c == 0 and b is XT_hi and a is w13_hi),
                                               stop=(c == ND - 1 and a is w13_lo))
                    mm.then_inc(hb[k].full, 1)
                    if e >= 1 and m == 1:
                        down(e - 1)
                down(NX - 1)


def convolution_stage(nc, w, resid, ident, norm, next_weights):
    LA, LB = 32, 16
    ROWS = 2 * MODES
    GROUPS = D // 4
    NFT = NF // P
    HALF = NFT // 2
    TURNS = B
    with ExitStack() as outer:
        fwd = outer.enter_context(nc.sbuf_tensor("fwd", [P, NJ, NF], F32))
        inv = outer.enter_context(nc.sbuf_tensor("inv", [P, NFT, S], F32))
        ka = outer.enter_context(nc.sbuf_tensor("ka", [P, HALF, 2, D], F32))
        kb = outer.enter_context(nc.sbuf_tensor("kb", [P, HALF, 2, D], F32))
        mats_in = outer.enter_context(nc.semaphore("mats_in"))
        convolution_kernel(nc, w, fwd, inv, ka, kb, mats_in, LA, LB, ROWS, GROUPS, NFT, HALF)

        with ExitStack() as ctx:
            def sb(name, shape, dt=F32):
                return ctx.enter_context(nc.sbuf_tensor(name, shape, dt))

            def sem(name):
                return ctx.enter_context(nc.semaphore(name))

            norm.next_stage()
            pa = sb("pa", [P, 2, 2, D])
            pb = sb("pb", [P, 2, 2, D])
            ys = sb("ys", [P, HALF, 2, D])
            spec = ctx.enter_context(nc.psum_tensor("spec", [P, HALF, 2, D], F32))
            back = ctx.enter_context(nc.psum_tensor("back", [P, 2, 2, D], F32))
            sp_h = [Handoff(ctx, nc, f"c_spec{k}") for k in range(HALF)]
            pr_h = [Handoff(ctx, nc, f"c_prod{k}", range(k, HALF, 2)) for k in range(2)]
            back_h = [Handoff(ctx, nc, f"c_back{k}") for k in range(2)]
            ys_done = sem("c_ys_done")

            block = ctx.enter_context(nc.Block())

            @block.sync
            def _(sp):
                for h in (*sp_h, *pr_h, *back_h):
                    h.open(sp)
                next_weights.load(sp, w)

            @block.gpsimd
            def _(pool):
                def body(t, u):
                    for m in range(HALF):
                        sp_h[m].wait_emptied(pool, t)
                        pool.tensor_tensor(ys[:, m, :, :], pa[:, m % 2, :, :], pb[:, m % 2, :, :], ALU.add)\
                            .then_inc(pr_h[m % 2].free, 1)
                    if u is not None:
                        norm.pool_root(pool, u)

                ahead(pool, TURNS, lambda u: norm.pool_root(pool, u), body)

            @block.vector
            def _(dve):
                def normalise(u):
                    norm.vector(dve, u, resid)

                def body(t, u):
                    for m in range(HALF):
                        sp_h[m].wait_full(dve, t)
                        pr_h[m % 2].wait_free(dve, t, m)
                        dve.tensor_tensor(pa[:, m % 2, :, :], spec[:, m, 0, :].unsqueeze(1).broadcast_to([P, 2, D]),
                                          ka[:, m, :, :], ALU.mult)
                        dve.tensor_tensor(pb[:, m % 2, :, :], spec[:, m, 1, :].unsqueeze(1).broadcast_to([P, 2, D]),
                                          kb[:, m, :, :], ALU.mult).then_inc(sp_h[m].free, 1)
                    if u is not None:
                        normalise(u)
                    for k in range(2):
                        back_h[k].wait_full(dve, t)
                        rows = resid[:, bass.ds(t * NJ + 2 * k, 2), :]
                        dve.tensor_tensor(rows, rows, back[:, k, :, :], ALU.add).then_inc(back_h[k].free, 1)

                ahead(dve, TURNS, normalise, body)

            @block.tensor
            def _(pe):
                with pe.Fori(0, TURNS) as t:
                    norm.wait(pe, t)
                    for m in range(HALF):
                        sp_h[m].wait_free(pe, t)
                        for part in range(2):
                            f = (part * HALF + m) * P
                            for j in range(NJ):
                                mm = pe.matmul(spec[:, m, part, :], fwd[:, j, f:f + P], norm.x[:, j, :],
                                               start=(j == 0), stop=(j == NJ - 1))
                        mm.then_inc(sp_h[m].full, 1)
                    for m in (HALF - 2, HALF - 1):
                        pr_h[m % 2].wait_emptied(pe, t, m)
                    for j in range(NJ):
                        if j % 2 == 0:
                            back_h[j // 2].wait_free(pe, t)
                        for f in range(NFT):
                            mm = pe.matmul(back[:, j // 2, j % 2, :], inv[:, f, j * P:(j + 1) * P],
                                           ys[:, f % HALF, f // HALF, :], start=(f == 0), stop=(f == NFT - 1))
                        if j % 2 == 1:
                            mm.then_inc(back_h[j // 2].full, 1)


def convolution_kernel(nc, w, fwd, inv, ka, kb, mats_in, LA, LB, ROWS, GROUPS, NFT, HALF):
    CH = 8
    NCA, NCB = LA // 2 // CH, LB // 2 // CH
    HALVES = [slice(0, ROWS), slice(ROWS, 2 * ROWS)]
    MAGIC = 1.5 * 2.0 ** 23
    TWO_PI_HI = 6.28125
    TWO_PI_LO = 2 * np.pi - TWO_PI_HI
    PI = 3.1415925
    with ExitStack() as ctx:
        def sb(name, shape, dt=F32):
            return ctx.enter_context(nc.sbuf_tensor(name, shape, dt))

        def sem(name):
            return ctx.enter_context(nc.semaphore(name))

        par = sb("par", [P, 5, D])
        lv = sb("lv", [P, (LA + LB) // 2])
        names = ("dt", "are", "dre", "dim", "em1", "er", "sn", "cs", "hs", "nr", "ni", "wr", "wi",
                 "den", "u", "v", "al", "be")
        v = {n: sb("k_" + n, [P, D]) for n in names}
        th = sb("th", [P, CH, D])
        kk = sb("kk", [P, CH, D])
        mg = sb("mg", [P, CH, D])
        arg = sb("arg", [P, CH, D])
        cz = sb("cz", [P, CH, D])
        q = sb("q", [P, GROUPS, 4, LA])
        pz = sb("pz", [P, LB, D])
        kl = mg[:, 0:LB * GROUPS // D, :].rearrange("p c (b g) -> p (c b) g", g=GROUPS)
        kt = arg[:, 0:NJ, :]
        drow = sb("drow", [1, D])
        turn = sb("turn", [P, 2])
        scratch = nc.dram_tensor("k_scratch", (S, D), F32).ap()
        kp = ctx.enter_context(nc.psum_tensor("kp", [P, 8, 8, 64], F32))

        params_in = sem("params_in")
        vec = sem("k_vector_order")
        tables_done = sem("k_tables_done")
        q_cleared = sem("k_q_cleared")
        pz_done = sem("k_pz_done")
        pz_whole = sem("k_pz_whole")
        ask = sem("k_ask")
        ans = sem("k_answer")
        products = sem("k_products")
        gathered = sem("k_gathered")
        stored = sem("k_stored")
        loaded = sem("k_loaded")
        spectra = sem("k_spectra")

        block = ctx.enter_context(nc.Block())

        @block.sync
        def _(sp):
            for quarter in range(4):
                rows = slice(MODES * quarter, MODES * (quarter + 1))
                sp.dma_start(par[rows, 0, :], w["log_dt"].partition_broadcast(MODES)
                             .rearrange("p a h -> p (a h)")).then_inc(params_in, 16)
                sp.dma_start(par[rows, 1:5, :], w["modes"]).then_inc(params_in, 16)
            sp.dma_start(lv[:, :], w["lvals"]).then_inc(params_in, 16)
            sp.dma_start(turn[:, :], w["turn"]).then_inc(params_in, 16)
            sp.dma_start(drow[:, :], w["skip"]).then_inc(params_in, 16)
            sp.dma_start(fwd[:, :, :], w["fwd"].rearrange("(j p) f -> p j f", p=P)).then_inc(mats_in, 16)
            sp.dma_start(inv[:, :, :], w["inv"].rearrange("(m p) l -> p m l", p=P)).then_inc(mats_in, 16)
            sp.wait_ge(pz_done, 1)
            for k in range(2):
                steps = slice(LB // 2 * k, LB // 2 * (k + 1))
                sp.dma_start(pz[HALVES[1 - k], steps, :], pz[HALVES[k], steps, :]).then_inc(pz_whole, 16)
            sp.wait_ge(gathered, 8)
            dst = scratch.rearrange("(a b) (j g) -> j a b g", b=LB, j=4)
            for j in range(4):
                sp.dma_start(dst[j], kl[32 * j:32 * j + 32, :, :]).then_inc(stored, 16)
            sp.wait_ge(stored, 4 * 16)
            sp.dma_start(kt[:, :, :], scratch.rearrange("(t p) h -> p t h", p=P)).then_inc(loaded, 16)

        asked = [(ACT.Exp, v["dt"], par[:, 0, :], 1.0), (ACT.Exp, v["are"], par[:, 1, :], 1.0),
                 (ACT.Tanh, v["em1"], v["dre"][:, :], 0.5)]
        trig = [(v["sn"], v["sn"]), (v["cs"], v["cs"]), (v["hs"], v["hs"])]

        @block.gpsimd
        def _(pool):
            pool.memset(q[:, :, :, :], 0.0).then_inc(q_cleared, 1)

        @block.scalar
        def _(act):
            act.wait_ge(params_in, 11 * 16)
            for n, (f, out, src, scale) in enumerate(asked):
                if n == 2:
                    act.wait_ge(ask, 1)
                act.activation(out[:, :], src, f, scale=scale).then_inc(ans, 1)
            act.wait_ge(ask, 2)
            for out, src in trig:
                act.activation(out[:, :], src[:, :], ACT.Sin).then_inc(ans, 1)
            for n in range(NCA + NCB):
                act.wait_ge(ask, 3 + n)
                act.activation(mg[:, :, :], mg[:, :, :], ACT.Exp).then_inc(ans, 1)
                act.activation(arg[:, :, :], arg[:, :, :], ACT.Sin).then_inc(ans, 1)
                if n >= NCA:
                    act.activation(cz[:, :, :], cz[:, :, :], ACT.Sin).then_inc(ans, 1)

        @block.vector
        def _(dve):
            count = [0]

            def after(ins):
                count[0] += 1
                ins.then_inc(vec, 1)
                dve.wait_ge(vec, count[0])

            def tt(o, a, b, op):
                after(dve.tensor_tensor(v[o][:, :], v[a][:, :], v[b][:, :], op))

            def stt(o, a, s, b, op0, op1):
                after(dve.scalar_tensor_tensor(out=v[o][:, :], in0=v[a][:, :], scalar=s, in1=v[b][:, :],
                                               op0=op0, op1=op1))

            def ts(o, a, s1, s2, op0, op1):
                after(dve.tensor_scalar(v[o][:, :], v[a][:, :], s1, s2, op0, op1))

            def reduce_angle(angle, turns):
                after(dve.tensor_scalar(turns, angle, 1 / (2 * np.pi), MAGIC, ALU.mult, ALU.add))
                after(dve.tensor_scalar(turns, turns, -MAGIC, None, ALU.add))
                after(dve.scalar_tensor_tensor(out=angle, in0=turns, scalar=-TWO_PI_HI, in1=angle,
                                               op0=ALU.mult, op1=ALU.add))
                after(dve.scalar_tensor_tensor(out=angle, in0=turns, scalar=-TWO_PI_LO, in1=angle,
                                               op0=ALU.mult, op1=ALU.add))
                after(dve.tensor_scalar(angle, angle, PI, -PI, ALU.min, ALU.max))

            def cosine_angle(out, angle):
                after(dve.scalar_tensor_tensor(out=out, in0=angle, scalar=-1.0, in1=angle,
                                               op0=ALU.mult, op1=ALU.min))
                after(dve.tensor_scalar(out, out, float(np.pi / 2), None, ALU.add))

            M, A_, S_ = ALU.mult, ALU.add, ALU.subtract
            dve.wait_ge(params_in, 11 * 16)
            dve.wait_ge(ans, 2)
            ts("are", "are", -1.0, None, M, ALU.bypass)
            tt("dre", "are", "dt", M)
            after(dve.tensor_tensor(v["dim"][:, :], par[:, 2, :], v["dt"][:, :], M))
            dve.sem_inc(ask, 1)
            after(dve.tensor_copy(v["sn"][:, :], v["dim"][:, :]))
            reduce_angle(v["sn"][:, :], v["u"][:, :])
            cosine_angle(v["cs"][:, :], v["sn"][:, :])
            ts("hs", "sn", 0.5, None, M, ALU.bypass)
            dve.sem_inc(ask, 1)
            dve.wait_ge(ans, 6)
            ts("u", "em1", -1.0, 1.0, M, A_)
            after(dve.reciprocal(v["u"][:, :], v["u"][:, :]))
            stt("em1", "em1", 2.0, "u", M, M)
            ts("er", "em1", 1.0, None, A_, ALU.bypass)
            tt("nr", "em1", "cs", M)
            tt("hs", "hs", "hs", M)
            stt("nr", "hs", -2.0, "nr", M, A_)
            tt("ni", "er", "sn", M)
            after(dve.tensor_tensor(v["wr"][:, :], par[:, 3, :], v["nr"][:, :], M))
            after(dve.tensor_tensor(v["u"][:, :], par[:, 4, :], v["ni"][:, :], M))
            tt("wr", "wr", "u", S_)
            after(dve.tensor_tensor(v["wi"][:, :], par[:, 3, :], v["ni"][:, :], M))
            after(dve.tensor_tensor(v["u"][:, :], par[:, 4, :], v["nr"][:, :], M))
            tt("wi", "wi", "u", A_)
            tt("den", "are", "are", M)
            after(dve.tensor_tensor(v["u"][:, :], par[:, 2, :], par[:, 2, :], M))
            tt("den", "den", "u", A_)
            after(dve.reciprocal(v["den"][:, :], v["den"][:, :]))
            tt("u", "wr", "are", M)
            after(dve.tensor_tensor(v["v"][:, :], v["wi"][:, :], par[:, 2, :], M))
            tt("u", "u", "v", A_)
            tt("u", "u", "den", M)
            tt("v", "wi", "are", M)
            after(dve.tensor_tensor(v["wr"][:, :], v["wr"][:, :], par[:, 2, :], M))
            tt("v", "v", "wr", S_)
            tt("v", "v", "den", M)
            for half in HALVES:
                re, im = slice(half.start, half.start + MODES), slice(half.start + MODES, half.stop)
                after(dve.tensor_scalar(v["al"][re, :], v["u"][re, :], 2.0, None, M))
                after(dve.tensor_scalar(v["be"][re, :], v["v"][re, :], -2.0, None, M))
                after(dve.tensor_scalar(v["al"][im, :], v["v"][im, :], -2.0, None, M))
                after(dve.tensor_scalar(v["be"][im, :], v["u"][im, :], -2.0, None, M))
            dve.wait_ge(q_cleared, 1)

            got = 6
            for n in range(NCA + NCB):
                steps = bcast(lv[:, CH * n:CH * (n + 1)], [P, CH, D])
                after(dve.tensor_tensor(mg[:, :, :], steps, v["dre"][:, :].unsqueeze(1)
                                        .broadcast_to([P, CH, D]), M))
                after(dve.tensor_tensor(th[:, :, :], steps, v["dim"][:, :].unsqueeze(1)
                                        .broadcast_to([P, CH, D]), M))
                reduce_angle(th[:, :, :], kk[:, :, :])
                if n < NCA:
                    after(dve.scalar_tensor_tensor(out=arg[:, :, :], in0=th[:, :, :], scalar=turn[:, 0:1],
                                                   in1=th[:, :, :], op0=ALU.mult, op1=ALU.min))
                    after(dve.tensor_scalar(arg[:, :, :], arg[:, :, :], turn[:, 1:2], None, ALU.add))
                else:
                    after(dve.tensor_copy(arg[:, :, :], th[:, :, :]))
                    cosine_angle(cz[:, :, :], th[:, :, :])
                dve.sem_inc(ask, 1)
                got += 2 if n < NCA else 3
                dve.wait_ge(ans, got)
                if n < NCA:
                    for k, rows in enumerate(HALVES):
                        at = LA // 2 * k + CH * n
                        ins = dve.tensor_tensor(q[rows, :, :, at:at + CH].rearrange("r g j a -> r a j g"),
                                                mg[rows, :, :].rearrange("r a (j g) -> r a j g", j=4),
                                                arg[rows, :, :].rearrange("r a (j g) -> r a j g", j=4), M)
                    after(ins)
                else:
                    after(dve.tensor_tensor(cz[:, :, :], cz[:, :, :], v["al"][:, :].unsqueeze(1)
                                            .broadcast_to([P, CH, D]), M))
                    after(dve.tensor_tensor(arg[:, :, :], arg[:, :, :], v["be"][:, :].unsqueeze(1)
                                            .broadcast_to([P, CH, D]), M))
                    after(dve.tensor_tensor(cz[:, :, :], cz[:, :, :], arg[:, :, :], A_))
                    for k, rows in enumerate(HALVES):
                        at = LB // 2 * k + CH * (n - NCA)
                        ins = dve.tensor_tensor(pz[rows, at:at + CH, :], mg[rows, :, :], cz[rows, :, :], M)
                    after(ins)
            dve.sem_inc(pz_done, 1)
            dve.sem_inc(tables_done, 1)
            for k in range(8):
                dve.wait_ge(products, k + 1)
                for j in range(4):
                    rows = slice(32 * j, 32 * j + 32)
                    ins = dve.tensor_copy(kl[rows, :, 8 * k:8 * k + 8],
                                          kp[rows, k, :, LB * j:LB * (j + 1)].rearrange("p g b -> p b g"))
                ins.then_inc(gathered, 1)
            dve.wait_ge(loaded, 16)
            dve.tensor_tensor(kt[0:1, 0, :], kt[0:1, 0, :], drow[:, :], A_).then_inc(gathered, 1)
            dve.wait_ge(spectra, HALF)
            for m in range(HALF):
                kr, ki = kp[:, m, 0:4, :].rearrange("p a b -> p (a b)"), kp[:, m, 4:8, :].rearrange("p a b -> p (a b)")
                dve.tensor_copy(ka[:, m, 0, :], kr)
                dve.tensor_copy(ka[:, m, 1, :], ki)
                dve.tensor_scalar(kb[:, m, 0, :], ki, -1.0, None, M)
                after(dve.tensor_copy(kb[:, m, 1, :], kr))
            first = kp[0:1, 0, 4:8, :].rearrange("p a b -> p (a b)")
            dve.tensor_scalar(ka[0:1, 0, 1, :], first, 0.0, None, M)
            dve.tensor_scalar(kb[0:1, 0, 0, :], first, 0.0, None, M)
            after(dve.tensor_copy(kb[0:1, 0, 1, :], first))

        @block.tensor
        def _(pe):
            pe.wait_ge(tables_done, 1)
            pe.wait_ge(pz_whole, 2 * 16)
            qv = q[:, :, :, :].rearrange("r g j a -> r g (j a)")
            pv = pz[:, :, :].rearrange("r b (j g) -> r g j b", j=4)
            for k in range(8):
                for i in range(8):
                    grp = 8 * k + i
                    mm = pe.matmul(kp[:, k, i, :], qv[:, grp, :], pv[:, grp, :, :], start=True, stop=True)
                mm.then_inc(products, 1)
            pe.wait_ge(mats_in, 2 * 16)
            pe.wait_ge(gathered, 9)
            for m in range(HALF):
                for part in range(2):
                    f = (part * HALF + m) * P
                    for j in range(NJ):
                        mm = pe.matmul(kp[:, m, 4 * part:4 * part + 4, :], fwd[:, j, f:f + P], kt[:, j, :],
                                       start=(j == 0), stop=(j == NJ - 1))
                mm.then_inc(spectra, 1)


class LowRankWeights:

    def __init__(self, ctx, nc):
        def sb(name, shape):
            return ctx.enter_context(nc.sbuf_tensor(name, shape, F32))

        self.u1 = sb("u1", [P, ND, RANK])
        self.v1 = sb("f_v1", [RANK, FF])
        self.b1 = sb("b1", [P, FF // P])
        self.u2 = sb("u2", [P, FF // P, RANK])
        self.v2 = sb("v2", [RANK + 1, D])
        self.loaded = ctx.enter_context(nc.semaphore("f_weights_in"))

    def load(self, sp, w):
        sp.dma_start(self.u1[:, :, :], w["U1"].rearrange("(c p) r -> p c r", p=P)).then_inc(self.loaded, 16)
        sp.dma_start(self.v1[:, :], w["V1"]).then_inc(self.loaded, 16)
        sp.dma_start(self.b1[:, :], w["fb1"]).then_inc(self.loaded, 16)
        sp.dma_start(self.u2[:, :, :], w["U2"].rearrange("(c p) r -> p c r", p=P)).then_inc(self.loaded, 16)
        sp.dma_start(self.v2[:, :], w["V2"]).then_inc(self.loaded, 16)

    def wait(self, eng):
        eng.wait_ge(self.loaded, 5 * 16)


def low_rank_stage(nc, w, resid, ident, norm, weights, out):
    TURNS = B
    NFT = FF // P
    with ExitStack() as ctx:
        def sb(name, shape, dt=F32):
            return ctx.enter_context(nc.sbuf_tensor(name, shape, dt))

        def sem(name):
            return ctx.enter_context(nc.semaphore(name))

        norm.next_stage()
        u1, v1, b1, u2, v2 = weights.u1, weights.v1, weights.b1, weights.u2, weights.v2
        XT = sb("f_XT", [P, ND, S])
        PT = sb("PT", [RANK, S])
        H = sb("H", [P, NFT, S])
        QT = sb("QT", [RANK + 1, S])
        y = sb("f_y", [P, NJ, D])

        xb = ctx.enter_context(nc.psum_tensor("f_xps", [P, 2, BANK], F32))
        hb = ctx.enter_context(nc.psum_tensor("f_hps", [P, 2, BANK], F32))
        rb = ctx.enter_context(nc.psum_tensor("f_r", [P, 2, BANK], F32))
        yb = ctx.enter_context(nc.psum_tensor("f_y_out", [P, 2, BANK], F32))
        x_h = [Handoff(ctx, nc, f"f_x{k}") for k in range(2)]
        h_h = [Handoff(ctx, nc, f"f_h{k}", range(k, NFT, 2)) for k in range(2)]
        r_h = [Handoff(ctx, nc, f"f_r{k}") for k in range(2)]
        y_h = [Handoff(ctx, nc, f"f_yb{k}") for k in range(2)]
        ones_done = sem("f_ones_done")
        stored = sem("f_stored")
        block = ctx.enter_context(nc.Block())

        @block.sync
        def _(sp):
            for h in (*x_h, *h_h, *r_h, *y_h):
                h.open(sp)
            sp.sem_inc(stored, 1)
            with sp.Fori(0, TURNS) as t:
                for k in range(2):
                    y_h[k].wait_emptied(sp, t)
                sp.dma_start(out[t].rearrange("(j p) d -> p j d", p=P), y[:, :, :]).then_inc(stored, 16)
            sp.wait_ge(stored, TURNS * 16 + 1)

        @block.gpsimd
        def _(pool):
            pool.memset(QT[RANK:RANK + 1, :], 1.0).then_inc(ones_done, 1)
            pool.wait_ge(ones_done, 1)
            with pool.Fori(0, TURNS) as t:
                norm.pool_root(pool, t)

        @block.scalar
        def _(act):
            weights.wait(act)
            act.preload_act_table_set("gelu_apprx_tanh_and_others")
            with act.Fori(0, TURNS) as t:
                for c in range(ND):
                    x_h[c].wait_full(act, t)
                    act.activation(XT[:, c, :], xb[:, c, :], ACT.Copy).then_inc(x_h[c].free, 1)
                r_h[0].wait_full(act, t)
                act.activation(PT[:, :], rb[0:RANK, 0, :], ACT.Copy).then_inc(r_h[0].free, 1)
                for f in range(NFT):
                    h_h[f % 2].wait_full(act, t, f)
                    act.activation(H[:, f, :], hb[:, f % 2, :], ACT.Gelu_apprx_tanh, bias=b1[:, f:f + 1])\
                       .then_inc(h_h[f % 2].free, 1)
                r_h[1].wait_full(act, t)
                act.activation(QT[0:RANK, :], rb[0:RANK, 1, :], ACT.Copy).then_inc(r_h[1].free, 1)

        @block.vector
        def _(dve):
            def normalise(u):
                norm.vector(dve, u, resid)

            def body(t, u):
                if u is not None:
                    x_h[1].wait_emptied(dve, t)
                    normalise(u)
                dve.wait_ge(stored, t * 16 + 1)
                for k in range(2):
                    y_h[k].wait_full(dve, t)
                    dve.tensor_tensor(y[:, 2 * k:2 * k + 2, :], resid[:, bass.ds(t * NJ + 2 * k, 2), :],
                                      yb[:, k, :].rearrange("p (j d) -> p j d", j=2), ALU.add)\
                        .then_inc(y_h[k].free, 1)

            ahead(dve, TURNS, normalise, body)

        @block.tensor
        def _(pe):
            weights.wait(pe)
            pe.wait_ge(ones_done, 1)
            with pe.Fori(0, TURNS) as t:
                norm.wait(pe, t)
                for c in range(ND):
                    x_h[c].wait_free(pe, t)
                    transpose_sequence(pe, xb[:, c, :], norm.x, c, ident).then_inc(x_h[c].full, 1)
                for c in range(ND):
                    x_h[c].wait_emptied(pe, t)
                r_h[0].wait_free(pe, t)
                for c in range(ND):
                    mm = pe.matmul(rb[0:RANK, 0, :], u1[:, c, :], XT[:, c, :], start=(c == 0), stop=(c == ND - 1))
                mm.then_inc(r_h[0].full, 1)
                r_h[0].wait_emptied(pe, t)
                for f in range(NFT):
                    h_h[f % 2].wait_free(pe, t, f)
                    pe.matmul(hb[:, f % 2, :], v1[:, f * P:(f + 1) * P], PT[:, :], start=True, stop=True)\
                      .then_inc(h_h[f % 2].full, 1)
                r_h[1].wait_free(pe, t)
                for f in range(NFT):
                    h_h[f % 2].wait_emptied(pe, t, f)
                    mm = pe.matmul(rb[0:RANK, 1, :], u2[:, f, :], H[:, f, :], start=(f == 0), stop=(f == NFT - 1))
                mm.then_inc(r_h[1].full, 1)
                r_h[1].wait_emptied(pe, t)
                for k in range(2):
                    y_h[k].wait_free(pe, t)
                    for j in range(2):
                        mm = pe.matmul(yb[:, k, j * D:(j + 1) * D], QT[:, (2 * k + j) * P:(2 * k + j + 1) * P],
                                       v2[:, :], start=True, stop=True)
                    mm.then_inc(y_h[k].full, 1)


def constants_into(nc, ident, minus_half):
    with ExitStack() as ctx:
        made = ctx.enter_context(nc.semaphore("ident_made"))
        block = ctx.enter_context(nc.Block())

        @block.gpsimd
        def _(pool):
            pool.memset(ident[:, :], 0.0).then_inc(made, 1)
            pool.wait_ge(made, 1)
            pool.affine_select(out=ident[:, :], in_=ident[:, :], compare_op=ALU.not_equal, fill=1.0,
                               base=0, pattern=[[-1, P]], channel_multiplier=1).then_inc(made, 1)
            pool.wait_ge(made, 2)
            pool.memset(minus_half[:, :, :], -0.5).then_inc(made, 1)
            pool.wait_ge(made, 3)


def tower(nc, w, out):
    after_attention = nc.dram_tensor("after_attention", (B, S, D), F32).ap()
    after_delta = nc.dram_tensor("after_delta", (B, S, D), F32).ap()
    with ExitStack() as ctx:
        ident = ctx.enter_context(nc.sbuf_tensor("ident", [P, P], F32))
        minus_half = ctx.enter_context(nc.sbuf_tensor("minus_half", [P, 2, GH], F32))
        constants_into(nc, ident, minus_half)
        attention_stage(nc, w, ident, after_attention)
        delta_stage(nc, w, ident, minus_half, after_attention, after_delta)
        resid = ctx.enter_context(nc.sbuf_tensor("resid", [P, NT, D], F32))
        norm = Norm(ctx, nc, minus_half)
        experts_stage(nc, w, resid, ident, norm, after_delta)
        last_weights = LowRankWeights(ctx, nc)
        convolution_stage(nc, w, resid, ident, norm, last_weights)
        low_rank_stage(nc, w, resid, ident, norm, last_weights, out)


def layout(i):
    c = np.ascontiguousarray
    w = {}
    w["x"] = c(i["x"].reshape(B, S, D))
    w["wqkvT"] = c(i["L0_tok_w_qkv"].reshape(NH, 3, HD, D).transpose(3, 1, 0, 2).reshape(D, 3 * D))
    b = i["L0_tok_b_qkv"].reshape(NH, 3, HD).transpose(1, 0, 2).reshape(3, D)
    w["bqk"] = c(b[0:2].reshape(4, P).T)
    w["bv"] = c(b[2:3])
    w["woutT"] = c(i["L0_tok_w_out"].T)
    w["bo"] = c(i["L0_tok_b_out"].reshape(1, D))
    w.update(attention_constants())
    for name in ("Wq", "Wk", "Wv", "Wg", "Wo"):
        w[name] = c(i["L0_attn_" + name])
    w["wab"] = c(np.concatenate([i["L0_attn_Wb"], i["L0_attn_Wa"]], axis=1))
    w["Wfc"], w["Wproj"] = c(i["L0_attn_W_fc"]), c(i["L0_attn_W_proj"])
    w["dtb"], w["alog"], w["onw"] = (c(i["L0_attn_" + n][None]) for n in ("dt_bias", "A_log", "o_norm_w"))
    w.update(delta_constants())
    w["gw"], w["gb"] = c(i["L0_ffn_gate_w"].T), c(i["L0_ffn_gate_b"][None])
    at = np.arange(NE)
    w["before"] = (at[None, :] < at[:, None]).astype(np.float32).reshape(1, NE * NE)
    w1 = np.concatenate([i["L0_ffn_w1"], i["L0_ffn_sw1"][None]])
    w3 = np.concatenate([i["L0_ffn_w3"], i["L0_ffn_sw3"][None]])
    w13 = np.stack([w1, w3], axis=1)
    w["w13"] = c(w13.reshape(NE + 1, 2, ND, P, EH).transpose(0, 3, 1, 2, 4))
    b1 = np.concatenate([i["L0_ffn_b1"], i["L0_ffn_sb1"][None]])
    b3 = np.concatenate([i["L0_ffn_b3"], i["L0_ffn_sb3"][None]])
    b13 = np.zeros((NE + 1, 2, 3 * P), np.float32)
    b13[:, :, :EH] = np.stack([b1, b3], axis=1)
    w["b13"] = c(b13.reshape(NE + 1, 2, 3, P).transpose(3, 0, 1, 2))
    w2 = np.concatenate([i["L0_ffn_w2"], i["L0_ffn_sw2"][None]])
    b2 = np.concatenate([i["L0_ffn_b2"], i["L0_ffn_sb2"][None]])
    w["w2a"] = c(w2[:, :2 * P].reshape(NE + 1, 2, P, D).transpose(0, 2, 1, 3))
    w["w2b"] = c(np.concatenate([w2[:, 2 * P:], b2[:, None]], axis=1))
    w["log_dt"] = c(i["L1_attn_log_dt"][None])
    w["modes"] = c(np.stack([i["L1_attn_log_A_real"].T, i["L1_attn_A_imag"].T,
                             i["L1_attn_C"][:, :, 0].T, i["L1_attn_C"][:, :, 1].T], axis=1))
    w["skip"] = c(i["L1_attn_D"][None])
    w.update(fourier_constants())
    w["U1"], w["V1"], w["U2"] = c(i["L1_ffn_U1"]), c(i["L1_ffn_V1"]), c(i["L1_ffn_U2"])
    w["fb1"] = c(i["L1_ffn_b1"].reshape(FF // P, P).T)
    w["V2"] = c(np.concatenate([i["L1_ffn_V2"], i["L1_ffn_b2"][None]]))
    return w


def fourier_constants():
    l, f = np.arange(S)[:, None], np.arange(S)[None, :]
    angle = 2 * np.pi * (l * f % NF) / NF
    alternating = (-1.0) ** np.arange(S)
    fwd = np.concatenate([np.cos(angle), -np.sin(angle)], axis=1)
    fwd[:, S] = alternating
    weight = np.where(np.arange(S) == 0, 1.0, 2.0)[:, None] / NF
    inv = np.concatenate([weight * np.cos(angle.T), -weight * np.sin(angle.T)])
    inv[S] = alternating / NF
    steps = [np.concatenate([16 * np.arange(16) + 256 * k, np.arange(8) + 8 * k]) for k in range(2)]
    turn = np.tile(np.repeat([[-1.0, np.pi / 2], [1.0, 0.0]], MODES, axis=0), (2, 1))
    return {"fwd": fwd.astype(np.float32), "inv": inv.astype(np.float32),
            "lvals": np.repeat(steps, 2 * MODES, axis=0).astype(np.float32), "turn": turn.astype(np.float32)}


def delta_constants():
    at = np.arange(P)
    level0 = (at[:, None] // 2 == at // 2) & (at[:, None] % 2 == 0) & (at % 2 == 1)
    level = np.zeros((P, 7, P), np.float32)
    for l in range(1, 7):
        m = 1 << l
        level[:, l, :] = (at[:, None] // (2 * m) == at // (2 * m)) & (at[:, None] // m % 2 == 1) & (at // m % 2 == 0)
    return {
        "upto": (at[:, None] <= at).astype(np.float32),
        "beyond": (at[:, None] > at).astype(np.float32),
        "ones": np.ones((P, P), np.float32),
        "level0": level0.astype(np.float32),
        "level": level,
        "keep": (np.arange(NT) % NJ != 0).astype(np.float32)[None],
    }


def attention_constants():
    sel = np.zeros((P, 4, 4, P), np.float32)
    for kind, starts in enumerate(((0, 16), (32,), (0, 32), (16,))):
        for start in starts:
            for head in range(2):
                for e in range(HD):
                    for pair in range(4):
                        sel[32 * pair + head * HD + e, pair, kind, 64 * head + start + e] = 1.0
    selm = np.zeros((2, 2, P), np.float32)
    onerow = np.zeros((P, 1), np.float32)
    for head in range(2):
        for part in range(2):
            selm[head, part, 64 * head + 48 + part] = -1.0
            onerow[64 * head + 48 + part] = 1.0
    return {"sel": sel, "selm": selm, "onerow": onerow}


def kernel(**inputs):
    from concourse.bacc import Bacc
    from concourse.bass_utils import run_bass_kernel_spmd

    nc = Bacc("TRN2", target_bir_lowering=False, num_devices=1)
    arrays = layout({k: np.asarray(v) for k, v in inputs.items()})
    w = {}
    for name, a in arrays.items():
        w[name] = nc.dram_tensor("in_" + name, a.shape, mybir.dt.from_np(a.dtype), kind="ExternalInput").ap()
    out = nc.dram_tensor("out", (B, S, D), F32, kind="ExternalOutput").ap()
    tower(nc, w, out)
    result = run_bass_kernel_spmd(nc, [{"in_" + k: a for k, a in arrays.items()}], core_ids=[0])
    return result.results[0]["out"]
```
